# Optimizing a Trainium2 kernel written in Bass

```python
import numpy as np
import jax
import jax.numpy as jnp

def _softmax(x, axis=-1):
    return jax.nn.softmax(x, axis=axis)

def _gelu(x):
    return jax.nn.gelu(x, approximate=True)

def _silu(x):
    return jax.nn.silu(x)

def _sigmoid(x):
    return jax.nn.sigmoid(x)

def _layernorm(x, axis=-1, eps=1e-05):
    m = jnp.mean(x, axis=axis, keepdims=True)
    v = jnp.var(x, axis=axis, keepdims=True)
    return (x - m) / jnp.sqrt(v + eps)

def _scatter_add(tgt, idx, src, axis=0):
    return tgt.at[idx].add(src)

def _segment_sum(src, seg, n):
    return jax.ops.segment_sum(src, seg, n)
kernel_name = 'mk_seq_postln_d2_jaxref_r8_3b2a32'

def setup_inputs(seed: int=0):
    np.random.seed(seed)
    _w = jnp.asarray

    def _L0_attn_setup():
        import jax, jax.numpy as jnp
        import numpy as np
        D_MODEL = 128
        D_STATE = 16
        D_CONV = 4
        D_INNER = 2 * D_MODEL
        BATCH = 2
        SEQ = 256
        LN_EPS = 1e-05

        def _layernorm(x, w, b):
            mu = jnp.mean(x, axis=-1, keepdims=True)
            var = jnp.mean(jnp.square(x - mu), axis=-1, keepdims=True)
            return (x - mu) * jax.lax.rsqrt(var + LN_EPS) * w + b

        def _forward(x, norm_w, norm_b, in_proj_w, conv_w, conv_b, x_proj_w, dt_w, dt_b, out_proj_w):
            residual = x
            xn = _layernorm(x, norm_w, norm_b)
            xz = xn @ in_proj_w.T
            x_in, z = jnp.split(xz, 2, axis=-1)
            x_conv = jax.lax.conv_general_dilated(jnp.swapaxes(x_in, 1, 2), conv_w, window_strides=(1,), padding=[(D_CONV - 1, 0)], dimension_numbers=('NCH', 'OIH', 'NCH'))
            x_conv = jnp.swapaxes(x_conv, 1, 2) + conv_b
            x_act = jax.nn.silu(x_conv)
            x_ssm = x_act @ x_proj_w.T
            delta_s = x_ssm[..., :1]
            B_mat = x_ssm[..., 1:1 + D_STATE].astype(jnp.float32)
            C = x_ssm[..., 1 + D_STATE:].astype(jnp.float32)
            delta = jax.nn.softplus(delta_s @ dt_w.T + dt_b).astype(jnp.float32)
            x_f32 = x_act.astype(jnp.float32)

            def step(h, inputs):
                d_t, b_t, c_t, u_t = inputs
                h = h * jnp.exp(-d_t)[..., None] + b_t[:, None, :] * u_t[..., None]
                y_t = jnp.einsum('bds,bs->bd', h, c_t)
                return (h, y_t)
            h0 = jnp.zeros((x.shape[0], D_INNER, D_STATE), jnp.float32)
            xs = (jnp.moveaxis(delta, 1, 0), jnp.moveaxis(B_mat, 1, 0), jnp.moveaxis(C, 1, 0), jnp.moveaxis(x_f32, 1, 0))
            _, y = jax.lax.scan(step, h0, xs)
            y = jnp.moveaxis(y, 0, 1).astype(x.dtype)
            return y * jax.nn.silu(z) @ out_proj_w.T + residual
        key = jax.random.key(seed)
        ks = jax.random.split(key, 10)
        s = lambda k, shape, fan: jax.random.normal(k, shape, jnp.float32) * (1.0 / np.sqrt(fan))
        return {'x': jax.random.normal(ks[0], (BATCH, SEQ, D_MODEL), jnp.float32), 'norm_w': jnp.ones((D_MODEL,), jnp.float32), 'norm_b': jnp.zeros((D_MODEL,), jnp.float32), 'in_proj_w': s(ks[1], (2 * D_INNER, D_MODEL), D_MODEL), 'conv_w': s(ks[2], (D_INNER, D_INNER, D_CONV), D_INNER * D_CONV), 'conv_b': s(ks[3], (D_INNER,), D_INNER * D_CONV), 'x_proj_w': s(ks[4], (2 * D_STATE + 1, D_INNER), D_INNER), 'dt_w': s(ks[5], (D_INNER, 1), 1), 'dt_b': s(ks[6], (D_INNER,), 1), 'out_proj_w': s(ks[7], (D_MODEL, D_INNER), D_INNER)}
    _L0_attn_in = _L0_attn_setup()

    def _L0_ffn_setup():
        import jax, jax.numpy as jnp
        import numpy as np
        MAX_THRESHOLD = 0.125
        key = jax.random.key(seed)
        ks = jax.random.split(key, 5)
        B, S, D, FF, E = (2, 256, 128, 512, 8)
        sd = 1.0 / np.sqrt(D)
        sf = 1.0 / np.sqrt(FF)
        return {'inputs': jax.random.normal(ks[0], (B, S, D), dtype=jnp.float32), 'Wg': jax.random.normal(ks[1], (D, E), dtype=jnp.float32) * sd, 'bg': jnp.zeros((E,), dtype=jnp.float32), 'Wt': jax.random.normal(ks[2], (D, 1), dtype=jnp.float32) * sd, 'bt': jnp.zeros((1,), dtype=jnp.float32), 'W1': jax.random.normal(ks[3], (E, D, FF), dtype=jnp.float32) * sd, 'b1': jnp.zeros((E, FF), dtype=jnp.float32), 'W2': jax.random.normal(ks[4], (E, FF, D), dtype=jnp.float32) * sf, 'b2': jnp.zeros((E, D), dtype=jnp.float32)}
    _L0_ffn_in = _L0_ffn_setup()

    def _L1_attn_setup():
        import jax, jax.numpy as jnp
        import numpy as np
        from jax import lax
        B, L = (2, 256)
        DIM, HEADS = (128, 16)
        HD = DIM // HEADS
        D_STATE, D_CONV = (16, 4)
        D_INNER = 2 * DIM
        DT_RANK = DIM // 16

        def _mqa(x, wqkv, bqkv, w_attn_out, b_attn_out):
            b, l, d = x.shape
            qkv = x @ wqkv + bqkv
            q = qkv[..., :DIM].reshape(b, l, HEADS, HD)
            k = qkv[..., DIM:DIM + HD]
            v = qkv[..., DIM + HD:]
            scores = jnp.einsum('blhd,bmd->bhlm', q, k) / np.sqrt(HD).astype(np.float32)
            causal = jnp.tril(jnp.ones((l, l), bool))
            scores = jnp.where(causal, scores, jnp.finfo(scores.dtype).min)
            attn = jax.nn.softmax(scores, axis=-1)
            out = jnp.einsum('bhlm,bmd->blhd', attn, v).reshape(b, l, DIM)
            return out @ w_attn_out + b_attn_out

        def _mamba(x, w_in, conv_w, conv_b, w_xproj, w_dt, b_dt, A_log, Dp, w_out):
            b, l, d = x.shape
            xr = x @ w_in
            u0, res = (xr[..., :D_INNER], xr[..., D_INNER:])
            lhs = u0.transpose(0, 2, 1)
            rhs = conv_w[:, None, :]
            xc = lax.conv_general_dilated(lhs, rhs, window_strides=(1,), padding=[(D_CONV - 1, 0)], dimension_numbers=('NCH', 'OIH', 'NCH'), feature_group_count=D_INNER)
            u = jax.nn.silu((xc + conv_b[None, :, None]).transpose(0, 2, 1))
            x_dbl = u @ w_xproj
            delta = jax.nn.softplus(x_dbl[..., :DT_RANK] @ w_dt + b_dt)
            Bm = x_dbl[..., DT_RANK:DT_RANK + D_STATE]
            Cm = x_dbl[..., DT_RANK + D_STATE:]
            A = -jnp.exp(A_log)

            def step(h, inp):
                d_t, b_t, c_t, u_t = inp
                dA = jnp.exp(d_t[..., None] * A)
                h = dA * h + (d_t * u_t)[..., None] * b_t[:, None, :]
                y = jnp.einsum('bdn,bn->bd', h, c_t)
                return (h, y)
            xs = (delta.transpose(1, 0, 2), Bm.transpose(1, 0, 2), Cm.transpose(1, 0, 2), u.transpose(1, 0, 2))
            h0 = jnp.zeros((b, D_INNER, D_STATE), u.dtype)
            _, ys = lax.scan(step, h0, xs)
            y = ys.transpose(1, 0, 2) + u * Dp
            y = y * jax.nn.silu(res)
            return y @ w_out
        key = jax.random.key(seed)
        ks = jax.random.split(key, 12)
        w = lambda k, shape, s=0.02: jax.random.normal(k, shape, jnp.float32) * s
        A_log = jnp.log(jnp.tile(jnp.arange(1, D_STATE + 1, dtype=jnp.float32), (D_INNER, 1)))
        return {'x': jax.random.normal(ks[0], (B, L, DIM), jnp.float32), 'wqkv': w(ks[1], (DIM, DIM + 2 * HD)), 'bqkv': jnp.zeros((DIM + 2 * HD,), jnp.float32), 'w_attn_out': w(ks[2], (DIM, DIM)), 'b_attn_out': jnp.zeros((DIM,), jnp.float32), 'w_in': w(ks[3], (DIM, 2 * D_INNER)), 'conv_w': w(ks[4], (D_INNER, D_CONV), 0.1), 'conv_b': jnp.zeros((D_INNER,), jnp.float32), 'w_xproj': w(ks[5], (D_INNER, DT_RANK + 2 * D_STATE)), 'w_dt': w(ks[6], (DT_RANK, D_INNER)), 'b_dt': w(ks[7], (D_INNER,), 0.01), 'A_log': A_log, 'Dp': jnp.ones((D_INNER,), jnp.float32), 'w_out': w(ks[8], (D_INNER, DIM))}
    _L1_attn_in = _L1_attn_setup()

    def _L1_ffn_setup():
        import jax, jax.numpy as jnp
        import numpy as np
        DIM = 128
        DEPTH = 6
        HEADS = 16
        DIM_HEAD = 64
        WINDOW = 32
        INNER = HEADS * DIM_HEAD
        DIM_INNER = int(DIM * 4 * 2 / 3)
        QK_SCALE = 8.0

        def shift_tokens(t):
            a, s = jnp.split(t, 2, -1)
            s = jnp.pad(s, ((0, 0), (1, 0), (0, 0)))[:, :-1]
            return jnp.concatenate([a, s], -1)

        def l2norm(t):
            return t / jnp.maximum(jnp.linalg.norm(t, axis=-1, keepdims=True), 1e-12)

        def rotate_half(x):
            x1, x2 = jnp.split(x, 2, -1)
            return jnp.concatenate([-x2, x1], -1)

        def rotary_tables(n):
            half = jnp.arange(0, DIM_HEAD, 2, dtype=jnp.float32)
            inv_freq = 1.0 / 10000.0 ** (half / DIM_HEAD)
            t = jnp.arange(n, dtype=jnp.float32)
            freqs = t[:, None] * inv_freq[None, :]
            freqs = jnp.concatenate([freqs, freqs], -1)
            base_scale = (half + 0.4 * DIM_HEAD) / (1.4 * DIM_HEAD)
            power = (t - n // 2) / (WINDOW // 2)
            scale = base_scale[None, :] ** power[:, None]
            scale = jnp.concatenate([scale, scale], -1)
            return (freqs, scale)

        def local_attention(q, k, v):
            b, h, n, d = q.shape
            w = WINDOW
            nw = n // w
            bq = q.reshape(b, h, nw, w, d)
            bk = k.reshape(b, h, nw, w, d)
            bv = v.reshape(b, h, nw, w, d)

            def look(t):
                p = jnp.pad(t, ((0, 0), (0, 0), (1, 0), (0, 0), (0, 0)))
                return jnp.concatenate([p[:, :, :nw], p[:, :, 1:]], axis=3)
            bk2, bv2 = (look(bk), look(bv))
            seq = jnp.arange(n).reshape(nw, w)
            seq_p = jnp.pad(seq, ((1, 0), (0, 0)), constant_values=-1)
            jt = jnp.concatenate([seq_p[:nw], seq_p[1:]], axis=1)
            it = seq[:, :, None]
            jb = jt[:, None, :]
            mask = (it < jb) | (it > jb + w) | (jb == -1)
            sim = jnp.einsum('bhwie,bhwje->bhwij', bq, bk2) * QK_SCALE
            sim = jnp.where(mask, -jnp.finfo(sim.dtype).max, sim)
            attn = jax.nn.softmax(sim, -1)
            out = jnp.einsum('bhwij,bhwje->bhwie', attn, bv2)
            return out.reshape(b, h, n, d)

        def attn_layer(x, Wqkv, qs, ksc, Wo):
            b, n, _ = x.shape
            qkv = x @ Wqkv
            q, k, v = jnp.split(qkv, 3, -1)
            sh = lambda t: t.reshape(b, n, HEADS, DIM_HEAD).transpose(0, 2, 1, 3)
            q, k, v = (sh(q), sh(k), sh(v))
            q = l2norm(q) * qs
            k = l2norm(k) * ksc
            freqs, scale = rotary_tables(n)
            cos, sin = (jnp.cos(freqs), jnp.sin(freqs))
            q = q * cos * scale + rotate_half(q) * sin * scale
            inv = 1.0 / scale
            k = k * cos * inv + rotate_half(k) * sin * inv
            out = local_attention(q, k, v)
            out = out.transpose(0, 2, 1, 3).reshape(b, n, INNER)
            return out @ Wo

        def ffn_layer(x, g, bln, W1, b1, W2, b2):
            mu = x.mean(-1, keepdims=True)
            var = ((x - mu) ** 2).mean(-1, keepdims=True)
            xn = (x - mu) / jnp.sqrt(var + 1e-05) * g + bln
            hg = xn @ W1 + b1
            a, gate = jnp.split(hg, 2, -1)
            return a * jax.nn.gelu(gate, approximate=False) @ W2 + b2
        key = jax.random.key(seed)
        ks = jax.random.split(key, 8)
        B, N = (2, 256)
        init = lambda k, shape: jax.random.normal(k, shape, jnp.float32) * 0.02
        return {'x': jax.random.normal(ks[0], (B, N, DIM), jnp.float32), 'Wqkv': init(ks[1], (DEPTH, DIM, 3 * INNER)), 'q_scale': jnp.ones((DEPTH, DIM_HEAD), jnp.float32), 'k_scale': jnp.ones((DEPTH, DIM_HEAD), jnp.float32), 'Wo': init(ks[2], (DEPTH, INNER, DIM)), 'ln_g': jnp.ones((DEPTH, DIM), jnp.float32), 'ln_b': jnp.zeros((DEPTH, DIM), jnp.float32), 'W1': init(ks[3], (DEPTH, DIM, 2 * DIM_INNER)), 'b1': jnp.zeros((DEPTH, 2 * DIM_INNER), jnp.float32), 'W2': init(ks[4], (DEPTH, DIM_INNER, DIM)), 'b2': jnp.zeros((DEPTH, DIM), jnp.float32)}
    _L1_ffn_in = _L1_ffn_setup()
    _d = {'L0_attn_x': _L0_attn_in['x'], 'L0_attn_norm_w': _L0_attn_in['norm_w'], 'L0_attn_norm_b': _L0_attn_in['norm_b'], 'L0_attn_in_proj_w': _L0_attn_in['in_proj_w'], 'L0_attn_conv_w': _L0_attn_in['conv_w'], 'L0_attn_conv_b': _L0_attn_in['conv_b'], 'L0_attn_x_proj_w': _L0_attn_in['x_proj_w'], 'L0_attn_dt_w': _L0_attn_in['dt_w'], 'L0_attn_dt_b': _L0_attn_in['dt_b'], 'L0_attn_out_proj_w': _L0_attn_in['out_proj_w'], 'L0_ffn_Wg': _L0_ffn_in['Wg'], 'L0_ffn_bg': _L0_ffn_in['bg'], 'L0_ffn_Wt': _L0_ffn_in['Wt'], 'L0_ffn_bt': _L0_ffn_in['bt'], 'L0_ffn_W1': _L0_ffn_in['W1'], 'L0_ffn_b1': _L0_ffn_in['b1'], 'L0_ffn_W2': _L0_ffn_in['W2'], 'L0_ffn_b2': _L0_ffn_in['b2'], 'L1_attn_wqkv': _L1_attn_in['wqkv'], 'L1_attn_bqkv': _L1_attn_in['bqkv'], 'L1_attn_w_attn_out': _L1_attn_in['w_attn_out'], 'L1_attn_b_attn_out': _L1_attn_in['b_attn_out'], 'L1_attn_w_in': _L1_attn_in['w_in'], 'L1_attn_conv_w': _L1_attn_in['conv_w'], 'L1_attn_conv_b': _L1_attn_in['conv_b'], 'L1_attn_w_xproj': _L1_attn_in['w_xproj'], 'L1_attn_w_dt': _L1_attn_in['w_dt'], 'L1_attn_b_dt': _L1_attn_in['b_dt'], 'L1_attn_A_log': _L1_attn_in['A_log'], 'L1_attn_Dp': _L1_attn_in['Dp'], 'L1_attn_w_out': _L1_attn_in['w_out'], 'L1_ffn_Wqkv': _L1_ffn_in['Wqkv'], 'L1_ffn_q_scale': _L1_ffn_in['q_scale'], 'L1_ffn_k_scale': _L1_ffn_in['k_scale'], 'L1_ffn_Wo': _L1_ffn_in['Wo'], 'L1_ffn_ln_g': _L1_ffn_in['ln_g'], 'L1_ffn_ln_b': _L1_ffn_in['ln_b'], 'L1_ffn_W1': _L1_ffn_in['W1'], 'L1_ffn_b1': _L1_ffn_in['b1'], 'L1_ffn_W2': _L1_ffn_in['W2'], 'L1_ffn_b2': _L1_ffn_in['b2']}
    _x0 = _d['L0_attn_x']
    _d['L0_attn_x'] = jax.random.normal(jax.random.fold_in(jax.random.key(seed), 1), (4, 1024, 128), dtype=_x0.dtype)
    del _x0
    return _d

def reference(L0_attn_x, L0_attn_norm_w, L0_attn_norm_b, L0_attn_in_proj_w, L0_attn_conv_w, L0_attn_conv_b, L0_attn_x_proj_w, L0_attn_dt_w, L0_attn_dt_b, L0_attn_out_proj_w, L0_ffn_Wg, L0_ffn_bg, L0_ffn_Wt, L0_ffn_bt, L0_ffn_W1, L0_ffn_b1, L0_ffn_W2, L0_ffn_b2, L1_attn_wqkv, L1_attn_bqkv, L1_attn_w_attn_out, L1_attn_b_attn_out, L1_attn_w_in, L1_attn_conv_w, L1_attn_conv_b, L1_attn_w_xproj, L1_attn_w_dt, L1_attn_b_dt, L1_attn_A_log, L1_attn_Dp, L1_attn_w_out, L1_ffn_Wqkv, L1_ffn_q_scale, L1_ffn_k_scale, L1_ffn_Wo, L1_ffn_ln_g, L1_ffn_ln_b, L1_ffn_W1, L1_ffn_b1, L1_ffn_W2, L1_ffn_b2):

    def _L0_attn_ref(x, norm_w, norm_b, in_proj_w, conv_w, conv_b, x_proj_w, dt_w, dt_b, out_proj_w):
        import jax, jax.numpy as jnp
        import numpy as np
        D_MODEL = 128
        D_STATE = 16
        D_CONV = 4
        D_INNER = 2 * D_MODEL
        BATCH = 2
        SEQ = 256
        LN_EPS = 1e-05

        def _layernorm(x, w, b):
            mu = jnp.mean(x, axis=-1, keepdims=True)
            var = jnp.mean(jnp.square(x - mu), axis=-1, keepdims=True)
            return (x - mu) * jax.lax.rsqrt(var + LN_EPS) * w + b

        def _forward(x, norm_w, norm_b, in_proj_w, conv_w, conv_b, x_proj_w, dt_w, dt_b, out_proj_w):
            residual = x
            xn = _layernorm(x, norm_w, norm_b)
            xz = xn @ in_proj_w.T
            x_in, z = jnp.split(xz, 2, axis=-1)
            x_conv = jax.lax.conv_general_dilated(jnp.swapaxes(x_in, 1, 2), conv_w, window_strides=(1,), padding=[(D_CONV - 1, 0)], dimension_numbers=('NCH', 'OIH', 'NCH'))
            x_conv = jnp.swapaxes(x_conv, 1, 2) + conv_b
            x_act = jax.nn.silu(x_conv)
            x_ssm = x_act @ x_proj_w.T
            delta_s = x_ssm[..., :1]
            B_mat = x_ssm[..., 1:1 + D_STATE].astype(jnp.float32)
            C = x_ssm[..., 1 + D_STATE:].astype(jnp.float32)
            delta = jax.nn.softplus(delta_s @ dt_w.T + dt_b).astype(jnp.float32)
            x_f32 = x_act.astype(jnp.float32)

            def step(h, inputs):
                d_t, b_t, c_t, u_t = inputs
                h = h * jnp.exp(-d_t)[..., None] + b_t[:, None, :] * u_t[..., None]
                y_t = jnp.einsum('bds,bs->bd', h, c_t)
                return (h, y_t)
            h0 = jnp.zeros((x.shape[0], D_INNER, D_STATE), jnp.float32)
            xs = (jnp.moveaxis(delta, 1, 0), jnp.moveaxis(B_mat, 1, 0), jnp.moveaxis(C, 1, 0), jnp.moveaxis(x_f32, 1, 0))
            _, y = jax.lax.scan(step, h0, xs)
            y = jnp.moveaxis(y, 0, 1).astype(x.dtype)
            return y * jax.nn.silu(z) @ out_proj_w.T + residual
        return _forward(x, norm_w, norm_b, in_proj_w, conv_w, conv_b, x_proj_w, dt_w, dt_b, out_proj_w)

    def _L0_ffn_ref(inputs, Wg, bg, Wt, bt, W1, b1, W2, b2):
        import jax, jax.numpy as jnp
        import numpy as np
        MAX_THRESHOLD = 0.125
        x = inputs.reshape(-1, inputs.shape[-1])
        gate = jax.nn.softmax(x @ Wg + bg, axis=-1)
        thr = jax.nn.sigmoid(x @ Wt + bt) * MAX_THRESHOLD
        adapted = gate - thr
        mask = (adapted >= 0).astype(x.dtype)
        w = adapted * mask
        s = jnp.sum(w, axis=-1, keepdims=True)
        s = jnp.where(s == 0, jnp.ones_like(s), s)
        w = w / s
        h = jax.nn.gelu(jnp.einsum('td,edf->etf', x, W1) + b1[:, None, :])
        eo = jnp.einsum('etf,efd->etd', h, W2) + b2[:, None, :]
        out = jnp.einsum('te,etd->td', w, eo)
        return out.reshape(inputs.shape)

    def _L1_attn_ref(x, wqkv, bqkv, w_attn_out, b_attn_out, w_in, conv_w, conv_b, w_xproj, w_dt, b_dt, A_log, Dp, w_out):
        import jax, jax.numpy as jnp
        import numpy as np
        from jax import lax
        B, L = (2, 256)
        DIM, HEADS = (128, 16)
        HD = DIM // HEADS
        D_STATE, D_CONV = (16, 4)
        D_INNER = 2 * DIM
        DT_RANK = DIM // 16

        def _mqa(x, wqkv, bqkv, w_attn_out, b_attn_out):
            b, l, d = x.shape
            qkv = x @ wqkv + bqkv
            q = qkv[..., :DIM].reshape(b, l, HEADS, HD)
            k = qkv[..., DIM:DIM + HD]
            v = qkv[..., DIM + HD:]
            scores = jnp.einsum('blhd,bmd->bhlm', q, k) / np.sqrt(HD).astype(np.float32)
            causal = jnp.tril(jnp.ones((l, l), bool))
            scores = jnp.where(causal, scores, jnp.finfo(scores.dtype).min)
            attn = jax.nn.softmax(scores, axis=-1)
            out = jnp.einsum('bhlm,bmd->blhd', attn, v).reshape(b, l, DIM)
            return out @ w_attn_out + b_attn_out

        def _mamba(x, w_in, conv_w, conv_b, w_xproj, w_dt, b_dt, A_log, Dp, w_out):
            b, l, d = x.shape
            xr = x @ w_in
            u0, res = (xr[..., :D_INNER], xr[..., D_INNER:])
            lhs = u0.transpose(0, 2, 1)
            rhs = conv_w[:, None, :]
            xc = lax.conv_general_dilated(lhs, rhs, window_strides=(1,), padding=[(D_CONV - 1, 0)], dimension_numbers=('NCH', 'OIH', 'NCH'), feature_group_count=D_INNER)
            u = jax.nn.silu((xc + conv_b[None, :, None]).transpose(0, 2, 1))
            x_dbl = u @ w_xproj
            delta = jax.nn.softplus(x_dbl[..., :DT_RANK] @ w_dt + b_dt)
            Bm = x_dbl[..., DT_RANK:DT_RANK + D_STATE]
            Cm = x_dbl[..., DT_RANK + D_STATE:]
            A = -jnp.exp(A_log)

            def step(h, inp):
                d_t, b_t, c_t, u_t = inp
                dA = jnp.exp(d_t[..., None] * A)
                h = dA * h + (d_t * u_t)[..., None] * b_t[:, None, :]
                y = jnp.einsum('bdn,bn->bd', h, c_t)
                return (h, y)
            xs = (delta.transpose(1, 0, 2), Bm.transpose(1, 0, 2), Cm.transpose(1, 0, 2), u.transpose(1, 0, 2))
            h0 = jnp.zeros((b, D_INNER, D_STATE), u.dtype)
            _, ys = lax.scan(step, h0, xs)
            y = ys.transpose(1, 0, 2) + u * Dp
            y = y * jax.nn.silu(res)
            return y @ w_out
        attended = _mqa(x, wqkv, bqkv, w_attn_out, b_attn_out)
        x1 = attended + x
        y = _mamba(x1, w_in, conv_w, conv_b, w_xproj, w_dt, b_dt, A_log, Dp, w_out)
        return y + x1

    def _L1_ffn_ref(x, Wqkv, q_scale, k_scale, Wo, ln_g, ln_b, W1, b1, W2, b2):
        import jax, jax.numpy as jnp
        import numpy as np
        DIM = 128
        DEPTH = 6
        HEADS = 16
        DIM_HEAD = 64
        WINDOW = 32
        INNER = HEADS * DIM_HEAD
        DIM_INNER = int(DIM * 4 * 2 / 3)
        QK_SCALE = 8.0

        def shift_tokens(t):
            a, s = jnp.split(t, 2, -1)
            s = jnp.pad(s, ((0, 0), (1, 0), (0, 0)))[:, :-1]
            return jnp.concatenate([a, s], -1)

        def l2norm(t):
            return t / jnp.maximum(jnp.linalg.norm(t, axis=-1, keepdims=True), 1e-12)

        def rotate_half(x):
            x1, x2 = jnp.split(x, 2, -1)
            return jnp.concatenate([-x2, x1], -1)

        def rotary_tables(n):
            half = jnp.arange(0, DIM_HEAD, 2, dtype=jnp.float32)
            inv_freq = 1.0 / 10000.0 ** (half / DIM_HEAD)
            t = jnp.arange(n, dtype=jnp.float32)
            freqs = t[:, None] * inv_freq[None, :]
            freqs = jnp.concatenate([freqs, freqs], -1)
            base_scale = (half + 0.4 * DIM_HEAD) / (1.4 * DIM_HEAD)
            power = (t - n // 2) / (WINDOW // 2)
            scale = base_scale[None, :] ** power[:, None]
            scale = jnp.concatenate([scale, scale], -1)
            return (freqs, scale)

        def local_attention(q, k, v):
            b, h, n, d = q.shape
            w = WINDOW
            nw = n // w
            bq = q.reshape(b, h, nw, w, d)
            bk = k.reshape(b, h, nw, w, d)
            bv = v.reshape(b, h, nw, w, d)

            def look(t):
                p = jnp.pad(t, ((0, 0), (0, 0), (1, 0), (0, 0), (0, 0)))
                return jnp.concatenate([p[:, :, :nw], p[:, :, 1:]], axis=3)
            bk2, bv2 = (look(bk), look(bv))
            seq = jnp.arange(n).reshape(nw, w)
            seq_p = jnp.pad(seq, ((1, 0), (0, 0)), constant_values=-1)
            jt = jnp.concatenate([seq_p[:nw], seq_p[1:]], axis=1)
            it = seq[:, :, None]
            jb = jt[:, None, :]
            mask = (it < jb) | (it > jb + w) | (jb == -1)
            sim = jnp.einsum('bhwie,bhwje->bhwij', bq, bk2) * QK_SCALE
            sim = jnp.where(mask, -jnp.finfo(sim.dtype).max, sim)
            attn = jax.nn.softmax(sim, -1)
            out = jnp.einsum('bhwij,bhwje->bhwie', attn, bv2)
            return out.reshape(b, h, n, d)

        def attn_layer(x, Wqkv, qs, ksc, Wo):
            b, n, _ = x.shape
            qkv = x @ Wqkv
            q, k, v = jnp.split(qkv, 3, -1)
            sh = lambda t: t.reshape(b, n, HEADS, DIM_HEAD).transpose(0, 2, 1, 3)
            q, k, v = (sh(q), sh(k), sh(v))
            q = l2norm(q) * qs
            k = l2norm(k) * ksc
            freqs, scale = rotary_tables(n)
            cos, sin = (jnp.cos(freqs), jnp.sin(freqs))
            q = q * cos * scale + rotate_half(q) * sin * scale
            inv = 1.0 / scale
            k = k * cos * inv + rotate_half(k) * sin * inv
            out = local_attention(q, k, v)
            out = out.transpose(0, 2, 1, 3).reshape(b, n, INNER)
            return out @ Wo

        def ffn_layer(x, g, bln, W1, b1, W2, b2):
            mu = x.mean(-1, keepdims=True)
            var = ((x - mu) ** 2).mean(-1, keepdims=True)
            xn = (x - mu) / jnp.sqrt(var + 1e-05) * g + bln
            hg = xn @ W1 + b1
            a, gate = jnp.split(hg, 2, -1)
            return a * jax.nn.gelu(gate, approximate=False) @ W2 + b2
        for i in range(DEPTH):
            x = attn_layer(shift_tokens(x), Wqkv[i], q_scale[i], k_scale[i], Wo[i]) + x
            x = ffn_layer(shift_tokens(x), ln_g[i], ln_b[i], W1[i], b1[i], W2[i], b2[i]) + x
        return x
    x = L0_attn_x
    x = _layernorm(x + _L0_attn_ref(x, L0_attn_norm_w, L0_attn_norm_b, L0_attn_in_proj_w, L0_attn_conv_w, L0_attn_conv_b, L0_attn_x_proj_w, L0_attn_dt_w, L0_attn_dt_b, L0_attn_out_proj_w), axis=-1)
    x = _layernorm(x + _L0_ffn_ref(x, L0_ffn_Wg, L0_ffn_bg, L0_ffn_Wt, L0_ffn_bt, L0_ffn_W1, L0_ffn_b1, L0_ffn_W2, L0_ffn_b2), axis=-1)
    x = _layernorm(x + _L1_attn_ref(x, L1_attn_wqkv, L1_attn_bqkv, L1_attn_w_attn_out, L1_attn_b_attn_out, L1_attn_w_in, L1_attn_conv_w, L1_attn_conv_b, L1_attn_w_xproj, L1_attn_w_dt, L1_attn_b_dt, L1_attn_A_log, L1_attn_Dp, L1_attn_w_out), axis=-1)
    x = _layernorm(x + _L1_ffn_ref(x, L1_ffn_Wqkv, L1_ffn_q_scale, L1_ffn_k_scale, L1_ffn_Wo, L1_ffn_ln_g, L1_ffn_ln_b, L1_ffn_W1, L1_ffn_b1, L1_ffn_W2, L1_ffn_b2), axis=-1)
    return x

_drawn_inputs = setup_inputs


def setup_inputs(seed=0):
    import zlib

    import numpy as np

    out = dict(_drawn_inputs(seed))
    spreads = {'L0_attn_norm_w': (1.0, 0.2),
     'L0_attn_norm_b': (0.0, 0.1),
     'L0_ffn_bg': (0.0, 0.313),
     'L0_ffn_b1': (0.0, 0.1),
     'L0_ffn_b2': (0.0, 0.1),
     'L1_attn_bqkv': (0.0, 0.737),
     'L1_attn_b_attn_out': (0.0, 0.1),
     'L1_attn_conv_b': (0.0, 0.8),
     'L1_attn_Dp': (1.0, 0.6),
     'L1_ffn_q_scale': (1.0, 0.6),
     'L1_ffn_k_scale': (1.0, 0.6),
     'L1_ffn_ln_g': (1.0, 0.6),
     'L1_ffn_ln_b': (0.0, 0.8),
     'L1_ffn_b1': (0.0, 0.8),
     'L1_ffn_b2': (0.0, 0.1)}
    factors = {'L0_attn_conv_b': 2.764,
     'L1_attn_wqkv': 8.0,
     'L1_attn_w_attn_out': 4.909,
     'L1_attn_w_in': 8.0,
     'L1_attn_conv_w': 8.0,
     'L1_attn_w_xproj': 8.0,
     'L1_attn_w_dt': 8.0,
     'L1_attn_b_dt': 8.0,
     'L1_attn_A_log': 8.0,
     'L1_attn_w_out': 8.0,
     'L1_ffn_W1': 3.667,
     'L1_ffn_W2': 3.601}
    for name, (base, spread) in spreads.items():
        noise = np.random.default_rng([zlib.crc32(name.encode()), seed]).standard_normal(out[name].shape)
        drawn = base * np.exp(spread * noise) if base else spread * noise
        out[name] = jnp.asarray(drawn.astype(out[name].dtype))
    for name, factor in factors.items():
        out[name] = (out[name] * factor).astype(out[name].dtype)
    return out
```

```python
from contextlib import ExitStack

import concourse.bass as bass
import numpy as np
from concourse import mybir

F32 = mybir.dt.float32
BF16 = mybir.dt.bfloat16
ALU = mybir.AluOpType
ACT = mybir.ActivationFunctionType
AX = mybir.AxisListType

P = 128
DIM = 128
BATCH = 4
SEQ = 1024
TOKENS = BATCH * SEQ
CH = 512
HALVES = SEQ // CH
NT = TOKENS // P
D_INNER = 256
DB = D_INNER // P
STATES = 16
TAPS = 4
EPS = 1e-5
LOG1P_DEGREE = 10


def log1p_coefficients():
    fit = np.polynomial.chebyshev.Chebyshev.interpolate(lambda x: np.log1p(x + 1e-12) / (x + 1e-12), LOG1P_DEGREE, domain=[0, 1])
    return [float(c) for c in fit.convert(kind=np.polynomial.Polynomial).coef]


class Norm:

    def __init__(self, sem, name):
        self.mean = sem(f"{name}_mean_ready")
        self.cent = sem(f"{name}_centred_ready")
        self.sq = sem(f"{name}_squares_ready")
        self.var = sem(f"{name}_variance_ready")
        self.std = sem(f"{name}_std_ready")
        self.rstd = sem(f"{name}_rstd_ready")


def norm_pe(pe, ln, n, mean_w, x, cent_sq, mean_bank, var_bank):
    pe.matmul(mean_bank, lhsT=mean_w, rhs=x, start=True, stop=True).then_inc(ln.mean, 1)
    pe.wait_ge(ln.sq, n + 1)
    pe.matmul(var_bank, lhsT=mean_w, rhs=cent_sq, start=True, stop=True).then_inc(ln.var, 1)


def norm_act(act, ln, n, cent, cent_sq, var_bank, std, eps):
    act.wait_ge(ln.cent, n + 1)
    act.activation(cent_sq, cent, ACT.Square).then_inc(ln.sq, 1)
    act.wait_ge(ln.var, n + 1)
    act.activation(std, var_bank, ACT.Sqrt, bias=eps).then_inc(ln.std, 1)


def norm_dve(dve, ln, n, x, cent, std, rstd, mean_bank):
    dve.wait_ge(ln.mean, n + 1)
    dve.tensor_tensor(cent, x, mean_bank, ALU.subtract).then_inc(ln.cent, 1)
    dve.wait_ge(ln.std, n + 1)
    dve.reciprocal(rstd, std).then_inc(ln.rstd, 1)
    dve.wait_ge(ln.rstd, n + 1)


def load_tokens(nc, sem, x_dram, X, ident):
    with ExitStack() as mem:
        raw = mem.enter_context(nc.sbuf_tensor("raw_tokens", [P, NT, DIM], F32))
        bank = [mem.enter_context(nc.psum_tensor(f"load_bank{i}", [P, CH], F32)) for i in range(2)]
        landed = [sem(f"tokens_landed{b}") for b in range(BATCH)]
        turned = sem("tokens_turned")
        kept = sem("tokens_kept")
        per = CH // P
        block = mem.enter_context(nc.Block())

        @block.sync
        def _(sp):
            for b in range(BATCH):
                sp.dma_start(raw[:, b * 8:b * 8 + 8, :], x_dram[b].rearrange("(t p) d -> p t d", p=P)).then_inc(landed[b], 16)

        @block.tensor
        def _(pe):
            for g in range(NT // per):
                if g % 2 == 0:
                    pe.wait_ge(landed[g // 2], 16)
                if g >= 2:
                    pe.wait_ge(kept, g - 1)
                for j in range(per):
                    ins = pe.transpose(bank[g % 2][:, j * P:j * P + P], raw[:, g * per + j, :], ident)
                ins.then_inc(turned, 1)

        @block.scalar
        def _(act):
            for g in range(NT // per):
                act.wait_ge(turned, g + 1)
                act.activation(X[:, g * CH:g * CH + CH], bank[g % 2][:, :], ACT.Copy).then_inc(kept, 1)


def store_tokens(nc, sem, out_dram, X, ident):
    with ExitStack() as mem:
        raw = mem.enter_context(nc.sbuf_tensor("out_tokens", [P, NT, DIM], F32))
        bank = [mem.enter_context(nc.psum_tensor(f"store_bank{i}", [P, CH], F32)) for i in range(2)]
        turned = sem("out_turned")
        kept = sem("out_kept")
        stored = sem("out_stored")
        per = CH // P
        block = mem.enter_context(nc.Block())

        @block.tensor
        def _(pe):
            for g in range(NT // per):
                if g >= 2:
                    pe.wait_ge(kept, g - 1)
                for j in range(per):
                    t = g * per + j
                    ins = pe.transpose(bank[g % 2][:, j * P:j * P + P], X[:, t * P:t * P + P], ident)
                ins.then_inc(turned, 1)

        @block.scalar
        def _(act):
            for g in range(NT // per):
                act.wait_ge(turned, g + 1)
                act.activation(raw[:, g * per:g * per + per, :], bank[g % 2][:, :].rearrange("p (t d) -> p t d", t=per),
                               ACT.Copy).then_inc(kept, 1)

        @block.sync
        def _(sp):
            for b in range(BATCH):
                sp.wait_ge(kept, 2 * b + 2)
                sp.dma_start(out_dram[b].rearrange("(t p) d -> p t d", p=P), raw[:, b * 8:b * 8 + 8, :]).then_inc(stored, 16)
            sp.wait_ge(stored, 16 * BATCH)


def mamba(nc, sem, name, X, X1, w, consts):
    first = name == "a"
    ident, mean_w, eps = consts
    low = 1 if first else 8
    rows = low + 2 * STATES
    with ExitStack() as mem:
        def sb(label, shape, dt=F32):
            return mem.enter_context(nc.sbuf_tensor(f"{name}_{label}", shape, dt))

        def bank(label):
            return mem.enter_context(nc.psum_tensor(f"{name}_{label}", [P, CH], F32))

        w_in = sb("w_in", [P, 2 * D_INNER])
        w_conv = sb("w_conv", [P, TAPS, DB, D_INNER]) if first else None
        taps = None if first else sb("taps", [P, DB, TAPS])
        diag = None if first else sb("diag", [P, DB, TAPS, P])
        w_x = sb("w_x", [P, DB, rows])
        w_dt = sb("w_dt", [low, D_INNER])
        w_out = sb("w_out", [P, DB, DIM])
        vec = sb("vectors", [P, 8])
        neg_dt = sb("neg_dt_bias", [P, DB])
        a_log = None if first else sb("a_log", [P, DB, STATES])
        a_neg = None if first else sb("a_neg", [P, DB, STATES])
        select = sb("select", [rows, 2 * STATES, P])
        xs = sb("x", [P, CH])
        cent = sb("cent", [P, CH])
        cent_sq = sb("cent_sq", [P, CH])
        std = sb("std", [P, CH])
        rstd = sb("rstd", [P, CH])
        xn = sb("xn", [P, CH])
        xn2 = sb("xn2", [P, CH])
        x_in = sb("x_in", [P, DB, TAPS - 1 + SEQ])
        gate = sb("gate", [P, DB, CH])
        u = sb("u", [P, DB, CH])
        du = u if first else sb("du", [P, DB, CH])
        dec = sb("decay_or_delta", [P, DB, CH])
        soft = None if first else sb("soft", [P, DB, 3, CH])
        ssm = sb("ssm", [rows, CH])
        c_sb = sb("c_rows", [P, 2, CH])
        bu = sb("b_times_u", [P, 2, DB, CH])
        h = sb("state", [P, 2, DB, CH])
        hc = sb("state_times_c", [P, 2, DB, CH])
        a_ring = None if first else sb("decays", [P, 2, DB, CH])
        carry = sb("carry", [P, STATES, DB])
        g = sb("gated", [P, DB, CH])
        yd = None if first else sb("y_plus_skip", [P, DB, CH])
        r = sb("residual", [P, CH])
        r2 = sb("residual2", [P, CH])
        b_bank = [bank(f"b_bank{i}") for i in range(2)]
        c_bank = [bank(f"c_bank{i}") for i in range(2)]
        y_bank = [bank(f"y_bank{i}") for i in range(DB)]
        p_bank = [bank(f"p_bank{i}") for i in range(2)]

        loaded = sem(f"{name}_weights_loaded")
        setup = sem(f"{name}_setup_done")
        select_ones = sem(f"{name}_select_ones")
        ln1 = Norm(sem, f"{name}_ln1") if first else None
        ln2 = Norm(sem, f"{name}_ln2")
        x_ready = sem(f"{name}_x_ready")
        scaled = sem(f"{name}_norm_scaled")
        xn_ready = sem(f"{name}_xn_ready")
        pre_mm = sem(f"{name}_projection_ready")
        pre_ev = sem(f"{name}_projection_kept")
        soft_step = sem(f"{name}_softplus_step")
        poly_step = sem(f"{name}_log1p_step")
        log1p = log1p_coefficients()
        delta_ready = sem(f"{name}_delta_ready")
        b_ready = sem(f"{name}_b_ready")
        c_ready = sem(f"{name}_c_ready")
        c_kept = sem(f"{name}_c_kept")
        a_ready = sem(f"{name}_decay_ready")
        bu_ready = sem(f"{name}_bu_ready")
        h_ready = sem(f"{name}_state_ready")
        carried = sem(f"{name}_state_carried")
        hc_ready = sem(f"{name}_hc_ready")
        summed = sem(f"{name}_hc_summed")
        skip_ready = sem(f"{name}_skip_added")
        g_ready = sem(f"{name}_gated_ready")
        out_ready = sem(f"{name}_out_ready")
        res_ready = sem(f"{name}_residual_ready")
        done = sem(f"{name}_chunk_done")
        LOADS = 16 * (9 if first else 7)
        SETUP = 3 if first else 12
        PRE = 9
        block = mem.enter_context(nc.Block())

        def at(b, half, per, k):
            return b * (HALVES * per) + (half * per + k)

        def cols(b, half):
            return bass.ds(b * SEQ + half * CH, CH)

        @block.sync
        def _(sp):
            sp.dma_start(w_in[:, :], w["in_proj"]).then_inc(loaded, 16)
            if first:
                for k in range(TAPS):
                    sp.dma_start(w_conv[:, k, :, :], w["conv"][k].rearrange("(e p) o -> p e o", p=P)).then_inc(loaded, 16)
            else:
                sp.dma_start(taps[:, :, :], w["taps"].rearrange("(d p) k -> p d k", p=P)).then_inc(loaded, 16)
                sp.dma_start(a_log[:, :, :], w["a_log"].rearrange("(d p) n -> p d n", p=P)).then_inc(loaded, 16)
            sp.dma_start(w_x[:, :, :], w["x_proj"].rearrange("(e p) r -> p e r", p=P)).then_inc(loaded, 16)
            sp.dma_start(w_dt[:, :], w["dt"]).then_inc(loaded, 16)
            sp.dma_start(w_out[:, :, :], w["out_proj"].rearrange("(e p) o -> p e o", p=P)).then_inc(loaded, 16)
            sp.dma_start(vec[:, :], w["vectors"]).then_inc(loaded, 16)

        @block.tensor
        def _(pe):
            pe.wait_ge(loaded, LOADS)
            pe.wait_ge(setup, SETUP)
            with pe.Fori(0, BATCH) as b:
                for half in range(HALVES):
                    t0 = half * CH
                    pe.wait_ge(x_ready, at(b, half, 1, 1))
                    if first:
                        norm_pe(pe, ln1, at(b, half, 1, 0), mean_w, xs[:, :], cent_sq[:, :], p_bank[0][:, :], p_bank[1][:, :])
                        pe.wait_ge(xn_ready, at(b, half, 1, 1))
                    x_op = xn2 if first else xs
                    for m in range(4):
                        if m >= 2:
                            pe.wait_ge(pre_ev, at(b, half, PRE, m - 1))
                        pe.matmul(p_bank[m % 2][:, :], lhsT=w_in[:, m * P:m * P + P], rhs=x_op[:, :], start=True,
                                  stop=True).then_inc(pre_mm, 1)
                    for d in range(DB):
                        pe.wait_ge(pre_ev, at(b, half, PRE, 3 + d))
                        if first:
                            n_mm = TAPS * DB
                            for i in range(n_mm):
                                k, e = i // DB, i % DB
                                ins = pe.matmul(p_bank[d][:, :], lhsT=w_conv[:, k, e, d * P:d * P + P],
                                                rhs=x_in[:, e, t0 + k:t0 + k + CH], start=i == 0, stop=i == n_mm - 1)
                        else:
                            for k in range(TAPS):
                                ins = pe.matmul(p_bank[d][:, :], lhsT=diag[:, d, k, :], rhs=x_in[:, d, t0 + k:t0 + k + CH],
                                                start=k == 0, stop=k == TAPS - 1)
                        ins.then_inc(pre_mm, 1)
                    pe.wait_ge(pre_ev, at(b, half, PRE, 6))
                    for e in range(DB):
                        ins = pe.matmul(p_bank[0][0:rows, :], lhsT=w_x[:, e, :], rhs=u[:, e, :], start=e == 0, stop=e == DB - 1)
                    ins.then_inc(pre_mm, 1)
                    pe.wait_ge(pre_ev, at(b, half, PRE, 7))
                    for d in range(DB):
                        pe.matmul(p_bank[1 - d][:, :], lhsT=w_dt[:, d * P:d * P + P], rhs=ssm[0:low, :], start=True,
                                  stop=True).then_inc(pre_mm, 1)

                    def spread(s):
                        if s >= 2:
                            pe.wait_ge(bu_ready, at(b, half, 2 * STATES, 2 * (s - 1)))
                        pe.matmul(b_bank[s % 2][:, :], lhsT=select[:, s, :], rhs=ssm[:, :], start=True, stop=True).then_inc(b_ready, 1)
                        if s >= 2:
                            pe.wait_ge(c_kept, at(b, half, STATES, s - 1))
                        pe.matmul(c_bank[s % 2][:, :], lhsT=select[:, STATES + s, :], rhs=ssm[:, :], start=True,
                                  stop=True).then_inc(c_ready, 1)

                    spread(0)
                    spread(1)
                    for s in range(STATES):
                        for d in range(DB):
                            pe.wait_ge(hc_ready, at(b, half, 2 * STATES, 2 * s + d + 1))
                            pe.matmul(y_bank[d][:, :], lhsT=ident, rhs=hc[:, s % 2, d, :], start=s == 0,
                                      stop=s == STATES - 1).then_inc(summed, 1)
                        if s + 2 < STATES:
                            spread(s + 2)
                    for d in range(DB):
                        pe.wait_ge(g_ready, at(b, half, DB, d + 1))
                        ins = pe.matmul(p_bank[0][:, :], lhsT=w_out[:, d, :], rhs=g[:, d, :], start=d == 0, stop=d == DB - 1)
                    ins.then_inc(out_ready, 1)
                    pe.wait_ge(res_ready, at(b, half, 2, 2))
                    norm_pe(pe, ln2, at(b, half, 1, 0), mean_w, r2[:, :], cent_sq[:, :], p_bank[0][:, :], p_bank[1][:, :])

        @block.scalar
        def _(act):
            if not first:
                act.wait_ge(loaded, LOADS)
                act.activation(a_neg[:, :, :], a_log[:, :, :], ACT.Exp).then_inc(setup, 1)
            act.wait_ge(setup, SETUP)
            with act.Fori(0, BATCH) as b:
                for half in range(HALVES):
                    t0 = TAPS - 1 + half * CH
                    act.wait_ge(done, at(b, half, 1, 0))
                    act.activation(xs[:, :], (X if first else X1)[:, cols(b, half)], ACT.Copy).then_inc(x_ready, 1)
                    if first:
                        norm_act(act, ln1, at(b, half, 1, 0), cent[:, :], cent_sq[:, :], p_bank[1][:, :], std[:, :], eps)
                    for m in range(2):
                        act.wait_ge(pre_mm, at(b, half, PRE, m + 1))
                        act.activation(x_in[:, m, t0:t0 + CH], p_bank[m][:, :], ACT.Copy).then_inc(pre_ev, 1)
                    for m in range(2):
                        act.wait_ge(pre_mm, at(b, half, PRE, m + 3))
                        act.activation(gate[:, m, :], p_bank[m][:, :], ACT.Silu).then_inc(pre_ev, 1)
                    for d in range(DB):
                        act.wait_ge(pre_mm, at(b, half, PRE, 5 + d))
                        act.activation(u[:, d, :], p_bank[d][:, :], ACT.Silu, bias=vec[:, d:d + 1]).then_inc(pre_ev, 1)
                    act.wait_ge(pre_mm, at(b, half, PRE, 7))
                    act.activation(ssm[:, :], p_bank[0][0:rows, :], ACT.Copy).then_inc(pre_ev, 1)
                    for d in range(DB):
                        act.wait_ge(pre_mm, at(b, half, PRE, 8 + d))
                        if first:
                            act.activation(dec[:, d, :], p_bank[1 - d][:, :], ACT.Sigmoid, bias=neg_dt[:, d:d + 1],
                                           scale=-1.0).then_inc(pre_ev, 1)
                        else:
                            act.activation(soft[:, d, 0, :], p_bank[1 - d][:, :], ACT.Identity, bias=vec[:, 2 + d:3 + d]).then_inc(pre_ev, 1)
                    if not first:
                        act.wait_ge(pre_ev, at(b, half, PRE, 9))
                        act.activation(soft[:, :, 1, :], soft[:, :, 0, :], ACT.Abs).then_inc(soft_step, 1)
                        act.wait_ge(soft_step, at(b, half, 2, 1))
                        act.activation(soft[:, :, 2, :], soft[:, :, 1, :], ACT.Exp, scale=-1.0).then_inc(soft_step, 1)
                        act.wait_ge(delta_ready, at(b, half, 2, 1))

                    def decays(s):
                        for d in range(DB):
                            if s >= 2:
                                act.wait_ge(h_ready, at(b, half, 2 * STATES, 2 * (s - 2) + d + 1))
                            act.activation(a_ring[:, s % 2, d, :], dec[:, d, :], ACT.Exp, scale=a_neg[:, d, s:s + 1]).then_inc(a_ready, 1)

                    if not first:
                        decays(0)
                    for s in range(STATES):
                        act.wait_ge(c_ready, at(b, half, STATES, s + 1))
                        if s >= 2:
                            act.wait_ge(hc_ready, at(b, half, 2 * STATES, 2 * (s - 1)))
                        act.activation(c_sb[:, s % 2, :], c_bank[s % 2][:, :], ACT.Copy).then_inc(c_kept, 1)
                        if not first and s + 1 < STATES:
                            decays(s + 1)
                        if half == 0:
                            for d in range(DB):
                                act.wait_ge(h_ready, at(b, half, 2 * STATES, 2 * s + d + 1))
                                act.activation(carry[:, s, d:d + 1], h[:, s % 2, d, CH - 1:CH], ACT.Copy).then_inc(carried, 1)
                    norm_act(act, ln2, at(b, half, 1, 0), cent[:, :], cent_sq[:, :], p_bank[1][:, :], std[:, :], eps)

        @block.gpsimd
        def _(pool):
            pool.memset(x_in[:, :, 0:TAPS - 1], 0.0).then_inc(setup, 1)
            pool.memset(select[:, :, :], 1.0).then_inc(select_ones, 1)
            pool.wait_ge(select_ones, 1)
            pool.affine_select(out=select[:, :, :], in_=select[:, :, :], pattern=[[-1, 2 * STATES], [0, P]],
                               compare_op=ALU.is_equal, fill=0.0, base=-low, channel_multiplier=1).then_inc(setup, 1)
            with pool.Fori(0, BATCH) as b:
                for half in range(HALVES):
                    for s in range(STATES):
                        pool.wait_ge(c_kept, at(b, half, STATES, s + 1))
                        for d in range(DB):
                            pool.wait_ge(h_ready, at(b, half, 2 * STATES, 2 * s + d + 1))
                            if s >= 2:
                                pool.wait_ge(summed, at(b, half, 2 * STATES, 2 * (s - 2) + d + 1))
                            pool.tensor_tensor(hc[:, s % 2, d, :], h[:, s % 2, d, :], c_sb[:, s % 2, :], ALU.mult).then_inc(hc_ready, 1)

        @block.vector
        def _(dve):
            dve.wait_ge(loaded, LOADS)
            if first:
                dve.tensor_scalar(neg_dt[:, :], vec[:, 2:4], -1.0, None, ALU.mult).then_inc(setup, 1)
            else:
                for d in range(DB):
                    for k in range(TAPS):
                        dve.tensor_scalar(diag[:, d, k, :], ident, taps[:, d, k:k + 1], None, ALU.mult).then_inc(setup, 1)
                dve.wait_ge(setup, SETUP - 1)
                dve.tensor_scalar(a_neg[:, :, :], a_neg[:, :, :], -1.0, None, ALU.mult).then_inc(setup, 1)
            with dve.Fori(0, BATCH) as b:
                for half in range(HALVES):
                    if first:
                        dve.wait_ge(x_ready, at(b, half, 1, 1))
                        norm_dve(dve, ln1, at(b, half, 1, 0), xs[:, :], cent[:, :], std[:, :], rstd[:, :], p_bank[0][:, :])
                        dve.tensor_tensor(xn[:, :], cent[:, :], rstd[:, :], ALU.mult).then_inc(scaled, 1)
                        dve.wait_ge(scaled, at(b, half, 1, 1))
                        dve.tensor_scalar(xn2[:, :], xn[:, :], vec[:, 4:5], vec[:, 5:6], ALU.mult, ALU.add).then_inc(xn_ready, 1)
                        dve.wait_ge(pre_ev, at(b, half, PRE, 9))
                    else:
                        dve.wait_ge(soft_step, at(b, half, 2, 2))
                        e, q = soft[:, :, 2, :], soft[:, :, 1, :]
                        dve.tensor_scalar(q, e, log1p[LOG1P_DEGREE], None, ALU.mult).then_inc(poly_step, 1)
                        for k in range(LOG1P_DEGREE):
                            dve.wait_ge(poly_step, at(b, half, LOG1P_DEGREE + 1, k + 1))
                            dve.scalar_tensor_tensor(q, q, log1p[LOG1P_DEGREE - 1 - k], e, ALU.add, ALU.mult).then_inc(poly_step, 1)
                        dve.wait_ge(poly_step, at(b, half, LOG1P_DEGREE + 1, LOG1P_DEGREE + 1))
                        dve.scalar_tensor_tensor(dec[:, :, :], soft[:, :, 0, :], 0.0, soft[:, :, 1, :], ALU.max,
                                                 ALU.add).then_inc(delta_ready, 1)
                        dve.wait_ge(delta_ready, at(b, half, 2, 1))
                        dve.tensor_tensor(du[:, :, :], dec[:, :, :], u[:, :, :], ALU.mult).then_inc(delta_ready, 1)
                        dve.wait_ge(delta_ready, at(b, half, 2, 2))
                    for s in range(STATES):
                        dve.wait_ge(b_ready, at(b, half, STATES, s + 1))
                        for d in range(DB):
                            if s >= 2:
                                dve.wait_ge(h_ready, at(b, half, 2 * STATES, 2 * (s - 2) + d + 1))
                            dve.tensor_tensor(bu[:, s % 2, d, :], du[:, d, :], b_bank[s % 2][:, :], ALU.mult).then_inc(bu_ready, 1)
                        for d in range(DB):
                            dve.wait_ge(bu_ready, at(b, half, 2 * STATES, 2 * s + d + 1))
                            if s >= 2:
                                dve.wait_ge(hc_ready, at(b, half, 2 * STATES, 2 * (s - 2) + d + 1))
                                if half == 0:
                                    dve.wait_ge(carried, b * 2 * STATES + (2 * (s - 2) + d + 1))
                            elif half == 1:
                                dve.wait_ge(carried, b * 2 * STATES + 2 * STATES)
                            if not first:
                                dve.wait_ge(a_ready, at(b, half, 2 * STATES, 2 * s + d + 1))
                            decay = dec[:, d, :] if first else a_ring[:, s % 2, d, :]
                            start = 0.0 if half == 0 else carry[:, s, d:d + 1]
                            dve.tensor_tensor_scan(h[:, s % 2, d, :], decay, bu[:, s % 2, d, :], start, ALU.mult,
                                                   ALU.add).then_inc(h_ready, 1)
                    dve.wait_ge(summed, at(b, half, 2 * STATES, 2 * STATES))
                    for d in range(DB):
                        if first:
                            dve.tensor_tensor(g[:, d, :], gate[:, d, :], y_bank[d][:, :], ALU.mult).then_inc(g_ready, 1)
                        else:
                            dve.scalar_tensor_tensor(yd[:, d, :], u[:, d, :], vec[:, 6 + d:7 + d], y_bank[d][:, :], ALU.mult,
                                                     ALU.add).then_inc(skip_ready, 1)
                            dve.wait_ge(skip_ready, at(b, half, DB, d + 1))
                            dve.tensor_tensor(g[:, d, :], gate[:, d, :], yd[:, d, :], ALU.mult).then_inc(g_ready, 1)
                    dve.wait_ge(out_ready, at(b, half, 1, 1))
                    dve.tensor_tensor(r[:, :], xs[:, :], p_bank[0][:, :], ALU.add).then_inc(res_ready, 1)
                    dve.wait_ge(res_ready, at(b, half, 2, 1))
                    dve.tensor_tensor(r2[:, :], r[:, :], X[:, cols(b, half)], ALU.add).then_inc(res_ready, 1)
                    dve.wait_ge(res_ready, at(b, half, 2, 2))
                    norm_dve(dve, ln2, at(b, half, 1, 0), r2[:, :], cent[:, :], std[:, :], rstd[:, :], p_bank[0][:, :])
                    dve.tensor_tensor(X[:, cols(b, half)], cent[:, :], rstd[:, :], ALU.mult).then_inc(done, 1)


EXPERTS = 8
FF = 512
FB = FF // P
THRESHOLD = 0.125


def experts(nc, sem, X, d, consts):
    ident, mean_w, eps = consts
    G = EXPERTS + 1
    with ExitStack() as mem:
        def sb(label, shape, dt=F32):
            return mem.enter_context(nc.sbuf_tensor(f"b_{label}", shape, dt))

        def bank(label):
            return mem.enter_context(nc.psum_tensor(f"b_{label}", [P, CH], F32))

        w1 = sb("w1", [P, EXPERTS, FF])
        w2 = sb("w2", [P, EXPERTS, FB, DIM])
        b1 = sb("b1", [P, EXPERTS * FB])
        b2 = sb("b2", [EXPERTS, DIM])
        wg = sb("w_gate", [P, G])
        bg = sb("gate_bias", [P, G])
        select = sb("select", [EXPERTS, EXPERTS, P])
        logit = sb("logit", [P, NT, G])
        top = sb("top", [P, NT])
        ex = sb("exps", [P, NT, EXPERTS])
        total = sb("total", [P, NT])
        inv = sb("inverse", [P, NT])
        thr = sb("threshold", [P, NT])
        fix = sb("zero_fix", [P, NT])
        wt = sb("weights", [P, NT, EXPERTS])
        w_rows = sb("weight_rows", [EXPERTS, TOKENS])
        xs = sb("x", [P, CH])
        wc = sb("chunk_weights", [EXPERTS, CH])
        wb = sb("spread_weights", [P, 2, CH])
        hid = sb("hidden", [P, 4, CH])
        part = sb("weighted", [P, 2, CH])
        acc = sb("acc", [P, CH])
        res = sb("residual", [P, CH])
        cent = sb("cent", [P, CH])
        cent_sq = sb("cent_sq", [P, CH])
        std = sb("std", [P, CH])
        rstd = sb("rstd", [P, CH])
        h_bank = [bank(f"h_bank{i}") for i in range(3)]
        o_bank = [bank(f"o_bank{i}") for i in range(2)]
        w_bank = bank("w_bank")
        n_bank = [bank(f"n_bank{i}") for i in range(2)]

        loaded = sem("b_weights_loaded")
        gate_loaded = sem("b_gate_loaded")
        select_step = sem("b_select_step")
        logits_ready = sem("b_logits_ready")
        gate_step = sem("b_gate_step")
        gate_act = sem("b_gate_exps")
        gate_fix = sem("b_zero_sum_step")
        turned = sem("b_weights_turned")
        turned_kept = sem("b_weight_rows_kept")
        x_ready = sem("b_x_ready")
        hid_mm = sem("b_hidden_ready")
        gelu_ready = sem("b_gelu_ready")
        out_mm = sem("b_expert_out")
        spread_mm = sem("b_weights_spread")
        spread_kept = sem("b_spread_kept")
        weighted = sem("b_weighted")
        summed = sem("b_summed")
        bias_mm = sem("b_bias_ready")
        res_ready = sem("b_residual_ready")
        ln = Norm(sem, "b_ln")
        done = sem("b_chunk_done")
        UNITS = EXPERTS * FB
        CHUNKS = TOKENS // CH
        block = mem.enter_context(nc.Block())

        @block.sync
        def _(sp):
            sp.dma_start(wg[:, :], d["b_gate"]).then_inc(gate_loaded, 16)
            sp.dma_start(bg[:, :], d["b_gate_bias"]).then_inc(gate_loaded, 16)
            sp.dma_start(b1[:, :], d["b_b1"]).then_inc(loaded, 16)
            sp.dma_start(b2[:, :], d["b_b2"]).then_inc(loaded, 16)
            sp.dma_start(w1[:, :, :], d["b_w1"].rearrange("e p f -> p e f")).then_inc(loaded, 16)
            for e in range(EXPERTS):
                sp.dma_start(w2[:, e, :, :], d["b_w2"][e].rearrange("(f p) o -> p f o", p=P)).then_inc(loaded, 16)

        @block.gpsimd
        def _(pool):
            pool.memset(select[:, :, :], 1.0).then_inc(select_step, 1)
            pool.wait_ge(select_step, 1)
            pool.affine_select(out=select[:, :, :], in_=select[:, :, :], pattern=[[-1, EXPERTS], [0, P]],
                               compare_op=ALU.is_equal, fill=0.0, base=0, channel_multiplier=1).then_inc(select_step, 1)

        @block.tensor
        def _(pe):
            pe.wait_ge(gate_loaded, 32)
            logits = n_bank[0][:, 0:NT * G].rearrange("p (t g) -> p t g", g=G)
            for t in range(NT):
                ins = pe.matmul(logits[:, t, :], lhsT=X[:, t * P:t * P + P], rhs=wg[:, :], start=True, stop=True)
            ins.then_inc(logits_ready, 1)
            pe.wait_ge(gate_step, 11)
            for c in range(CHUNKS):
                if c >= 2:
                    pe.wait_ge(turned_kept, c - 1)
                for j in range(CH // P):
                    ins = pe.transpose(n_bank[c % 2][0:EXPERTS, j * P:j * P + P], wt[:, c * (CH // P) + j, :], ident)
                ins.then_inc(turned, 1)
            pe.wait_ge(loaded, 16 * (3 + EXPERTS))
            pe.wait_ge(select_step, 2)
            with pe.Fori(0, CHUNKS) as c:
                pe.wait_ge(x_ready, c * 2 + 2)

                def accumulate(u):
                    e, f = u // FB, u % FB
                    pe.wait_ge(gelu_ready, c * UNITS + (u + 1))
                    if f == 0 and e >= 2:
                        pe.wait_ge(weighted, c * EXPERTS + (e - 1))
                    pe.matmul(o_bank[e % 2][:, :], lhsT=w2[:, e, f, :], rhs=hid[:, u % 4, :], start=f == 0,
                              stop=f == FB - 1).then_inc(out_mm, 1)

                for u in range(UNITS):
                    e, f = u // FB, u % FB
                    if f == 0:
                        if e >= 1:
                            pe.wait_ge(spread_kept, c * EXPERTS + e)
                        pe.matmul(w_bank[:, :], lhsT=select[:, e, :], rhs=wc[:, :], start=True, stop=True).then_inc(spread_mm, 1)
                    if u >= 3:
                        pe.wait_ge(gelu_ready, c * UNITS + (u - 2))
                    pe.matmul(h_bank[u % 3][:, :], lhsT=w1[:, e, f * P:f * P + P], rhs=xs[:, :], start=True,
                              stop=True).then_inc(hid_mm, 1)
                    if u >= 2:
                        accumulate(u - 2)
                accumulate(UNITS - 2)
                accumulate(UNITS - 1)
                pe.matmul(n_bank[1][:, :], lhsT=b2[:, :], rhs=wc[:, :], start=True, stop=True).then_inc(bias_mm, 1)
                pe.wait_ge(res_ready, c * 2 + 2)
                norm_pe(pe, ln, c, mean_w, res[:, :], cent_sq[:, :], n_bank[0][:, :], n_bank[1][:, :])

        @block.scalar
        def _(act):
            act.wait_ge(gate_step, 3)
            act.activation(ex[:, :, :], ex[:, :, :], ACT.Exp).then_inc(gate_act, 1)
            act.activation(thr[:, :], logit[:, :, EXPERTS], ACT.Sigmoid).then_inc(gate_act, 1)
            for c in range(CHUNKS):
                act.wait_ge(turned, c + 1)
                act.activation(w_rows[:, c * CH:c * CH + CH], n_bank[c % 2][0:EXPERTS, :], ACT.Copy).then_inc(turned_kept, 1)
            act.wait_ge(turned_kept, CHUNKS)
            act.wait_ge(loaded, 16 * (3 + EXPERTS))
            with act.Fori(0, CHUNKS) as c:
                act.wait_ge(done, c)
                act.activation(xs[:, :], X[:, bass.ds(c * CH, CH)], ACT.Copy).then_inc(x_ready, 1)
                act.activation(wc[:, :], w_rows[:, bass.ds(c * CH, CH)], ACT.Copy).then_inc(x_ready, 1)
                for u in range(UNITS):
                    e, f = u // FB, u % FB
                    if f == 0:
                        act.wait_ge(spread_mm, c * EXPERTS + (e + 1))
                        if e >= 2:
                            act.wait_ge(weighted, c * EXPERTS + (e - 1))
                        act.activation(wb[:, e % 2, :], w_bank[:, :], ACT.Copy).then_inc(spread_kept, 1)
                    act.wait_ge(hid_mm, c * UNITS + (u + 1))
                    if u >= 4:
                        act.wait_ge(out_mm, c * UNITS + (u - 3))
                    act.activation(hid[:, u % 4, :], h_bank[u % 3][:, :], ACT.Gelu_apprx_tanh, bias=b1[:, u:u + 1]).then_inc(gelu_ready, 1)
                norm_act(act, ln, c, cent[:, :], cent_sq[:, :], n_bank[1][:, :], std[:, :], eps)

        @block.vector
        def _(dve):
            dve.wait_ge(logits_ready, 1)
            dve.tensor_tensor(logit[:, :, :], n_bank[0][:, 0:NT * G].rearrange("p (t g) -> p t g", g=G),
                              bg[:, :].unsqueeze(1).to_broadcast([P, NT, G]), ALU.add).then_inc(gate_step, 1)
            dve.wait_ge(gate_step, 1)
            dve.tensor_reduce(top[:, :], logit[:, :, 0:EXPERTS], AX.X, ALU.max).then_inc(gate_step, 1)
            dve.wait_ge(gate_step, 2)
            dve.tensor_tensor(ex[:, :, :], logit[:, :, 0:EXPERTS], top[:, :].unsqueeze(2).to_broadcast([P, NT, EXPERTS]),
                              ALU.subtract).then_inc(gate_step, 1)
            dve.wait_ge(gate_act, 2)
            dve.tensor_reduce(total[:, :], ex[:, :, :], AX.X, ALU.add).then_inc(gate_step, 1)
            dve.wait_ge(gate_step, 4)
            dve.reciprocal(inv[:, :], total[:, :]).then_inc(gate_step, 1)
            dve.wait_ge(gate_step, 5)
            dve.tensor_tensor(wt[:, :, :], ex[:, :, :], inv[:, :].unsqueeze(2).to_broadcast([P, NT, EXPERTS]), ALU.mult).then_inc(gate_step, 1)
            dve.wait_ge(gate_step, 6)
            dve.tensor_scalar(fix[:, :], thr[:, :], THRESHOLD, None, ALU.mult).then_inc(gate_step, 1)
            dve.wait_ge(gate_step, 7)
            dve.tensor_tensor(ex[:, :, :], wt[:, :, :], fix[:, :].unsqueeze(2).to_broadcast([P, NT, EXPERTS]),
                              ALU.subtract).then_inc(gate_step, 1)
            dve.wait_ge(gate_step, 8)
            dve.tensor_scalar(wt[:, :, :], ex[:, :, :], 0.0, None, ALU.max).then_inc(gate_step, 1)
            dve.wait_ge(gate_step, 9)
            dve.tensor_reduce(total[:, :], wt[:, :, :], AX.X, ALU.add).then_inc(gate_step, 1)
            dve.wait_ge(gate_step, 10)
            dve.scalar_tensor_tensor(fix[:, :], total[:, :], 0.0, total[:, :], ALU.is_equal, ALU.add).then_inc(gate_fix, 1)
            dve.wait_ge(gate_fix, 1)
            dve.reciprocal(inv[:, :], fix[:, :]).then_inc(gate_fix, 1)
            dve.wait_ge(gate_fix, 2)
            dve.tensor_tensor(wt[:, :, :], wt[:, :, :], inv[:, :].unsqueeze(2).to_broadcast([P, NT, EXPERTS]), ALU.mult).then_inc(gate_step, 1)
            with dve.Fori(0, CHUNKS) as c:
                for e in range(EXPERTS):
                    dve.wait_ge(out_mm, c * UNITS + (FB * e + FB))
                    dve.wait_ge(spread_kept, c * EXPERTS + (e + 1))
                    if e >= 2:
                        dve.wait_ge(summed, c * (EXPERTS - 1) + (e - 1))
                    dst = acc[:, :] if e == 0 else part[:, e % 2, :]
                    dve.tensor_tensor(dst, wb[:, e % 2, :], o_bank[e % 2][:, :], ALU.mult).then_inc(weighted, 1)
                    if e >= 1:
                        dve.wait_ge(weighted, c * EXPERTS + (e + 1))
                        dve.tensor_tensor(acc[:, :], acc[:, :], part[:, e % 2, :], ALU.add).then_inc(summed, 1)
                dve.wait_ge(bias_mm, c + 1)
                dve.wait_ge(summed, c * (EXPERTS - 1) + (EXPERTS - 1))
                dve.tensor_tensor(acc[:, :], acc[:, :], n_bank[1][:, :], ALU.add).then_inc(res_ready, 1)
                dve.wait_ge(res_ready, c * 2 + 1)
                dve.tensor_tensor(res[:, :], acc[:, :], xs[:, :], ALU.add).then_inc(res_ready, 1)
                dve.wait_ge(res_ready, c * 2 + 2)
                norm_dve(dve, ln, c, res[:, :], cent[:, :], std[:, :], rstd[:, :], n_bank[0][:, :])
                dve.tensor_tensor(X[:, bass.ds(c * CH, CH)], cent[:, :], rstd[:, :], ALU.mult).then_inc(done, 1)
                dve.wait_ge(done, c + 1)


HEADS = 16
HD = 8
GROUPS = 8
Q_PART = (0, 0, 1, 1, 0, 2, 1, 2)
K_PART = (0, 1, 0, 1, 2, 0, 2, 1)
KROWS = GROUPS * HD
QROWS = KROWS + 3
MASKED = -1e30
ROW_PIECES = [(i, lo, min(CH, P * (i + 1) - lo), lo + CH >= P * (i + 1)) for i in range(SEQ // P)
              for lo in range(0, P * (i + 1), CH)]
COL_PIECES = [(j, lo, CH - lo % CH) for j in range(SEQ // P) for lo in ([P * j, CH] if P * j < CH else [P * j])]
NP1 = len(ROW_PIECES)
NP2 = len(COL_PIECES)
TILES = SEQ // P
PROB_AT = [sum(SEQ - P * k for k in range(j)) for j in range(TILES + 1)]
PROB_COLS = PROB_AT[TILES]


def mqa(nc, sem, X, X1, d, consts):
    ident, mean_w, eps = consts
    with ExitStack() as mem:
        def sb(label, shape, dt=F32):
            return mem.enter_context(nc.sbuf_tensor(f"q_{label}", shape, dt))

        def bank(label):
            return mem.enter_context(nc.psum_tensor(f"q_{label}", [P, CH], F32))

        wq = sb("wq", [P, DIM])
        wk = sb("wk", [P, KROWS])
        wv = sb("wv", [P, HD])
        bq = sb("bq", [P, 1])
        bk = sb("bk", [KROWS, 1])
        bv = sb("bv", [P, HD])
        k_pick = sb("k_pick", [KROWS, 3])
        w_out = sb("w_out", [P, DIM])
        b_out = sb("b_out", [P, 1])
        ident16 = sb("ident16", [P, P], BF16)
        mask_row = sb("mask_row", [P, P], BF16)
        mask_col = sb("mask_col", [P, P], BF16)
        mask_f = sb("mask_f", [P, P])
        qf = sb("q", [P, 2, CH])
        qr = sb("q_rest", [P, 2, CH])
        qp = sb("q_parts", [P, 2, 3, CH], BF16)
        kf = sb("k", [KROWS, CH])
        kr = sb("k_rest", [KROWS, 2, CH])
        kp = sb("k_parts", [KROWS, 3, CH], BF16)
        kt = sb("k_sum", [KROWS, 2, CH])
        keys = sb("keys", [QROWS, 2, TOKENS], BF16)
        vals = sb("values", [P, NT, HD + 1])
        q_all = sb("q_all", [QROWS, HEADS, SEQ], BF16)
        k_now = sb("keys_now", [QROWS, 2, SEQ], BF16)
        v_now = sb("values_now", [P, TILES, HD + 1])
        piece_max = sb("piece_max", [P, NP1])
        pair_max = sb("pair_max", [P, TILES])
        neg_max = sb("neg_max", [P, 2, TILES])
        m_rest = sb("max_rest", [TILES, 2, P])
        m_part = sb("max_parts", [TILES, 2, 3, P], BF16)
        probs = [sb(f"probs{i}", [P, PROB_COLS]) for i in range(2)]
        inv = sb("inverse", [P, 2, TILES])
        att_t = sb("attended_t", [P, 2, CH])
        att = X1[:, :].rearrange("p (n h v) -> p n h v", h=HEADS, v=HD)
        s_bank = [bank(f"s_bank{i}") for i in range(2)]
        t_bank = [bank(f"t_bank{i}") for i in range(3)]
        o_bank = [bank(f"o_bank{i}") for i in range(2)]
        m_bank = bank("m_bank")
        parts_dram = nc.dram_tensor("q_parts_dram", (BATCH, 3, P, SEQ), BF16, kind="Internal").ap()

        loaded = sem("q_weights_loaded")
        mask_step = sem("q_mask_step")
        proj_mm = sem("q_projection_ready")
        proj_kept = sem("q_projection_kept")
        v_kept = sem("q_values_kept")
        q_step = sem("q_split_step")
        k_step = sem("q_key_split_step")
        stored = [sem(f"q_parts_stored{i}") for i in range(2)]
        CHUNKS = TOKENS // CH
        phase = ExitStack()
        block = phase.enter_context(nc.Block())

        @block.sync
        def _(sp):
            w = d["q_wqkv"]
            sp.dma_start(wq[:, :], w[:, 0:DIM]).then_inc(loaded, 16)
            for g in range(GROUPS):
                sp.dma_start(wk[:, g * HD:g * HD + HD], w[:, DIM:DIM + HD]).then_inc(loaded, 16)
                sp.dma_start(bk[g * HD:g * HD + HD, :], d["q_bias"][DIM:DIM + HD, :]).then_inc(loaded, 16)
            sp.dma_start(wv[:, :], w[:, DIM + HD:DIM + 2 * HD]).then_inc(loaded, 16)
            sp.dma_start(bq[:, :], d["q_bias"][0:DIM, :]).then_inc(loaded, 16)
            sp.dma_start(bv[:, :], d["q_value_bias"]).then_inc(loaded, 16)
            sp.dma_start(k_pick[:, :], d["q_key_pick"]).then_inc(loaded, 16)
            sp.dma_start(w_out[:, :], d["q_w_out"]).then_inc(loaded, 16)
            sp.dma_start(b_out[:, :], d["q_b_out"]).then_inc(loaded, 16)
            for c in range(CHUNKS):
                sp.wait_ge(q_step, 5 * c + 5)
                sp.dma_start(parts_dram[c // 2, :, :, (c % 2) * CH:(c % 2) * CH + CH].rearrange("s p t -> p s t"),
                             qp[:, c % 2, :, :]).then_inc(stored[c % 2], 16)
            for slot in range(2):
                sp.wait_ge(stored[slot], 16 * CHUNKS // 2)

        @block.gpsimd
        def _(pool):
            pool.memset(mask_f[:, :], 0.0).then_inc(mask_step, 1)
            pool.wait_ge(mask_step, 1)
            pool.affine_select(out=mask_row[:, :], in_=mask_f[:, :], pattern=[[-1, P]], compare_op=ALU.is_ge, fill=MASKED,
                               base=0, channel_multiplier=1).then_inc(mask_step, 1)
            pool.affine_select(out=mask_col[:, :], in_=mask_f[:, :], pattern=[[1, P]], compare_op=ALU.is_ge, fill=MASKED,
                               base=0, channel_multiplier=-1).then_inc(mask_step, 1)

        @block.tensor
        def _(pe):
            pe.wait_ge(loaded, 16 * (2 * GROUPS + 7))
            for c in range(CHUNKS):
                x = X[:, c * CH:c * CH + CH]
                if c >= 2:
                    pe.wait_ge(proj_kept, 2 * (c - 1))
                pe.matmul(s_bank[c % 2][:, :], lhsT=wq[:, :], rhs=x, start=True, stop=True).then_inc(proj_mm, 1)
                pe.matmul(o_bank[c % 2][0:KROWS, :], lhsT=wk[:, :], rhs=x, start=True, stop=True).then_inc(proj_mm, 1)
                if c >= 2:
                    pe.wait_ge(v_kept, c - 1)
                for j in range(CH // P):
                    ins = pe.matmul(t_bank[c % 2][:, j * HD:j * HD + HD], lhsT=X[:, c * CH + j * P:c * CH + j * P + P], rhs=wv[:, :],
                                    start=True, stop=True)
                ins.then_inc(proj_mm, 1)

        @block.scalar
        def _(act):
            act.activation(ident16[:, :], ident, ACT.Copy)
            act.wait_ge(loaded, 16 * (2 * GROUPS + 7))
            for c in range(CHUNKS):
                act.wait_ge(proj_mm, 3 * c + 1)
                if c >= 2:
                    act.wait_ge(q_step, 5 * (c - 1))
                act.activation(qf[:, c % 2, :], s_bank[c % 2][:, :], ACT.Identity, bias=bq[:, :]).then_inc(proj_kept, 1)
                act.wait_ge(proj_mm, 3 * c + 2)
                if c >= 1:
                    act.wait_ge(k_step, 8 * c)
                act.activation(kf[:, :], o_bank[c % 2][0:KROWS, :], ACT.Identity, bias=bk[:, :]).then_inc(proj_kept, 1)

        @block.vector
        def _(dve):
            dve.memset(vals[:, :, HD:HD + 1], 1.0)
            dve.memset(keys[KROWS:QROWS, 0, :], 0.0)
            dve.memset(keys[KROWS:QROWS, 1, :], 1.0)
            dve.memset(q_all[KROWS:QROWS, :, :], 0.0)
            for c in range(CHUNKS):
                dve.wait_ge(proj_mm, 3 * c + 3)
                dve.tensor_tensor(vals[:, 4 * c:4 * c + 4, 0:HD], t_bank[c % 2][:, 0:4 * HD].rearrange("p (t v) -> p t v", v=HD),
                                  bv[:, :].unsqueeze(1).to_broadcast([P, 4, HD]), ALU.add).then_inc(v_kept, 1)
                q, r, s = qf[:, c % 2, :], qr, qp[:, c % 2]
                dve.wait_ge(proj_kept, 2 * c + 1)
                if c >= 2:
                    dve.wait_ge(stored[c % 2], 16 * (c // 2))
                dve.tensor_copy(s[:, 0, :], q).then_inc(q_step, 1)
                dve.wait_ge(q_step, 5 * c + 1)
                dve.tensor_tensor(r[:, 0, :], q, s[:, 0, :], ALU.subtract).then_inc(q_step, 1)
                dve.wait_ge(q_step, 5 * c + 2)
                dve.tensor_copy(s[:, 1, :], r[:, 0, :]).then_inc(q_step, 1)
                dve.wait_ge(q_step, 5 * c + 3)
                dve.tensor_tensor(r[:, 1, :], r[:, 0, :], s[:, 1, :], ALU.subtract).then_inc(q_step, 1)
                dve.wait_ge(q_step, 5 * c + 4)
                dve.tensor_copy(s[:, 2, :], r[:, 1, :]).then_inc(q_step, 1)
                dve.wait_ge(proj_kept, 2 * c + 2)
                dve.tensor_copy(kp[:, 0, :], kf[:, :]).then_inc(k_step, 1)
                dve.wait_ge(k_step, 8 * c + 1)
                dve.tensor_tensor(kr[:, 0, :], kf[:, :], kp[:, 0, :], ALU.subtract).then_inc(k_step, 1)
                dve.wait_ge(k_step, 8 * c + 2)
                dve.tensor_copy(kp[:, 1, :], kr[:, 0, :]).then_inc(k_step, 1)
                dve.wait_ge(k_step, 8 * c + 3)
                dve.tensor_tensor(kr[:, 1, :], kr[:, 0, :], kp[:, 1, :], ALU.subtract).then_inc(k_step, 1)
                dve.wait_ge(k_step, 8 * c + 4)
                dve.tensor_scalar(kt[:, 0, :], kp[:, 0, :], k_pick[:, 0:1], None, ALU.mult).then_inc(k_step, 1)
                dve.tensor_copy(kp[:, 2, :], kr[:, 1, :]).then_inc(k_step, 1)
                dve.wait_ge(k_step, 8 * c + 6)
                dve.scalar_tensor_tensor(kt[:, 1, :], kp[:, 1, :], k_pick[:, 1:2], kt[:, 0, :], ALU.mult, ALU.add).then_inc(k_step, 1)
                dve.wait_ge(k_step, 8 * c + 7)
                for slot in range(2):
                    ins = dve.scalar_tensor_tensor(keys[0:KROWS, slot, c * CH:c * CH + CH], kp[:, 2, :], k_pick[:, 2:3], kt[:, 1, :],
                                                   ALU.mult, ALU.add)
                ins.then_inc(k_step, 1)
                dve.wait_ge(k_step, 8 * c + 8)

        phase.close()

        q_landed = sem("q_queries_landed")
        batch_copied = sem("q_batch_copied")
        row_scores = sem("q_row_scores_ready")
        row_max = sem("q_piece_max_ready")
        neg_ready = sem("q_neg_max_ready")
        max_turned = sem("q_max_turned")
        max_step = sem("q_max_split_step")
        max_landed = sem("q_max_rows_landed")
        col_scores = sem("q_col_scores_ready")
        exp_ready = sem("q_exps_ready")
        out_mm = sem("q_head_out_ready")
        norm_step = sem("q_norm_step")
        NMAX = 3

        def hcount(b, h, per, k):
            return b * (HEADS * per) + (h * per + k)

        phase = ExitStack()
        block = phase.enter_context(nc.Block())

        @block.sync
        def _(sp):
            with sp.Fori(0, BATCH) as b:
                sp.wait_ge(out_mm, b * HEADS)
                for g in range(GROUPS):
                    src = parts_dram[bass.ds(b, 1), Q_PART[g]].rearrange("o (h j) t -> j (o h) t", j=HD)
                    sp.dma_start(q_all[g * HD:g * HD + HD, :, :], src).then_inc(q_landed, 16)
                with sp.Fori(0, HEADS) as h:
                    sp.wait_ge(max_step, hcount(b, h, 5, 5))
                    for k in range(3):
                        sp.dma_start(q_all[KROWS + k:KROWS + k + 1, bass.ds(h, 1), :],
                                     m_part[:, 0, k, :]).then_inc(max_landed, 16)

        @block.tensor
        def _(pe):
            with pe.Fori(0, BATCH) as b:
                pe.wait_ge(batch_copied, b * 3 + 3)
                pe.wait_ge(q_landed, b * (16 * GROUPS) + 16 * GROUPS)

                def rows(h):
                    for n, (i, lo, size, last) in enumerate(ROW_PIECES):
                        pe.wait_ge(row_max, hcount(b, h, NP1, max(n - 1, 0)))
                        ins = pe.matmul(s_bank[n % 2][:, 0:size], lhsT=q_all[:, bass.ds(h, 1), i * P:i * P + P],
                                        rhs=k_now[:, 0, lo:lo + size], start=True, stop=not last)
                        if last:
                            ins = pe.matmul(s_bank[n % 2][:, size - P:size], lhsT=ident16[:, :], rhs=mask_row[:, :], start=False,
                                            stop=True)
                        ins.then_inc(row_scores, 1)

                def turn(h, slot):
                    pe.wait_ge(neg_ready, hcount(b, h, NMAX, NMAX))
                    pe.transpose(m_bank[0:TILES, 0:P], neg_max[:, slot, :], ident).then_inc(max_turned, 1)

                def cols(h, slot, turn_next):
                    pe.wait_ge(max_landed, hcount(b, h, 48, 48))

                    def product(i):
                        n_own = next(n for n, (j, lo, _) in enumerate(COL_PIECES) if j == i)
                        pe.wait_ge(exp_ready, hcount(b, h, NP2, n_own + 1))
                        for j in range(i + 1):
                            at = PROB_AT[j] + (i - j) * P
                            ins = pe.matmul(o_bank[slot][:, i * 16:i * 16 + HD + 1], lhsT=probs[slot][:, at:at + P],
                                            rhs=v_now[:, j, :], start=j == 0, stop=j == i)
                        return ins

                    for n, (j, lo, size) in enumerate(COL_PIECES):
                        pe.wait_ge(exp_ready, hcount(b, h, NP2, max(n - 2, 0)))
                        first = lo == j * P
                        ins = pe.matmul(t_bank[n % 3][:, 0:size], lhsT=k_now[:, 1, j * P:j * P + P],
                                        rhs=q_all[:, bass.ds(h, 1), lo:lo + size], start=True, stop=not first)
                        if first:
                            ins = pe.matmul(t_bank[n % 3][:, 0:P], lhsT=ident16[:, :], rhs=mask_col[:, :], start=False, stop=True)
                        ins.then_inc(col_scores, 1)
                        if first and j >= 2:
                            product(j - 2)
                        if n == 5 and turn_next:
                            turn(h + 1, 1 - slot)
                    product(TILES - 2)
                    product(TILES - 1).then_inc(out_mm, 1)

                rows(0)
                turn(0, 0)
                with pe.Fori(0, HEADS // 2 - 1) as g:
                    rows(g * 2 + 1)
                    cols(g * 2, 0, True)
                    rows(g * 2 + 2)
                    cols(g * 2 + 1, 1, True)
                rows(HEADS - 1)
                cols(HEADS - 2, 0, True)
                cols(HEADS - 1, 1, False)

        @block.scalar
        def _(act):
            with act.Fori(0, BATCH) as b:
                act.wait_ge(out_mm, b * HEADS)
                for slot in range(2):
                    act.activation(k_now[:, slot, :], keys[:, slot, bass.ds(b * SEQ, SEQ)], ACT.Copy).then_inc(batch_copied, 1)
                act.activation(v_now[:, :, :], vals[:, bass.ds(b * TILES, TILES), :], ACT.Copy).then_inc(batch_copied, 1)

                def exps(h, slot):
                    for n, (j, lo, size) in enumerate(COL_PIECES):
                        act.wait_ge(col_scores, hcount(b, h, NP2, n + 1))
                        at = PROB_AT[j] + lo - j * P
                        act.activation(probs[slot][:, at:at + size], t_bank[n % 3][:, 0:size], ACT.Exp,
                                       scale=float(HD) ** -0.5).then_inc(exp_ready, 1)

                with act.Fori(0, HEADS // 2) as g:
                    exps(g * 2, 0)
                    exps(g * 2 + 1, 1)

        @block.vector
        def _(dve):
            with dve.Fori(0, BATCH) as b:
                def reduces(h, first, end):
                    for n in range(first, end):
                        dve.wait_ge(row_scores, hcount(b, h, NP1, n + 1))
                        dve.tensor_reduce(piece_max[:, n:n + 1], s_bank[n % 2][:, 0:ROW_PIECES[n][2]], AX.X, ALU.max).then_inc(row_max, 1)

                def negate(h, slot):
                    dve.wait_ge(row_max, hcount(b, h, NP1, NP1))
                    dve.tensor_scalar(neg_max[:, slot, 0:4], piece_max[:, 0:4], -1.0, None, ALU.mult).then_inc(neg_ready, 1)
                    two = piece_max[:, 4:NP1].rearrange("p (i s) -> p i s", s=2)
                    dve.tensor_tensor(pair_max[:, 4:TILES], two[:, :, 0], two[:, :, 1], ALU.max).then_inc(neg_ready, 1)
                    dve.wait_ge(neg_ready, hcount(b, h, NMAX, 2))
                    dve.tensor_scalar(neg_max[:, slot, 4:TILES], pair_max[:, 4:TILES], -1.0, None, ALU.mult).then_inc(neg_ready, 1)

                def split(h, slot):
                    dve.wait_ge(max_turned, hcount(b, h, 1, 1))
                    dve.wait_ge(max_landed, hcount(b, h, 48, 0))
                    m, r, s = m_bank[0:TILES, 0:P], m_rest, m_part[:, 0]
                    dve.tensor_copy(s[:, 0, :], m).then_inc(max_step, 1)
                    dve.wait_ge(max_step, hcount(b, h, 5, 1))
                    dve.tensor_tensor(r[:, 0, :], m, s[:, 0, :], ALU.subtract).then_inc(max_step, 1)
                    dve.wait_ge(max_step, hcount(b, h, 5, 2))
                    dve.tensor_copy(s[:, 1, :], r[:, 0, :]).then_inc(max_step, 1)
                    dve.wait_ge(max_step, hcount(b, h, 5, 3))
                    dve.tensor_tensor(r[:, 1, :], r[:, 0, :], s[:, 1, :], ALU.subtract).then_inc(max_step, 1)
                    dve.wait_ge(max_step, hcount(b, h, 5, 4))
                    dve.tensor_copy(s[:, 2, :], r[:, 1, :]).then_inc(max_step, 1)

                def normalise(h, slot):
                    dve.wait_ge(out_mm, hcount(b, h, 1, 1))
                    o = o_bank[slot][:, 0:16 * TILES].rearrange("p (i v) -> p i v", v=16)
                    dve.reciprocal(inv[:, slot, :], o[:, :, HD]).then_inc(norm_step, 1)
                    dve.wait_ge(norm_step, hcount(b, h, 2, 1))
                    dve.tensor_tensor(att[:, bass.ds(b * TILES, TILES), bass.ds(h, 1), :].squeeze(2), o[:, :, 0:HD],
                                      inv[:, slot, :].unsqueeze(2).to_broadcast([P, TILES, HD]), ALU.mult).then_inc(norm_step, 1)

                def step(h, slot):
                    reduces(h + 1, 0, 4)
                    split(h, slot)
                    reduces(h + 1, 4, NP1)
                    negate(h + 1, 1 - slot)
                    normalise(h, slot)

                reduces(0, 0, NP1)
                negate(0, 0)
                with dve.Fori(0, HEADS // 2 - 1) as g:
                    step(g * 2, 0)
                    step(g * 2 + 1, 1)
                step(HEADS - 2, 0)
                split(HEADS - 1, 1)
                normalise(HEADS - 1, 1)

        phase.close()
        turned = sem("q_att_turned")
        att_kept = sem("q_att_kept")
        proj = sem("q_out_projected")
        x1_step = sem("q_x1_step")
        block = mem.enter_context(nc.Block())

        @block.tensor
        def _(pe):
            flat = X1[:, :]
            for c in range(CHUNKS):
                if c >= 2:
                    pe.wait_ge(att_kept, c - 1)
                for j in range(CH // P):
                    t = c * (CH // P) + j
                    ins = pe.transpose(s_bank[c % 2][:, j * P:j * P + P], flat[:, t * P:t * P + P], ident)
                ins.then_inc(turned, 1)
                pe.wait_ge(att_kept, c + 1)
                if c >= 2:
                    pe.wait_ge(x1_step, 2 * (c - 1))
                pe.matmul(t_bank[c % 2][:, :], lhsT=w_out[:, :], rhs=att_t[:, c % 2, :], start=True, stop=True).then_inc(proj, 1)

        @block.scalar
        def _(act):
            for c in range(CHUNKS):
                act.wait_ge(turned, c + 1)
                if c >= 2:
                    act.wait_ge(proj, c - 1)
                act.activation(att_t[:, c % 2, :], s_bank[c % 2][:, :], ACT.Copy).then_inc(att_kept, 1)

        @block.vector
        def _(dve):
            for c in range(CHUNKS):
                dve.wait_ge(proj, c + 1)
                x1 = X1[:, c * CH:c * CH + CH]
                dve.scalar_tensor_tensor(x1, t_bank[c % 2][:, :], b_out[:, 0:1], X[:, c * CH:c * CH + CH], ALU.add, ALU.add).then_inc(x1_step, 2)


DEPTH = 6
LH = 16
LD = 64
INNER = LH * LD
WINDOW = 32
FFI = 341
FF_BLOCKS = ((0, P), (P, P), (2 * P, FFI - 2 * P))
HG = 4
NG = LH // HG
QK_SCALE = 8.0
OUT_BANKS = ((0, 7), (7, 14), (14, 16))
NORM_SCALE = 2.0 ** 20
LANES = 8 * LD


def head_of(g, j):
    return g // 2 * 8 + 2 * j + g % 2


PLACES = [head_of(g, j) for g in range(NG) for j in range(HG)]


def rotary_tables():
    f = np.float32
    half = np.arange(0, LD, 2, dtype=f)
    inv_freq = (f(1.0) / np.power(f(10000.0), half / f(LD))).astype(f)
    t = np.arange(SEQ, dtype=f)
    freqs = (t[:, None] * inv_freq[None, :]).astype(f)
    base = ((half + f(0.4 * LD)) / f(1.4 * LD)).astype(f)
    power = ((t - SEQ // 2) / f(WINDOW // 2)).astype(f)
    scale = np.power(base[None, :], power[:, None]).astype(f)
    cos, sin = np.cos(freqs).astype(f), np.sin(freqs).astype(f)
    inv = (f(1.0) / scale).astype(f)
    both = lambda a, b: np.concatenate([a, b], axis=1)
    tables = np.stack([both(cos * scale, cos * scale), both(-sin * scale, sin * scale),
                       both(cos * inv, cos * inv), both(-sin * inv, sin * inv)], axis=1)
    return np.ascontiguousarray(tables.reshape(TILES, P, 4, LD).transpose(1, 0, 2, 3).astype(f))


def local_layers(nc, sem, Xp, X1p, d, consts):
    ident, mean_w, eps = consts
    X, X1 = Xp[:, 1:], X1p[:, 1:]
    with ExitStack() as mem:
        def sb(label, shape, dt=F32):
            return mem.enter_context(nc.sbuf_tensor(f"d_{label}", shape, dt))

        def bank(label):
            return mem.enter_context(nc.psum_tensor(f"d_{label}", [P, CH], F32))

        w_qkv = sb("w_qkv", [P, 3 * INNER])
        w_o = sb("w_o", [P, INNER // P, DIM])
        w_1 = sb("w_1", [P, 2 * FFI])
        w_2 = sb("w_2", [P, 3, DIM])
        b_1 = sb("b_1", [P, 6])
        vec = sb("vectors", [P, 3])
        base = sb("rotary", [P, TILES, 4, LD])
        table = sb("scaled_rotary", [P, TILES, 4, LD])
        qk_scale = sb("qk_scale", [P, 4, LD])
        ident16 = sb("ident16", [P, P], BF16)
        mask = sb("mask", [P, HG, P], BF16)
        mask_prev = sb("mask_prev", [WINDOW, LH, WINDOW], BF16)
        mask_now = sb("mask_now", [WINDOW, LH, WINDOW], BF16)
        shown = sb("shown", [P, NT])
        hidden = sb("hidden", [P, NT])
        norm_bias = sb("norm_bias", [P, 1])
        xs = [sb(f"x{i}", [P, P]) for i in range(2)]
        sq = sb("squares", [P, 2, 8, LD])
        t1 = sb("rotated1", [P, 4, 8, LD])
        t2 = sb("rotated2", [P, 4, 8, LD])
        ssq = sb("square_sums", [P, 4 * 8])
        ssq_c = sb("square_sums_guarded", [P, 4 * 8])
        ssq_l = sb("square_sums_log", [P, 4 * 8])
        inv_n = sb("inverse_norms", [P, 4 * 8])
        q_t = sb("q_turned", [P, LH // 2, P])
        k_t = [sb(f"k_turned{i}", [P, LH // 2, P]) for i in range(2)]
        v = [sb(f"v{i}", [P, LH, LD + 1]) for i in range(2)]
        v_prev = [sb(f"v_prev{i}", [P, NG, HG, LD + 1]) for i in range(2)]
        top = sb("top", [P, LH])
        top_prev = sb("top_prev", [WINDOW, LH])
        z = sb("exps", [P, NG, HG, P])
        z_prev = sb("exps_prev", [WINDOW, LH, WINDOW])
        pt = sb("probs_turned", [P, NG, HG, P])
        pt_prev = sb("probs_turned_prev", [P, NG, P])
        inv_s = sb("inverse_sums", [P, LH])
        att = sb("attended", [P, LH, LD])
        att_t = sb("attended_turned", [P, INNER // P, P])
        flat = lambda t: t[:, :, :, :].rearrange("p a b c -> p (a b c)")
        f1, f2 = flat(t1), flat(t2)
        fx = [f1[:, i * CH:i * CH + CH] for i in range(2)]
        fc = [f1[:, (2 + i) * CH:(3 + i) * CH] for i in range(2)]
        fq = [f2[:, i * CH:i * CH + CH] for i in range(2)]
        fl = [f2[:, (2 + i) * CH:(3 + i) * CH] for i in range(2)]
        zf, pf = flat(z), flat(pt)
        fr = [zf[:, i * CH:i * CH + CH] for i in range(2)]
        fn = [zf[:, (2 + i) * CH:(3 + i) * CH] for i in range(2)]
        gl = [pf[:, i * CH:i * CH + CH] for i in range(2)]
        hh = [pf[:, (2 + i) * CH:(3 + i) * CH] for i in range(2)]
        hh += [flat(table)[:, 0:CH]]
        s_b = [bank(f"s_bank{i}") for i in range(3)]
        p_b = [bank(f"p_bank{i}") for i in range(2)]
        t_b = [bank(f"t_bank{i}") for i in range(2)]
        w_b = bank("w_bank")
        rotary = nc.inline_tensor(rotary_tables(), "rotary_tables").ap()
        kept_x = nc.dram_tensor("x_before_local", (P, TOKENS), F32, kind="Internal").ap()

        setup = sem("d_setup")
        setup_loads = sem("d_setup_loads")
        x_stored = sem("d_x_stored")
        qkv_loaded = sem("d_qkv_loaded")
        ffn_loaded = sem("d_ffn_loaded")
        table_step = sem("d_table_step")
        x_ready = sem("d_x_ready")
        proj = sem("d_projected")
        sq_ready = sem("d_squares_ready")
        rope_ready = sem("d_rope_ready")
        rope_sum = sem("d_rope_sum_ready")
        ssq_step = sem("d_square_sum_step")
        inv_step = sem("d_inverse_norm_step")
        unit_ready = sem("d_unit_ready")
        v_kept = sem("d_v_kept")
        vp_landed = [sem(f"d_v_prev_landed{i}") for i in range(2)]
        qk_turned = sem("d_qk_turned")
        qk_kept = sem("d_qk_kept")
        mask_ready = sem("d_mask_ready")
        even_done = sem("d_even_heads_done")
        scores = sem("d_scores_ready")
        max_step = sem("d_max_step")
        sub_ready = sem("d_less_max_ready")
        exp_ready = sem("d_exps_ready")
        p_turned = sem("d_probs_turned")
        p_kept = sem("d_probs_kept")
        out_mm = sem("d_attended_ready")
        out_inv = sem("d_inverse_sum_ready")
        out_norm = sem("d_attended_normed")
        a_turned = sem("d_attended_turned")
        a_kept = sem("d_attended_kept")
        o_mm = sem("d_out_projected")
        x1_ready = sem("d_x1_ready")
        f_x = sem("d_ff_x_ready")
        f_mean = sem("d_ff_mean_ready")
        f_cent = sem("d_ff_centred_ready")
        f_sq = sem("d_ff_squares_ready")
        f_var = sem("d_ff_variance_ready")
        f_rstd = sem("d_ff_rstd_step")
        f_norm = sem("d_ff_normed_step")
        f_gate = sem("d_ff_gate_ready")
        f_lin = sem("d_ff_linear_ready")
        f_gelu = sem("d_ff_gelu_ready")
        f_prod = sem("d_ff_product_ready")
        f_out = sem("d_ff_out_ready")
        f_done = sem("d_ff_chunk_done")
        b_step = sem("d_ff_bias_step")
        CHUNKS = TOKENS // CH
        STEPS = NT
        QKV_LOADS = 16 * 5
        FFN_LOADS = 16 * 4

        with nc.Block() as block:
            @block.sync
            def _(sp):
                sp.dma_start(base[:, :, :, :], rotary).then_inc(setup_loads, 16)
                sp.dma_start(kept_x, X[:, 0:TOKENS]).then_inc(x_stored, 16)
                sp.wait_ge(setup_loads, 16)
                sp.wait_ge(x_stored, 16)

            @block.gpsimd
            def _(pool):
                step = [0]

                def after(ins):
                    ins.then_inc(setup, 1)
                    step[0] += 1
                    pool.wait_ge(setup, step[0])

                after(pool.memset(mask[:, :, :], 0.0))
                after(pool.affine_select(out=mask[:, :, :], in_=mask[:, :, :], pattern=[[0, HG], [-1, P]], compare_op=ALU.is_ge,
                                         fill=MASKED, base=0, channel_multiplier=1))
                after(pool.affine_select(out=mask[:, :, :], in_=mask[:, :, :], pattern=[[0, HG], [1, P]], compare_op=ALU.is_ge,
                                         fill=MASKED, base=WINDOW, channel_multiplier=-1))
                after(pool.memset(mask_prev[:, :, :], 0.0))
                after(pool.affine_select(out=mask_prev[:, :, :], in_=mask_prev[:, :, :], pattern=[[0, LH], [1, WINDOW]],
                                         compare_op=ALU.is_ge, fill=MASKED, base=0, channel_multiplier=-1))

            @block.vector
            def _(dve):
                dve.memset(shown[:, :], 1.0)
                dve.memset(hidden[:, :], 0.0)
                dve.memset(norm_bias[:, :], float(0.5 * np.log(NORM_SCALE)))
                for i in range(2):
                    dve.memset(v[i][:, :, LD:LD + 1], 1.0)
                    dve.memset(v_prev[i][:, :, :, :], 0.0)
                    dve.memset(k_t[i][:, :, :], 0.0)
                dve.memset(pt_prev[:, :, :], 0.0)
                dve.memset(Xp[:, 0:1], 0.0)
                dve.memset(X1p[:, 0:1], 0.0)
                dve.tensor_copy(ident16[:, :], ident).then_inc(table_step, 1)
                dve.wait_ge(table_step, 1)
                for b in range(BATCH):
                    dve.memset(shown[:, b * TILES:b * TILES + 1], 0.0)
                    ins = dve.memset(hidden[:, b * TILES:b * TILES + 1], MASKED)
                ins.then_inc(table_step, 1)

        def cnt(t, per, k):
            return t * per + k

        layers = ExitStack()
        block = layers.enter_context(nc.Block())

        @block.sync
        def _(sp):
            with sp.Fori(0, DEPTH) as L:
                sp.wait_ge(f_done, L * CHUNKS)
                one = bass.ds(L, 1)
                sp.dma_start(w_qkv[:, :], d["d_wqkv"][one].rearrange("o p n -> p (o n)")).then_inc(qkv_loaded, 16)
                sp.dma_start(w_o[:, :, :], d["d_wo"][one].rearrange("o (k p) n -> p (o k) n", p=P)).then_inc(qkv_loaded, 16)
                sp.dma_start(qk_scale[:, :, :], d["d_scales"][one].rearrange("o p s n -> p (o s) n")).then_inc(qkv_loaded, 16)
                sp.dma_start(b_1[:, :], d["d_b1"][one].rearrange("o p n -> p (o n)")).then_inc(qkv_loaded, 16)
                sp.dma_start(vec[:, :], d["d_ln"][one].rearrange("o p n -> p (o n)")).then_inc(qkv_loaded, 16)
                sp.dma_start(w_1[:, :], d["d_w1"][one].rearrange("o p n -> p (o n)")).then_inc(ffn_loaded, 16)
                for n, (lo, size) in enumerate(FF_BLOCKS):
                    sp.dma_start(w_2[0:size, n, :], d["d_w2"][one, lo:lo + size].rearrange("o p n -> p (o n)")).then_inc(ffn_loaded, 16)

                def prev_values(t, par):
                    sp.wait_ge(v_kept, cnt(t - 1, 2, 2))
                    sp.wait_ge(out_mm, t * 3 - 3)
                    src = v[1 - par][P - WINDOW:P, :, :].rearrange("p (g j) c -> p g j c", j=HG)
                    for j in range(HG):
                        sp.dma_start(v_prev[par][j * WINDOW:j * WINDOW + WINDOW, :, j, :], src[:, :, j, :]).then_inc(vp_landed[par], 16)

                prev_values(L * STEPS + 1, 1)
                with sp.Fori(1, NT // 2) as g:
                    prev_values(L * STEPS + g * 2, 0)
                    prev_values(L * STEPS + g * 2 + 1, 1)

        @block.gpsimd
        def _(pool):
            def add(L, i, n):
                t = L * STEPS + i
                pool.wait_ge(rope_ready, cnt(t, 4, n + 1))
                pool.tensor_tensor(t1[:, n, :, :], t1[:, n, :, :], t2[:, n, :, :], ALU.add).then_inc(rope_sum, 1)

            with pool.Fori(0, DEPTH) as L:
                with pool.Fori(0, NT) as i:
                    for n in range(4):
                        add(L, i, n)

        def half(n):
            return t1[:, n, :, :].rearrange("p h c -> p (h c)")

        @block.tensor
        def _(pe):
            def project(t, par, n):
                if n == 0:
                    pe.wait_ge(x_ready, cnt(t, 2, 2))
                    pe.wait_ge(v_kept, t * 2)
                elif n >= 2:
                    pe.wait_ge(rope_ready, cnt(t, 4, n - 1))
                pe.matmul(p_b[n % 2][:, :], lhsT=xs[par][:, :], rhs=w_qkv[:, n * LANES:n * LANES + LANES], start=True,
                          stop=True).then_inc(proj, 1)

            def turn_qk(t, n, prior):
                pe.wait_ge(unit_ready, cnt(t, 4, n + 1))
                if n >= 2:
                    pe.wait_ge(qk_kept, cnt(t, 4, n - 1))
                elif prior:
                    pe.wait_ge(p_kept, cnt(t - 1, 5, 4 + n))
                for j in range(4):
                    ins = pe.transpose(t_b[n % 2][:, j * P:j * P + P], half(n)[:, j * P:j * P + P], ident)
                ins.then_inc(qk_turned, 1)

            def score(t, par, g, prior):
                if g >= 2:
                    pe.wait_ge(sub_ready, cnt(t, 5, g - 1))
                elif prior:
                    pe.wait_ge(out_norm, cnt(t, 3, -3 + g + 1))
                b = s_b[g % 2]
                for j in range(HG):
                    h = head_of(g, j)
                    lo = (h % 2) * LD
                    pe.matmul(b[:, j * P:j * P + P], lhsT=q_t[lo:lo + LD, h // 2, :], rhs=k_t[par][lo:lo + LD, h // 2, :],
                              start=j == 0, stop=False, skip_group_check=True)
                pe.matmul(b[:, :], lhsT=ident16[:, :], rhs=mask[:, :, :].rearrange("p h c -> p (h c)"), start=False,
                          stop=True, skip_group_check=True).then_inc(scores, 1)

            def add_prev(par, odd):
                lo = odd * LD
                for g in (odd, 2 + odd):
                    for j in range(HG):
                        c = (g * HG + j) * WINDOW
                        h = head_of(g, j)
                        ins = pe.matmul(s_b[2][0:WINDOW, c:c + WINDOW], lhsT=q_t[lo:lo + LD, h // 2, 0:WINDOW],
                                        rhs=k_t[1 - par][lo:lo + LD, h // 2, P - WINDOW:P], start=c == 0, stop=False,
                                        skip_group_check=True)
                return ins

            def first_scores(t, par, prior, masks):
                pe.wait_ge(qk_kept, cnt(t, 4, 4))
                if prior:
                    pe.wait_ge(out_norm, cnt(t, 3, 0))
                if par == 0:
                    pe.wait_ge(mask_ready, masks)
                score(t, par, 0, prior)
                add_prev(par, 0).then_inc(even_done, 1)
                pe.wait_ge(even_done, t + 1)
                score(t, par, 1, prior)
                add_prev(par, 1)
                m = mask_now if par == 0 else mask_prev
                pe.matmul(s_b[2][0:WINDOW, :], lhsT=ident16[0:WINDOW, 0:WINDOW], rhs=m[:, :, :].rearrange("p h c -> p (h c)"),
                          start=False, stop=True, skip_group_check=True).then_inc(scores, 1)

            def turn_probs(t, n, prior):
                if n == NG - 1:
                    pe.wait_ge(x1_ready, t)
                    pe.wait_ge(exp_ready, cnt(t, 5, 5))
                else:
                    pe.wait_ge(exp_ready, cnt(t, 5, n + 1))
                bk = t_b[(n + 1) % 2]
                if n >= 2:
                    pe.wait_ge(p_kept, cnt(t, 5, n - 1))
                elif prior:
                    pe.wait_ge(a_kept, cnt(t - 1, 2, n + 1))
                for j in range(HG):
                    ins = pe.transpose(bk[:, j * P:j * P + P], z[:, n, j, :], ident)
                ins.then_inc(p_turned, 1)
                if n == NG - 1:
                    zp = z_prev[:, :, :].rearrange("p (g j) c -> p g (j c)", j=HG)
                    for g in range(NG):
                        ins = pe.transpose(w_b[:, P + g * WINDOW:P + (g + 1) * WINDOW], zp[:, g, :], ident[0:WINDOW, 0:WINDOW])
                    ins.then_inc(p_turned, 1)

            def attend(t, par, n, landed):
                if n == 0:
                    pe.wait_ge(p_kept, cnt(t, 5, 5))
                    pe.wait_ge(v_kept, cnt(t, 2, 2))
                    pe.wait_ge(vp_landed[par], landed)
                lo, hi = OUT_BANKS[n]
                for p in range(lo, hi):
                    c = (p - lo) * (LD + 1)
                    pe.matmul(s_b[n][:, c:c + LD + 1], lhsT=pt[:, p // HG, p % HG, :], rhs=v[par][:, p, :], start=p == lo,
                              stop=False, skip_group_check=True)
                for g in range(lo // HG, (hi - 1) // HG + 1):
                    first, end = max(lo, g * HG), min(hi, g * HG + HG)
                    c = (first - lo) * (LD + 1)
                    cols = v_prev[par][:, g, first - g * HG:end - g * HG, :].rearrange("p j c -> p (j c)")
                    ins = pe.matmul(s_b[n][:, c:c + (end - first) * (LD + 1)], lhsT=pt_prev[:, g, :], rhs=cols, start=False,
                                    stop=True, skip_group_check=True)
                ins.then_inc(out_mm, 1)

            def turn_out(t, n, prior_kept):
                pe.wait_ge(out_norm, cnt(t, 3, 2 + n))
                pe.wait_ge(qk_kept, prior_kept)
                a = att[:, :, :].rearrange("p h c -> p (h c)")
                for j in range(4):
                    ins = pe.transpose(t_b[(n + 1) % 2][:, j * P:j * P + P], a[:, (4 * n + j) * P:(4 * n + j) * P + P], ident)
                ins.then_inc(a_turned, 1)

            def project_out(t):
                pe.wait_ge(a_kept, cnt(t, 2, 2))
                pe.wait_ge(x1_ready, t)
                for j in range(INNER // P):
                    ins = pe.matmul(w_b[:, 0:P], lhsT=w_o[:, j, :], rhs=att_t[:, j, :], start=j == 0, stop=j == INNER // P - 1)
                ins.then_inc(o_mm, 1)

            def step(L, i, par, has_c, has_a, landed_c, even):
                t = L * STEPS + i
                prior = has_c
                if has_c:
                    for n in range(3):
                        attend(t - 1, 1 - par, n, landed_c)
                if has_a:
                    project(t + 1, 1 - par, 0)
                    project(t + 1, 1 - par, 1)
                first_scores(t, par, prior, even)
                if has_c:
                    for n in range(2):
                        turn_out(t - 1, n, cnt(t, 4, 4))
                if has_a:
                    project(t + 1, 1 - par, 2)
                if has_c:
                    project_out(t - 1)
                if has_a:
                    project(t + 1, 1 - par, 3)
                score(t, par, 2, prior)
                if has_a:
                    project(t + 1, 1 - par, 4)
                score(t, par, 3, prior)
                if has_a:
                    project(t + 1, 1 - par, 5)
                for n in range(NG):
                    turn_probs(t, n, prior)
                if has_a:
                    for n in range(4):
                        turn_qk(t + 1, n, True)

            with pe.Fori(0, DEPTH) as L:
                pe.wait_ge(qkv_loaded, L * QKV_LOADS + QKV_LOADS)
                for n in range(6):
                    project(L * STEPS, 0, n)
                for n in range(4):
                    turn_qk(L * STEPS, n, False)

                even0 = L * (NT // 2) + 1
                step(L, 0, 0, False, True, None, even0)
                with pe.Fori(0, NT // 2 - 1) as g:
                    step(L, g * 2 + 1, 1, True, True, L * (64 * (NT // 2 - 1)) + g * 64, None)
                    step(L, g * 2 + 2, 0, True, True, L * (64 * (NT // 2)) + (g * 64 + 64), L * (NT // 2) + (g + 2))
                step(L, NT - 1, 1, True, False, L * (64 * (NT // 2 - 1)) + 64 * (NT // 2 - 1), None)
                t_last = L * STEPS + (NT - 1)
                for n in range(3):
                    attend(t_last, 1, n, L * (64 * (NT // 2)) + 64 * (NT // 2))
                for n in range(2):
                    turn_out(t_last, n, cnt(t_last, 4, 4))
                project_out(t_last)

                def norm(c, s):
                    n = L * CHUNKS + c
                    pe.wait_ge(f_x, n + 1)
                    pe.wait_ge(f_cent, n)
                    pe.matmul(p_b[s][:, :], lhsT=mean_w, rhs=fx[s], start=True, stop=True).then_inc(f_mean, 1)
                    pe.wait_ge(f_sq, n + 1)
                    pe.wait_ge(f_rstd, n * 2)
                    pe.matmul(t_b[s][:, :], lhsT=mean_w, rhs=fq[s], start=True, stop=True).then_inc(f_var, 1)

                with pe.Fori(0, CHUNKS // 2) as g:
                    norm(g * 2, 0)
                    norm(g * 2 + 1, 1)

                def feed(c, s):
                    n = L * CHUNKS + c
                    pe.wait_ge(ffn_loaded, L * FFN_LOADS + FFN_LOADS)
                    pe.wait_ge(f_norm, L * (CHUNKS * 2) + CHUNKS * 2)
                    x = X[:, bass.ds(c * CH, CH)]
                    for m, (lo, size) in enumerate(FF_BLOCKS):
                        pe.wait_ge(f_gelu, n * 3 + max(m - 1, 0))
                        pe.matmul(s_b[m % 2][0:size, :], lhsT=w_1[:, FFI + lo:FFI + lo + size], rhs=x, start=True,
                                  stop=True).then_inc(f_gate, 1)
                        pe.wait_ge(f_prod, n * 3 + max(m - 1, 0))
                        pe.matmul(p_b[m % 2][0:size, :], lhsT=w_1[:, lo:lo + size], rhs=x, start=True, stop=True).then_inc(f_lin, 1)
                    pe.wait_ge(f_done, n)
                    for m, (lo, size) in enumerate(FF_BLOCKS):
                        pe.wait_ge(f_prod, n * 3 + m + 1)
                        ins = pe.matmul(t_b[s][:, :], lhsT=w_2[0:size, m, :], rhs=hh[m][0:size, :], start=m == 0, stop=m == 2)
                    ins.then_inc(f_out, 1)

                with pe.Fori(0, CHUNKS // 2) as g:
                    feed(g * 2, 0)
                    feed(g * 2 + 1, 1)

        @block.scalar
        def _(act):
            def take(L, i, par, first=False):
                t = L * STEPS + i
                if first:
                    act.wait_ge(f_done, L * CHUNKS)
                act.wait_ge(proj, t * 6 if first else cnt(t, 6, -6))
                act.activation(xs[par][0:64, :], X[0:64, bass.ds(i * P, P)], ACT.Copy)
                act.activation(xs[par][64:P, :], Xp[64:P, bass.ds(i * P, P)], ACT.Copy).then_inc(x_ready, 1)
                act.wait_ge(x_ready, cnt(t, 2, 1))
                act.activation(xs[par][64:P, 0:1], xs[par][64:P, 0:1], ACT.Identity, scale=shown[64:P, bass.ds(i, 1)]).then_inc(x_ready, 1)

            def mask_for(L, i):
                t = L * STEPS + i
                act.wait_ge(scores, cnt(t, 5, 0))
                before = k_t[1][:, :, P - WINDOW:P]
                act.activation(before, before, ACT.Identity, scale=shown[:, bass.ds(i, 1)])
                act.activation(mask_now[:, :, :], mask_prev[:, :, :], ACT.Identity, bias=hidden[0:WINDOW, bass.ds(i, 1)]).then_inc(mask_ready, 1)

            def square(t, n):
                act.wait_ge(proj, cnt(t, 6, n + 1))
                act.wait_ge(ssq_step, cnt(t, 5, max(n - 1, 0)))
                act.activation(sq[:, n % 2, :, :].rearrange("p h c -> p (h c)"), p_b[n % 2][:, :], ACT.Square).then_inc(sq_ready, 1)

            def values(t, par, n, landed=None):
                if landed is not None:
                    act.wait_ge(vp_landed[1 - par], landed)
                act.wait_ge(proj, cnt(t, 6, n + 5))
                act.activation(v[par][:, 8 * n:8 * n + 8, 0:LD], p_b[n % 2][:, :].rearrange("p (h c) -> p h c", c=LD),
                               ACT.Copy).then_inc(v_kept, 1)

            def inverse_norms(t):
                act.wait_ge(ssq_step, cnt(t, 5, 5))
                act.activation(ssq_l[:, :], ssq_c[:, :], ACT.Ln, scale=NORM_SCALE).then_inc(inv_step, 1)
                act.wait_ge(inv_step, cnt(t, 2, 1))
                act.activation(inv_n[:, :], ssq_l[:, :], ACT.Exp, scale=-0.5, bias=norm_bias[:, 0:1]).then_inc(inv_step, 1)

            def keep_qk(t, par, n):
                act.wait_ge(qk_turned, cnt(t, 4, n + 1))
                dst = (q_t if n < 2 else k_t[par])[:, 4 * (n % 2):4 * (n % 2) + 4, :]
                act.activation(dst.rearrange("p j c -> p (j c)"), t_b[n % 2][:, :], ACT.Copy).then_inc(qk_kept, 1)

            def exps(t, n):
                act.wait_ge(sub_ready, cnt(t, 5, n + 1))
                e = z[:, n, :, :].rearrange("p h c -> p (h c)") if n < 4 else z_prev[:, :, :].rearrange("p h c -> p (h c)")
                act.activation(e, e, ACT.Exp, scale=QK_SCALE).then_inc(exp_ready, 1)

            def keep_probs(t, n):
                act.wait_ge(p_turned, cnt(t, 5, n + 1))
                if n < 4:
                    act.activation(pt[:, n, :, :].rearrange("p h c -> p (h c)"), t_b[(n + 1) % 2][:, :], ACT.Copy).then_inc(p_kept, 1)
                else:
                    act.activation(pt_prev[:, :, 0:WINDOW], w_b[:, P:2 * P].rearrange("p (g c) -> p g c", c=WINDOW),
                                   ACT.Copy).then_inc(p_kept, 1)

            def keep_out(t, n):
                act.wait_ge(a_turned, cnt(t, 2, n + 1))
                act.activation(att_t[:, 4 * n:4 * n + 4, :].rearrange("p j c -> p (j c)"), t_b[(n + 1) % 2][:, :], ACT.Copy).then_inc(a_kept, 1)

            def step(L, i, par, has_c, has_a, takes, landed):
                t = L * STEPS + i
                if has_a:
                    square(t + 1, 0)
                    square(t + 1, 1)
                exps(t, 0)
                if takes:
                    take(L, i + 2, par)
                if has_c:
                    for n in range(2):
                        keep_out(t - 1, n)
                if has_a:
                    square(t + 1, 2)
                exps(t, 1)
                if has_a:
                    square(t + 1, 3)
                exps(t, 2)
                if has_a:
                    values(t + 1, 1 - par, 0, landed)
                exps(t, 3)
                exps(t, 4)
                if has_a:
                    values(t + 1, 1 - par, 1)
                    inverse_norms(t + 1)
                for n in range(5):
                    keep_probs(t, n)
                if par == 1 and has_a:
                    mask_for(L, i + 1)
                if has_a:
                    for n in range(4):
                        keep_qk(t + 1, 1 - par, n)

            act.preload_act_table_set("natural_log_exp_and_others")
            with act.Fori(0, DEPTH) as L:
                act.preload_act_table_set("natural_log_exp_and_others")
                t = L * STEPS
                take(L, 0, 0, first=True)
                mask_for(L, 0)
                take(L, 1, 1)
                for n in range(4):
                    square(t, n)
                for n in range(2):
                    values(t, 0, n)
                inverse_norms(t)
                for n in range(4):
                    keep_qk(t, 0, n)
                odd, even = L * (64 * (NT // 2)), L * (64 * (NT // 2 - 1))
                step(L, 0, 0, False, True, True, None)
                with act.Fori(0, NT // 2 - 2) as g:
                    step(L, g * 2 + 1, 1, True, True, True, odd + (g * 64 + 64))
                    step(L, g * 2 + 2, 0, True, True, True, even + (g * 64 + 64))
                step(L, NT - 3, 1, True, True, True, odd + 64 * (NT // 2 - 1))
                step(L, NT - 2, 0, True, True, False, even + 64 * (NT // 2 - 1))
                step(L, NT - 1, 1, True, False, False, None)
                for n in range(2):
                    keep_out(L * STEPS + (NT - 1), n)
                act.wait_ge(x1_ready, L * STEPS + STEPS)

                def norm(c, s):
                    n = L * CHUNKS + c
                    act.activation(fx[s][0:64, :], X1[0:64, bass.ds(c * CH, CH)], ACT.Copy)
                    act.activation(fx[s][64:P, :], X1p[64:P, bass.ds(c * CH, CH)], ACT.Copy).then_inc(b_step, 1)
                    act.wait_ge(b_step, n + 1)
                    act.activation(fx[s][64:P, 0:1], fx[s][64:P, 0:1], ACT.Identity,
                                   scale=shown[64:P, bass.ds(c * 4, 1)]).then_inc(f_x, 1)
                    act.wait_ge(f_cent, n + 1)
                    act.activation(fq[s], fc[s], ACT.Square).then_inc(f_sq, 1)
                    act.wait_ge(f_var, n + 1)
                    act.activation(fl[s], t_b[s][:, :], ACT.Ln, bias=eps).then_inc(f_rstd, 1)
                    act.wait_ge(f_rstd, n * 2 + 1)
                    act.activation(fr[s], fl[s], ACT.Exp, scale=-0.5).then_inc(f_rstd, 1)

                with act.Fori(0, CHUNKS // 2) as g:
                    norm(g * 2, 0)
                    norm(g * 2 + 1, 1)

                def feed(c, s):
                    n = L * CHUNKS + c
                    for m, (lo, size) in enumerate(FF_BLOCKS):
                        act.wait_ge(f_gate, n * 3 + m + 1)
                        act.wait_ge(f_prod, n * 3 + max(m - 1, 0))
                        act.activation(gl[m % 2][0:size, :], s_b[m % 2][0:size, :], ACT.Gelu, bias=b_1[0:size, 3 + m:4 + m]).then_inc(f_gelu, 1)

                act.preload_act_table(ACT.Gelu)
                with act.Fori(0, CHUNKS // 2) as g:
                    feed(g * 2, 0)
                    feed(g * 2 + 1, 1)

        @block.vector
        def _(dve):
            def rope(t, i8, n):
                dve.wait_ge(sq_ready, cnt(t, 4, n + 1))
                x = p_b[n % 2][:, :].rearrange("p (h c) -> p h c", c=LD)
                which = 0 if n < 2 else 2
                cos = table[:, bass.ds(i8, 1), which, :].to_broadcast([P, 8, LD])
                sin = table[:, bass.ds(i8, 1), which + 1, :]
                dve.tensor_tensor(t1[:, n, :, :], x, cos, ALU.mult)
                H = LD // 2
                dve.tensor_tensor(t2[:, n, :, 0:H], x[:, :, H:LD], sin[:, :, 0:H].to_broadcast([P, 8, H]), ALU.mult)
                dve.tensor_tensor(t2[:, n, :, H:LD], x[:, :, 0:H], sin[:, :, H:LD].to_broadcast([P, 8, H]), ALU.mult).then_inc(rope_ready, 1)

            def square_sum(t, n):
                dve.tensor_reduce(ssq[:, 8 * n:8 * n + 8], sq[:, n % 2, :, :], AX.X, ALU.add).then_inc(ssq_step, 1)

            def guard(t):
                dve.wait_ge(ssq_step, cnt(t, 5, 4))
                dve.tensor_scalar(ssq_c[:, :], ssq[:, :], 1e-24, None, ALU.max).then_inc(ssq_step, 1)

            def unit(t, n):
                if n == 0:
                    dve.wait_ge(inv_step, cnt(t, 2, 2))
                dve.wait_ge(rope_sum, cnt(t, 4, n + 1))
                dve.tensor_tensor(t1[:, n, :, :], t1[:, n, :, :], inv_n[:, 8 * n:8 * n + 8].unsqueeze(2).to_broadcast([P, 8, LD]),
                                  ALU.mult).then_inc(unit_ready, 1)

            def max_prev(t):
                dve.wait_ge(scores, cnt(t, 5, 3))
                dve.tensor_reduce(top_prev[:, :], s_b[2][0:WINDOW, :].rearrange("p (h c) -> p h c", c=WINDOW), AX.X,
                                  ALU.max).then_inc(max_step, 1)

            def less_max(t, g):
                dve.wait_ge(scores, cnt(t, 5, g + 2 if g >= 2 else g + 1))
                s = s_b[g % 2][:, :].rearrange("p (h c) -> p h c", c=P)
                hs = slice(g * HG, g * HG + HG)
                dve.tensor_reduce(top[:, hs], s, AX.X, ALU.max).then_inc(max_step, 1)
                dve.wait_ge(max_step, cnt(t, 9, 2 + 2 * g))
                dve.tensor_tensor(top[0:WINDOW, hs], top[0:WINDOW, hs], top_prev[:, hs], ALU.max).then_inc(max_step, 1)
                dve.wait_ge(max_step, cnt(t, 9, 3 + 2 * g))
                dve.tensor_tensor(z[:, g, :, :], s, top[:, hs].unsqueeze(2).to_broadcast([P, HG, P]), ALU.subtract).then_inc(sub_ready, 1)

            def less_max_prev(t):
                s = s_b[2][0:WINDOW, :].rearrange("p (h c) -> p h c", c=WINDOW)
                dve.tensor_tensor(z_prev[:, :, :], s, top[0:WINDOW, :].unsqueeze(2).to_broadcast([WINDOW, LH, WINDOW]),
                                  ALU.subtract).then_inc(sub_ready, 1)

            def normalise(t, n):
                dve.wait_ge(out_mm, cnt(t, 3, n + 1))
                lo, hi = OUT_BANKS[n]
                o = s_b[n][:, 0:(hi - lo) * (LD + 1)].rearrange("p (h c) -> p h c", c=LD + 1)
                dve.reciprocal(inv_s[:, lo:hi], o[:, :, LD]).then_inc(out_inv, 1)
                dve.wait_ge(out_inv, cnt(t, 3, n + 1))
                dve.tensor_tensor(att[:, lo:hi, :], o[:, :, 0:LD], inv_s[:, lo:hi].unsqueeze(2).to_broadcast([P, hi - lo, LD]),
                                  ALU.mult).then_inc(out_norm, 1)

            def add_x(L, i):
                t = L * STEPS + i
                dve.wait_ge(o_mm, t + 1)
                dve.tensor_tensor(X1[:, bass.ds(i * P, P)], X[:, bass.ds(i * P, P)], w_b[:, 0:P], ALU.add).then_inc(x1_ready, 1)

            def step(L, i, has_c, has_a):
                t = L * STEPS + i
                i8 = (i + 1) % TILES
                if has_c:
                    for n in range(3):
                        normalise(t - 1, n)
                if has_a:
                    for n in range(2):
                        rope(t + 1, i8, n)
                        square_sum(t + 1, n)
                max_prev(t)
                less_max(t, 0)
                if has_a:
                    rope(t + 1, i8, 2)
                    square_sum(t + 1, 2)
                less_max(t, 1)
                if has_c:
                    add_x(L, i - 1)
                if has_a:
                    rope(t + 1, i8, 3)
                    square_sum(t + 1, 3)
                less_max(t, 2)
                if has_a:
                    guard(t + 1)
                less_max(t, 3)
                less_max_prev(t)
                if has_a:
                    for n in range(4):
                        unit(t + 1, n)

            with dve.Fori(0, DEPTH) as L:
                dve.wait_ge(qkv_loaded, L * QKV_LOADS + QKV_LOADS)
                dve.wait_ge(f_done, L * CHUNKS)
                for k in range(4):
                    ins = dve.tensor_tensor(table[:, :, k, :], base[:, :, k, :], qk_scale[:, k, :].unsqueeze(1).to_broadcast([P, TILES, LD]),
                                            ALU.mult)
                ins.then_inc(table_step, 1)
                dve.wait_ge(table_step, L + 3)
                t = L * STEPS
                for n in range(4):
                    rope(t, 0, n)
                    square_sum(t, n)
                guard(t)
                for n in range(4):
                    unit(t, n)
                step(L, 0, False, True)
                with dve.Fori(0, NT // 2 - 1) as g:
                    step(L, g * 2 + 1, True, True)
                    step(L, g * 2 + 2, True, True)
                step(L, NT - 1, True, False)
                for n in range(3):
                    normalise(L * STEPS + (NT - 1), n)
                add_x(L, NT - 1)

                def norm(c, s):
                    n = L * CHUNKS + c
                    dve.wait_ge(f_mean, n + 1)
                    dve.tensor_tensor(fc[s], fx[s], p_b[s][:, :], ALU.subtract).then_inc(f_cent, 1)
                    dve.wait_ge(f_rstd, n * 2 + 2)
                    dve.tensor_tensor(fn[s], fc[s], fr[s], ALU.mult).then_inc(f_norm, 1)
                    dve.wait_ge(f_norm, n * 2 + 1)
                    dve.tensor_scalar(X[:, bass.ds(c * CH, CH)], fn[s], vec[:, 0:1], vec[:, 1:2], ALU.mult, ALU.add).then_inc(f_norm, 1)

                with dve.Fori(0, CHUNKS // 2) as g:
                    norm(g * 2, 0)
                    norm(g * 2 + 1, 1)

                def feed(c, s):
                    n = L * CHUNKS + c
                    for m, (lo, size) in enumerate(FF_BLOCKS):
                        dve.wait_ge(f_lin, n * 3 + m + 1)
                        dve.wait_ge(f_gelu, n * 3 + m + 1)
                        if m == 0:
                            dve.wait_ge(f_out, n)
                        dve.scalar_tensor_tensor(hh[m][0:size, :], p_b[m % 2][0:size, :], b_1[0:size, m:m + 1], gl[m % 2][0:size, :],
                                                 ALU.add, ALU.mult).then_inc(f_prod, 1)
                    dve.wait_ge(f_out, n + 1)
                    dve.scalar_tensor_tensor(X[:, bass.ds(c * CH, CH)], t_b[s][:, :], vec[:, 2:3], X1[:, bass.ds(c * CH, CH)], ALU.add,
                                             ALU.add).then_inc(f_done, 1)

                with dve.Fori(0, CHUNKS // 2) as g:
                    feed(g * 2, 0)
                    feed(g * 2 + 1, 1)

        layers.close()

        landed = [sem(f"d_x_landed{i}") for i in range(2)]
        e_sum = sem("d_end_sum_ready")
        e_ln = Norm(sem, "d_end_ln")
        e_done = sem("d_end_done")
        with nc.Block() as block:
            @block.sync
            def _(sp):
                for c in range(CHUNKS):
                    if c >= 2:
                        sp.wait_ge(e_sum, c - 1)
                    sp.dma_start(fx[c % 2], kept_x[:, c * CH:c * CH + CH]).then_inc(landed[c % 2], 16)

            @block.tensor
            def _(pe):
                for c in range(CHUNKS):
                    pe.wait_ge(e_sum, c + 1)
                    norm_pe(pe, e_ln, c, mean_w, X[:, c * CH:c * CH + CH], fq[0], p_b[0][:, :], p_b[1][:, :])

            @block.scalar
            def _(act):
                for c in range(CHUNKS):
                    norm_act(act, e_ln, c, fc[0], fq[0], p_b[1][:, :], fl[0], eps)

            @block.vector
            def _(dve):
                for c in range(CHUNKS):
                    x = X[:, c * CH:c * CH + CH]
                    dve.wait_ge(landed[c % 2], 16 * (c // 2) + 16)
                    dve.tensor_tensor(x, x, fx[c % 2], ALU.add).then_inc(e_sum, 1)
                    dve.wait_ge(e_sum, c + 1)
                    norm_dve(dve, e_ln, c, x, fc[0], fl[0], fr[0], p_b[0][:, :])
                    dve.tensor_tensor(x, fc[0], fr[0], ALU.mult).then_inc(e_done, 1)


def build(nc, d, out):
    with ExitStack() as ctx:
        def sem(label):
            return ctx.enter_context(nc.semaphore(label))

        Xp = ctx.enter_context(nc.sbuf_tensor("X", [P, 1 + TOKENS], F32))
        X1p = ctx.enter_context(nc.sbuf_tensor("X1", [P, 1 + TOKENS], F32))
        X, X1 = Xp[:, 1:], X1p[:, 1:]
        ident = ctx.enter_context(nc.sbuf_tensor("ident", [P, P], F32))
        mean_w = ctx.enter_context(nc.sbuf_tensor("mean_weights", [P, P], F32))
        eps = ctx.enter_context(nc.sbuf_tensor("eps", [P, 1], F32))
        const_step = sem("const_step")
        with nc.Block() as block:
            @block.gpsimd
            def _(pool):
                pool.memset(mean_w[:, :], 1.0 / DIM)
                pool.memset(eps[:, :], EPS)
                pool.memset(ident[:, :], 0.0).then_inc(const_step, 1)
                pool.wait_ge(const_step, 1)
                pool.affine_select(out=ident[:, :], in_=ident[:, :], pattern=[[-1, P]], compare_op=ALU.not_equal, fill=1.0,
                                   base=0, channel_multiplier=1)
        consts = (ident[:, :], mean_w[:, :], eps[:, 0:1])
        def stage_sem(label):
            return nc.alloc_semaphore(name=label)

        with nc.cleanup_on_exit():
            load_tokens(nc, stage_sem, d["x"], X, ident[:, :])
        with nc.cleanup_on_exit():
            mamba(nc, stage_sem, "a", X, X1, dict(in_proj=d["a_in_proj"], conv=d["a_conv"], x_proj=d["a_x_proj"], dt=d["a_dt"],
                                                  out_proj=d["a_out_proj"], vectors=d["a_vectors"]), consts)
        with nc.cleanup_on_exit():
            experts(nc, stage_sem, X, d, consts)
        with nc.cleanup_on_exit():
            mqa(nc, stage_sem, X, X1, d, consts)
        with nc.cleanup_on_exit():
            mamba(nc, stage_sem, "c", X, X1, dict(in_proj=d["c_w_in"], taps=d["c_conv_w"], x_proj=d["c_w_xproj"], dt=d["c_w_dt"],
                                                  out_proj=d["c_w_out"], vectors=d["c_vectors"], a_log=d["c_a_log"]), consts)
        with nc.cleanup_on_exit():
            local_layers(nc, stage_sem, Xp, X1p, d, consts)
    with nc.cleanup_on_exit():
        store_tokens(nc, stage_sem, out, X, ident[:, :])


def layout(i):
    def t(a):
        return np.ascontiguousarray(np.transpose(a))

    def cols(*vs):
        parts = [v.reshape(-1, P).T for v in vs]
        n = sum(p.shape[1] for p in parts)
        parts.append(np.zeros((P, 8 - n), np.float32))
        return np.ascontiguousarray(np.concatenate(parts, axis=1))

    swap = np.concatenate([np.arange(LD // 2, LD), np.arange(LD // 2)])
    q, k = i["L1_ffn_q_scale"], i["L1_ffn_k_scale"]
    scales = np.broadcast_to(np.stack([q, q[:, swap], k, k[:, swap]], axis=1)[:, None], (DEPTH, P, 4, LD))
    b1 = np.zeros((DEPTH, P, 6), np.float32)
    for m, (lo, size) in enumerate(FF_BLOCKS):
        b1[:, :size, m] = i["L1_ffn_b1"][:, lo:lo + size]
        b1[:, :size, 3 + m] = i["L1_ffn_b1"][:, FFI + lo:FFI + lo + size]
    wqkv = i["L1_ffn_Wqkv"].reshape(DEPTH, DIM, 3, LH, LD).copy()
    wqkv[:, :, 2] = wqkv[:, :, 2][:, :, PLACES]
    wo = i["L1_ffn_Wo"].reshape(DEPTH, LH, LD, DIM)[:, PLACES].reshape(DEPTH, INNER, DIM)
    return {
        "x": i["L0_attn_x"],
        "a_in_proj": t(i["L0_attn_in_proj_w"]),
        "a_conv": np.ascontiguousarray(np.transpose(i["L0_attn_conv_w"], (2, 1, 0))),
        "a_x_proj": t(i["L0_attn_x_proj_w"]),
        "a_dt": t(i["L0_attn_dt_w"]),
        "a_out_proj": t(i["L0_attn_out_proj_w"]),
        "a_vectors": cols(i["L0_attn_conv_b"], i["L0_attn_dt_b"], i["L0_attn_norm_w"], i["L0_attn_norm_b"]),
        "b_gate": np.ascontiguousarray(np.concatenate([i["L0_ffn_Wg"], i["L0_ffn_Wt"]], axis=1)),
        "b_gate_bias": np.ascontiguousarray(np.broadcast_to(np.concatenate([i["L0_ffn_bg"], i["L0_ffn_bt"]]), (P, 9))),
        "b_w1": i["L0_ffn_W1"],
        "b_b1": np.ascontiguousarray(i["L0_ffn_b1"].reshape(8, 4, P).transpose(2, 0, 1).reshape(P, 32)),
        "b_w2": i["L0_ffn_W2"],
        "b_b2": i["L0_ffn_b2"],
        "q_wqkv": i["L1_attn_wqkv"],
        "q_bias": np.ascontiguousarray(i["L1_attn_bqkv"].reshape(-1, 1)),
        "q_value_bias": np.ascontiguousarray(np.broadcast_to(i["L1_attn_bqkv"][DIM + HD:], (P, HD))),
        "q_key_pick": np.ascontiguousarray(np.repeat(np.array([[k == p for p in range(3)] for k in K_PART], np.float32), HD, axis=0)),
        "q_w_out": i["L1_attn_w_attn_out"],
        "q_b_out": np.ascontiguousarray(i["L1_attn_b_attn_out"].reshape(-1, 1)),
        "c_w_in": i["L1_attn_w_in"],
        "c_conv_w": i["L1_attn_conv_w"],
        "c_w_xproj": i["L1_attn_w_xproj"],
        "c_w_dt": i["L1_attn_w_dt"],
        "c_w_out": i["L1_attn_w_out"],
        "c_a_log": i["L1_attn_A_log"],
        "c_vectors": cols(i["L1_attn_conv_b"], i["L1_attn_b_dt"], np.zeros(2 * P, np.float32), i["L1_attn_Dp"]),
        "d_wqkv": wqkv.reshape(DEPTH, DIM, 3 * INNER),
        "d_wo": wo,
        "d_w1": i["L1_ffn_W1"],
        "d_w2": i["L1_ffn_W2"],
        "d_scales": scales,
        "d_b1": b1,
        "d_ln": np.ascontiguousarray(np.stack([i["L1_ffn_ln_g"], i["L1_ffn_ln_b"], i["L1_ffn_b2"]], axis=2)),
    }


def kernel(**inputs):
    import numpy as _np
    import concourse.bacc as _bacc
    from concourse import mybir as _mybir
    from concourse.bass_utils import run_bass_kernel_spmd as _run

    nc = _bacc.Bacc("TRN2", target_bir_lowering=False, num_devices=1)
    arrays, aps = {}, {}
    for name, a in layout({k: _np.asarray(v) for k, v in inputs.items()}).items():
        a = _np.ascontiguousarray(a)
        arrays[f"in_{name}"] = a
        aps[name] = nc.dram_tensor(f"in_{name}", a.shape, _mybir.dt.from_np(a.dtype), kind="ExternalInput").ap()
    out = nc.dram_tensor("out_0", (BATCH, SEQ, DIM), F32, kind="ExternalOutput").ap()
    build(nc, aps, out)
    r = _run(nc, [arrays], core_ids=[0])
    return r.results[0]["out_0"]
```

```python
from contextlib import ExitStack

import concourse.bass as bass
import numpy as np
from concourse import mybir

F32 = mybir.dt.float32
BF16 = mybir.dt.bfloat16
ALU = mybir.AluOpType
ACT = mybir.ActivationFunctionType
AX = mybir.AxisListType

P = 128
DIM = 128
BATCH = 4
SEQ = 1024
TOKENS = BATCH * SEQ
CH = 512
HALVES = SEQ // CH
NT = TOKENS // P
D_INNER = 256
DB = D_INNER // P
STATES = 16
TAPS = 4
EPS = 1e-5
LOG1P_DEGREE = 10


def log1p_coefficients():
    fit = np.polynomial.chebyshev.Chebyshev.interpolate(lambda x: np.log1p(x + 1e-12) / (x + 1e-12), LOG1P_DEGREE, domain=[0, 1])
    return [float(c) for c in fit.convert(kind=np.polynomial.Polynomial).coef]


class Norm:

    def __init__(self, sem, name):
        self.mean = sem(f"{name}_mean_ready")
        self.cent = sem(f"{name}_centred_ready")
        self.sq = sem(f"{name}_squares_ready")
        self.var = sem(f"{name}_variance_ready")
        self.std = sem(f"{name}_std_ready")
        self.rstd = sem(f"{name}_rstd_ready")


def norm_pe(pe, ln, n, mean_w, x, cent_sq, mean_bank, var_bank):
    pe.matmul(mean_bank, lhsT=mean_w, rhs=x, start=True, stop=True).then_inc(ln.mean, 1)
    pe.wait_ge(ln.sq, n + 1)
    pe.matmul(var_bank, lhsT=mean_w, rhs=cent_sq, start=True, stop=True).then_inc(ln.var, 1)


def norm_act(act, ln, n, cent, cent_sq, var_bank, std, eps):
    act.wait_ge(ln.cent, n + 1)
    act.activation(cent_sq, cent, ACT.Square).then_inc(ln.sq, 1)
    act.wait_ge(ln.var, n + 1)
    act.activation(std, var_bank, ACT.Sqrt, bias=eps).then_inc(ln.std, 1)


def norm_dve(dve, ln, n, x, cent, std, rstd, mean_bank):
    dve.wait_ge(ln.mean, n + 1)
    dve.tensor_tensor(cent, x, mean_bank, ALU.subtract).then_inc(ln.cent, 1)
    dve.wait_ge(ln.std, n + 1)
    dve.reciprocal(rstd, std).then_inc(ln.rstd, 1)
    dve.wait_ge(ln.rstd, n + 1)


def load_tokens(nc, sem, x_dram, X, ident):
    with ExitStack() as mem:
        raw = mem.enter_context(nc.sbuf_tensor("raw_tokens", [P, NT, DIM], F32))
        bank = [mem.enter_context(nc.psum_tensor(f"load_bank{i}", [P, CH], F32)) for i in range(2)]
        landed = [sem(f"tokens_landed{b}") for b in range(BATCH)]
        turned = sem("tokens_turned")
        kept = sem("tokens_kept")
        per = CH // P
        block = mem.enter_context(nc.Block())

        @block.sync
        def _(sp):
            for b in range(BATCH):
                sp.dma_start(raw[:, b * 8:b * 8 + 8, :], x_dram[b].rearrange("(t p) d -> p t d", p=P)).then_inc(landed[b], 16)

        @block.tensor
        def _(pe):
            for g in range(NT // per):
                if g % 2 == 0:
                    pe.wait_ge(landed[g // 2], 16)
                if g >= 2:
                    pe.wait_ge(kept, g - 1)
                for j in range(per):
                    ins = pe.transpose(bank[g % 2][:, j * P:j * P + P], raw[:, g * per + j, :], ident)
                ins.then_inc(turned, 1)

        @block.scalar
        def _(act):
            for g in range(NT // per):
                act.wait_ge(turned, g + 1)
                act.activation(X[:, g * CH:g * CH + CH], bank[g % 2][:, :], ACT.Copy).then_inc(kept, 1)


def store_tokens(nc, sem, out_dram, X, ident):
    with ExitStack() as mem:
        raw = mem.enter_context(nc.sbuf_tensor("out_tokens", [P, NT, DIM], F32))
        bank = [mem.enter_context(nc.psum_tensor(f"store_bank{i}", [P, CH], F32)) for i in range(2)]
        turned = sem("out_turned")
        kept = sem("out_kept")
        stored = sem("out_stored")
        per = CH // P
        block = mem.enter_context(nc.Block())

        @block.tensor
        def _(pe):
            for g in range(NT // per):
                if g >= 2:
                    pe.wait_ge(kept, g - 1)
                for j in range(per):
                    t = g * per + j
                    ins = pe.transpose(bank[g % 2][:, j * P:j * P + P], X[:, t * P:t * P + P], ident)
                ins.then_inc(turned, 1)

        @block.scalar
        def _(act):
            for g in range(NT // per):
                act.wait_ge(turned, g + 1)
                act.activation(raw[:, g * per:g * per + per, :], bank[g % 2][:, :].rearrange("p (t d) -> p t d", t=per),
                               ACT.Copy).then_inc(kept, 1)

        @block.sync
        def _(sp):
            for b in range(BATCH):
                sp.wait_ge(kept, 2 * b + 2)
                sp.dma_start(out_dram[b].rearrange("(t p) d -> p t d", p=P), raw[:, b * 8:b * 8 + 8, :]).then_inc(stored, 16)
            sp.wait_ge(stored, 16 * BATCH)


def mamba(nc, sem, name, X, X1, w, consts):
    first = name == "a"
    ident, mean_w, eps = consts
    low = 1 if first else 8
    rows = low + 2 * STATES
    with ExitStack() as mem:
        def sb(label, shape, dt=F32):
            return mem.enter_context(nc.sbuf_tensor(f"{name}_{label}", shape, dt))

        def bank(label):
            return mem.enter_context(nc.psum_tensor(f"{name}_{label}", [P, CH], F32))

        w_in = sb("w_in", [P, 2 * D_INNER])
        w_conv = sb("w_conv", [P, TAPS, DB, D_INNER]) if first else None
        taps = None if first else sb("taps", [P, DB, TAPS])
        diag = None if first else sb("diag", [P, DB, TAPS, P])
        w_x = sb("w_x", [P, DB, rows])
        w_dt = sb("w_dt", [low, D_INNER])
        w_out = sb("w_out", [P, DB, DIM])
        vec = sb("vectors", [P, 8])
        neg_dt = sb("neg_dt_bias", [P, DB])
        a_log = None if first else sb("a_log", [P, DB, STATES])
        a_neg = None if first else sb("a_neg", [P, DB, STATES])
        select = sb("select", [rows, 2 * STATES, P])
        xs = sb("x", [P, CH])
        cent = sb("cent", [P, CH])
        cent_sq = sb("cent_sq", [P, CH])
        std = sb("std", [P, CH])
        rstd = sb("rstd", [P, CH])
        xn = sb("xn", [P, CH])
        xn2 = sb("xn2", [P, CH])
        x_in = sb("x_in", [P, DB, TAPS - 1 + SEQ])
        gate = sb("gate", [P, DB, CH])
        u = sb("u", [P, DB, CH])
        du = u if first else sb("du", [P, DB, CH])
        dec = sb("decay_or_delta", [P, DB, CH])
        soft = None if first else sb("soft", [P, DB, 3, CH])
        ssm = sb("ssm", [rows, CH])
        c_sb = sb("c_rows", [P, 2, CH])
        bu = sb("b_times_u", [P, 2, DB, CH])
        h = sb("state", [P, 2, DB, CH])
        hc = sb("state_times_c", [P, 2, DB, CH])
        a_ring = None if first else sb("decays", [P, 2, DB, CH])
        carry = sb("carry", [P, STATES, DB])
        g = sb("gated", [P, DB, CH])
        yd = None if first else sb("y_plus_skip", [P, DB, CH])
        r = sb("residual", [P, CH])
        r2 = sb("residual2", [P, CH])
        b_bank = [bank(f"b_bank{i}") for i in range(2)]
        c_bank = [bank(f"c_bank{i}") for i in range(2)]
        y_bank = [bank(f"y_bank{i}") for i in range(DB)]
        p_bank = [bank(f"p_bank{i}") for i in range(2)]

        loaded = sem(f"{name}_weights_loaded")
        setup = sem(f"{name}_setup_done")
        select_ones = sem(f"{name}_select_ones")
        ln1 = Norm(sem, f"{name}_ln1") if first else None
        ln2 = Norm(sem, f"{name}_ln2")
        x_ready = sem(f"{name}_x_ready")
        scaled = sem(f"{name}_norm_scaled")
        xn_ready = sem(f"{name}_xn_ready")
        pre_mm = sem(f"{name}_projection_ready")
        pre_ev = sem(f"{name}_projection_kept")
        soft_step = sem(f"{name}_softplus_step")
        poly_step = sem(f"{name}_log1p_step")
        log1p = log1p_coefficients()
        delta_ready = sem(f"{name}_delta_ready")
        b_ready = sem(f"{name}_b_ready")
        c_ready = sem(f"{name}_c_ready")
        c_kept = sem(f"{name}_c_kept")
        a_ready = sem(f"{name}_decay_ready")
        bu_ready = sem(f"{name}_bu_ready")
        h_ready = sem(f"{name}_state_ready")
        carried = sem(f"{name}_state_carried")
        hc_ready = sem(f"{name}_hc_ready")
        summed = sem(f"{name}_hc_summed")
        skip_ready = sem(f"{name}_skip_added")
        g_ready = sem(f"{name}_gated_ready")
        out_ready = sem(f"{name}_out_ready")
        res_ready = sem(f"{name}_residual_ready")
        done = sem(f"{name}_chunk_done")
        LOADS = 16 * (9 if first else 7)
        SETUP = 3 if first else 12
        PRE = 9
        block = mem.enter_context(nc.Block())

        def at(b, half, per, k):
            return b * (HALVES * per) + (half * per + k)

        def cols(b, half):
            return bass.ds(b * SEQ + half * CH, CH)

        @block.sync
        def _(sp):
            sp.dma_start(w_in[:, :], w["in_proj"]).then_inc(loaded, 16)
            if first:
                for k in range(TAPS):
                    sp.dma_start(w_conv[:, k, :, :], w["conv"][k].rearrange("(e p) o -> p e o", p=P)).then_inc(loaded, 16)
            else:
                sp.dma_start(taps[:, :, :], w["taps"].rearrange("(d p) k -> p d k", p=P)).then_inc(loaded, 16)
                sp.dma_start(a_log[:, :, :], w["a_log"].rearrange("(d p) n -> p d n", p=P)).then_inc(loaded, 16)
            sp.dma_start(w_x[:, :, :], w["x_proj"].rearrange("(e p) r -> p e r", p=P)).then_inc(loaded, 16)
            sp.dma_start(w_dt[:, :], w["dt"]).then_inc(loaded, 16)
            sp.dma_start(w_out[:, :, :], w["out_proj"].rearrange("(e p) o -> p e o", p=P)).then_inc(loaded, 16)
            sp.dma_start(vec[:, :], w["vectors"]).then_inc(loaded, 16)

        @block.tensor
        def _(pe):
            pe.wait_ge(loaded, LOADS)
            pe.wait_ge(setup, SETUP)
            with pe.Fori(0, BATCH) as b:
                for half in range(HALVES):
                    t0 = half * CH
                    pe.wait_ge(x_ready, at(b, half, 1, 1))
                    if first:
                        norm_pe(pe, ln1, at(b, half, 1, 0), mean_w, xs[:, :], cent_sq[:, :], p_bank[0][:, :], p_bank[1][:, :])
                        pe.wait_ge(xn_ready, at(b, half, 1, 1))
                    x_op = xn2 if first else xs
                    for m in range(4):
                        if m >= 2:
                            pe.wait_ge(pre_ev, at(b, half, PRE, m - 1))
                        pe.matmul(p_bank[m % 2][:, :], lhsT=w_in[:, m * P:m * P + P], rhs=x_op[:, :], start=True,
                                  stop=True).then_inc(pre_mm, 1)
                    for d in range(DB):
                        pe.wait_ge(pre_ev, at(b, half, PRE, 3 + d))
                        if first:
                            n_mm = TAPS * DB
                            for i in range(n_mm):
                                k, e = i // DB, i % DB
                                ins = pe.matmul(p_bank[d][:, :], lhsT=w_conv[:, k, e, d * P:d * P + P],
                                                rhs=x_in[:, e, t0 + k:t0 + k + CH], start=i == 0, stop=i == n_mm - 1)
                        else:
                            for k in range(TAPS):
                                ins = pe.matmul(p_bank[d][:, :], lhsT=diag[:, d, k, :], rhs=x_in[:, d, t0 + k:t0 + k + CH],
                                                start=k == 0, stop=k == TAPS - 1)
                        ins.then_inc(pre_mm, 1)
                    pe.wait_ge(pre_ev, at(b, half, PRE, 6))
                    for e in range(DB):
                        ins = pe.matmul(p_bank[0][0:rows, :], lhsT=w_x[:, e, :], rhs=u[:, e, :], start=e == 0, stop=e == DB - 1)
                    ins.then_inc(pre_mm, 1)
                    pe.wait_ge(pre_ev, at(b, half, PRE, 7))
                    for d in range(DB):
                        pe.matmul(p_bank[1 - d][:, :], lhsT=w_dt[:, d * P:d * P + P], rhs=ssm[0:low, :], start=True,
                                  stop=True).then_inc(pre_mm, 1)

                    def spread(s):
                        if s >= 2:
                            pe.wait_ge(bu_ready, at(b, half, 2 * STATES, 2 * (s - 1)))
                        pe.matmul(b_bank[s % 2][:, :], lhsT=select[:, s, :], rhs=ssm[:, :], start=True, stop=True).then_inc(b_ready, 1)
                        if s >= 2:
                            pe.wait_ge(c_kept, at(b, half, STATES, s - 1))
                        pe.matmul(c_bank[s % 2][:, :], lhsT=select[:, STATES + s, :], rhs=ssm[:, :], start=True,
                                  stop=True).then_inc(c_ready, 1)

                    spread(0)
                    spread(1)
                    for s in range(STATES):
                        for d in range(DB):
                            pe.wait_ge(hc_ready, at(b, half, 2 * STATES, 2 * s + d + 1))
                            pe.matmul(y_bank[d][:, :], lhsT=ident, rhs=hc[:, s % 2, d, :], start=s == 0,
                                      stop=s == STATES - 1).then_inc(summed, 1)
                        if s + 2 < STATES:
                            spread(s + 2)
                    for d in range(DB):
                        pe.wait_ge(g_ready, at(b, half, DB, d + 1))
                        ins = pe.matmul(p_bank[0][:, :], lhsT=w_out[:, d, :], rhs=g[:, d, :], start=d == 0, stop=d == DB - 1)
                    ins.then_inc(out_ready, 1)
                    pe.wait_ge(res_ready, at(b, half, 2, 2))
                    norm_pe(pe, ln2, at(b, half, 1, 0), mean_w, r2[:, :], cent_sq[:, :], p_bank[0][:, :], p_bank[1][:, :])

        @block.scalar
        def _(act):
            if not first:
                act.wait_ge(loaded, LOADS)
                act.activation(a_neg[:, :, :], a_log[:, :, :], ACT.Exp).then_inc(setup, 1)
            act.wait_ge(setup, SETUP)
            with act.Fori(0, BATCH) as b:
                for half in range(HALVES):
                    t0 = TAPS - 1 + half * CH
                    act.wait_ge(done, at(b, half, 1, 0))
                    act.activation(xs[:, :], (X if first else X1)[:, cols(b, half)], ACT.Copy).then_inc(x_ready, 1)
                    if first:
                        norm_act(act, ln1, at(b, half, 1, 0), cent[:, :], cent_sq[:, :], p_bank[1][:, :], std[:, :], eps)
                    for m in range(2):
                        act.wait_ge(pre_mm, at(b, half, PRE, m + 1))
                        act.activation(x_in[:, m, t0:t0 + CH], p_bank[m][:, :], ACT.Copy).then_inc(pre_ev, 1)
                    for m in range(2):
                        act.wait_ge(pre_mm, at(b, half, PRE, m + 3))
                        act.activation(gate[:, m, :], p_bank[m][:, :], ACT.Silu).then_inc(pre_ev, 1)
                    for d in range(DB):
                        act.wait_ge(pre_mm, at(b, half, PRE, 5 + d))
                        act.activation(u[:, d, :], p_bank[d][:, :], ACT.Silu, bias=vec[:, d:d + 1]).then_inc(pre_ev, 1)
                    act.wait_ge(pre_mm, at(b, half, PRE, 7))
                    act.activation(ssm[:, :], p_bank[0][0:rows, :], ACT.Copy).then_inc(pre_ev, 1)
                    for d in range(DB):
                        act.wait_ge(pre_mm, at(b, half, PRE, 8 + d))
                        if first:
                            act.activation(dec[:, d, :], p_bank[1 - d][:, :], ACT.Sigmoid, bias=neg_dt[:, d:d + 1],
                                           scale=-1.0).then_inc(pre_ev, 1)
                        else:
                            act.activation(soft[:, d, 0, :], p_bank[1 - d][:, :], ACT.Identity, bias=vec[:, 2 + d:3 + d]).then_inc(pre_ev, 1)
                    if not first:
                        act.wait_ge(pre_ev, at(b, half, PRE, 9))
                        act.activation(soft[:, :, 1, :], soft[:, :, 0, :], ACT.Abs).then_inc(soft_step, 1)
                        act.wait_ge(soft_step, at(b, half, 2, 1))
                        act.activation(soft[:, :, 2, :], soft[:, :, 1, :], ACT.Exp, scale=-1.0).then_inc(soft_step, 1)
                        act.wait_ge(delta_ready, at(b, half, 2, 1))

                    def decays(s):
                        for d in range(DB):
                            if s >= 2:
                                act.wait_ge(h_ready, at(b, half, 2 * STATES, 2 * (s - 2) + d + 1))
                            act.activation(a_ring[:, s % 2, d, :], dec[:, d, :], ACT.Exp, scale=a_neg[:, d, s:s + 1]).then_inc(a_ready, 1)

                    if not first:
                        decays(0)
                    for s in range(STATES):
                        act.wait_ge(c_ready, at(b, half, STATES, s + 1))
                        if s >= 2:
                            act.wait_ge(hc_ready, at(b, half, 2 * STATES, 2 * (s - 1)))
                        act.activation(c_sb[:, s % 2, :], c_bank[s % 2][:, :], ACT.Copy).then_inc(c_kept, 1)
                        if not first and s + 1 < STATES:
                            decays(s + 1)
                        if half == 0:
                            for d in range(DB):
                                act.wait_ge(h_ready, at(b, half, 2 * STATES, 2 * s + d + 1))
                                act.activation(carry[:, s, d:d + 1], h[:, s % 2, d, CH - 1:CH], ACT.Copy).then_inc(carried, 1)
                    norm_act(act, ln2, at(b, half, 1, 0), cent[:, :], cent_sq[:, :], p_bank[1][:, :], std[:, :], eps)

        @block.gpsimd
        def _(pool):
            pool.memset(x_in[:, :, 0:TAPS - 1], 0.0).then_inc(setup, 1)
            pool.memset(select[:, :, :], 1.0).then_inc(select_ones, 1)
            pool.wait_ge(select_ones, 1)
            pool.affine_select(out=select[:, :, :], in_=select[:, :, :], pattern=[[-1, 2 * STATES], [0, P]],
                               compare_op=ALU.is_equal, fill=0.0, base=-low, channel_multiplier=1).then_inc(setup, 1)
            with pool.Fori(0, BATCH) as b:
                for half in range(HALVES):
                    for s in range(STATES):
                        pool.wait_ge(c_kept, at(b, half, STATES, s + 1))
                        for d in range(DB):
                            pool.wait_ge(h_ready, at(b, half, 2 * STATES, 2 * s + d + 1))
                            if s >= 2:
                                pool.wait_ge(summed, at(b, half, 2 * STATES, 2 * (s - 2) + d + 1))
                            pool.tensor_tensor(hc[:, s % 2, d, :], h[:, s % 2, d, :], c_sb[:, s % 2, :], ALU.mult).then_inc(hc_ready, 1)

        @block.vector
        def _(dve):
            dve.wait_ge(loaded, LOADS)
            if first:
                dve.tensor_scalar(neg_dt[:, :], vec[:, 2:4], -1.0, None, ALU.mult).then_inc(setup, 1)
            else:
                for d in range(DB):
                    for k in range(TAPS):
                        dve.tensor_scalar(diag[:, d, k, :], ident, taps[:, d, k:k + 1], None, ALU.mult).then_inc(setup, 1)
                dve.wait_ge(setup, SETUP - 1)
                dve.tensor_scalar(a_neg[:, :, :], a_neg[:, :, :], -1.0, None, ALU.mult).then_inc(setup, 1)
            with dve.Fori(0, BATCH) as b:
                for half in range(HALVES):
                    if first:
                        dve.wait_ge(x_ready, at(b, half, 1, 1))
                        norm_dve(dve, ln1, at(b, half, 1, 0), xs[:, :], cent[:, :], std[:, :], rstd[:, :], p_bank[0][:, :])
                        dve.tensor_tensor(xn[:, :], cent[:, :], rstd[:, :], ALU.mult).then_inc(scaled, 1)
                        dve.wait_ge(scaled, at(b, half, 1, 1))
                        dve.tensor_scalar(xn2[:, :], xn[:, :], vec[:, 4:5], vec[:, 5:6], ALU.mult, ALU.add).then_inc(xn_ready, 1)
                        dve.wait_ge(pre_ev, at(b, half, PRE, 9))
                    else:
                        dve.wait_ge(soft_step, at(b, half, 2, 2))
                        e, q = soft[:, :, 2, :], soft[:, :, 1, :]
                        dve.tensor_scalar(q, e, log1p[LOG1P_DEGREE], None, ALU.mult).then_inc(poly_step, 1)
                        for k in range(LOG1P_DEGREE):
                            dve.wait_ge(poly_step, at(b, half, LOG1P_DEGREE + 1, k + 1))
                            dve.scalar_tensor_tensor(q, q, log1p[LOG1P_DEGREE - 1 - k], e, ALU.add, ALU.mult).then_inc(poly_step, 1)
                        dve.wait_ge(poly_step, at(b, half, LOG1P_DEGREE + 1, LOG1P_DEGREE + 1))
                        dve.scalar_tensor_tensor(dec[:, :, :], soft[:, :, 0, :], 0.0, soft[:, :, 1, :], ALU.max,
                                                 ALU.add).then_inc(delta_ready, 1)
                        dve.wait_ge(delta_ready, at(b, half, 2, 1))
                        dve.tensor_tensor(du[:, :, :], dec[:, :, :], u[:, :, :], ALU.mult).then_inc(delta_ready, 1)
                        dve.wait_ge(delta_ready, at(b, half, 2, 2))
                    for s in range(STATES):
                        dve.wait_ge(b_ready, at(b, half, STATES, s + 1))
                        for d in range(DB):
                            if s >= 2:
                                dve.wait_ge(h_ready, at(b, half, 2 * STATES, 2 * (s - 2) + d + 1))
                            dve.tensor_tensor(bu[:, s % 2, d, :], du[:, d, :], b_bank[s % 2][:, :], ALU.mult).then_inc(bu_ready, 1)
                        for d in range(DB):
                            dve.wait_ge(bu_ready, at(b, half, 2 * STATES, 2 * s + d + 1))
                            if s >= 2:
                                dve.wait_ge(hc_ready, at(b, half, 2 * STATES, 2 * (s - 2) + d + 1))
                                if half == 0:
                                    dve.wait_ge(carried, b * 2 * STATES + (2 * (s - 2) + d + 1))
                            elif half == 1:
                                dve.wait_ge(carried, b * 2 * STATES + 2 * STATES)
                            if not first:
                                dve.wait_ge(a_ready, at(b, half, 2 * STATES, 2 * s + d + 1))
                            decay = dec[:, d, :] if first else a_ring[:, s % 2, d, :]
                            start = 0.0 if half == 0 else carry[:, s, d:d + 1]
                            dve.tensor_tensor_scan(h[:, s % 2, d, :], decay, bu[:, s % 2, d, :], start, ALU.mult,
                                                   ALU.add).then_inc(h_ready, 1)
                    dve.wait_ge(summed, at(b, half, 2 * STATES, 2 * STATES))
                    for d in range(DB):
                        if first:
                            dve.tensor_tensor(g[:, d, :], gate[:, d, :], y_bank[d][:, :], ALU.mult).then_inc(g_ready, 1)
                        else:
                            dve.scalar_tensor_tensor(yd[:, d, :], u[:, d, :], vec[:, 6 + d:7 + d], y_bank[d][:, :], ALU.mult,
                                                     ALU.add).then_inc(skip_ready, 1)
                            dve.wait_ge(skip_ready, at(b, half, DB, d + 1))
                            dve.tensor_tensor(g[:, d, :], gate[:, d, :], yd[:, d, :], ALU.mult).then_inc(g_ready, 1)
                    dve.wait_ge(out_ready, at(b, half, 1, 1))
                    dve.tensor_tensor(r[:, :], xs[:, :], p_bank[0][:, :], ALU.add).then_inc(res_ready, 1)
                    dve.wait_ge(res_ready, at(b, half, 2, 1))
                    dve.tensor_tensor(r2[:, :], r[:, :], X[:, cols(b, half)], ALU.add).then_inc(res_ready, 1)
                    dve.wait_ge(res_ready, at(b, half, 2, 2))
                    norm_dve(dve, ln2, at(b, half, 1, 0), r2[:, :], cent[:, :], std[:, :], rstd[:, :], p_bank[0][:, :])
                    dve.tensor_tensor(X[:, cols(b, half)], cent[:, :], rstd[:, :], ALU.mult).then_inc(done, 1)


EXPERTS = 8
FF = 512
FB = FF // P
THRESHOLD = 0.125


def experts(nc, sem, X, d, consts):
    ident, mean_w, eps = consts
    G = EXPERTS + 1
    with ExitStack() as mem:
        def sb(label, shape, dt=F32):
            return mem.enter_context(nc.sbuf_tensor(f"b_{label}", shape, dt))

        def bank(label):
            return mem.enter_context(nc.psum_tensor(f"b_{label}", [P, CH], F32))

        w1 = sb("w1", [P, EXPERTS, FF])
        w2 = sb("w2", [P, EXPERTS, FB, DIM])
        b1 = sb("b1", [P, EXPERTS * FB])
        b2 = sb("b2", [EXPERTS, DIM])
        wg = sb("w_gate", [P, G])
        bg = sb("gate_bias", [P, G])
        select = sb("select", [EXPERTS, EXPERTS, P])
        logit = sb("logit", [P, NT, G])
        top = sb("top", [P, NT])
        ex = sb("exps", [P, NT, EXPERTS])
        total = sb("total", [P, NT])
        inv = sb("inverse", [P, NT])
        thr = sb("threshold", [P, NT])
        fix = sb("zero_fix", [P, NT])
        wt = sb("weights", [P, NT, EXPERTS])
        w_rows = sb("weight_rows", [EXPERTS, TOKENS])
        xs = sb("x", [P, CH])
        wc = sb("chunk_weights", [EXPERTS, CH])
        wb = sb("spread_weights", [P, 2, CH])
        hid = sb("hidden", [P, 4, CH])
        part = sb("weighted", [P, 2, CH])
        acc = sb("acc", [P, CH])
        res = sb("residual", [P, CH])
        cent = sb("cent", [P, CH])
        cent_sq = sb("cent_sq", [P, CH])
        std = sb("std", [P, CH])
        rstd = sb("rstd", [P, CH])
        h_bank = [bank(f"h_bank{i}") for i in range(3)]
        o_bank = [bank(f"o_bank{i}") for i in range(2)]
        w_bank = bank("w_bank")
        n_bank = [bank(f"n_bank{i}") for i in range(2)]

        loaded = sem("b_weights_loaded")
        gate_loaded = sem("b_gate_loaded")
        select_step = sem("b_select_step")
        logits_ready = sem("b_logits_ready")
        gate_step = sem("b_gate_step")
        gate_act = sem("b_gate_exps")
        gate_fix = sem("b_zero_sum_step")
        turned = sem("b_weights_turned")
        turned_kept = sem("b_weight_rows_kept")
        x_ready = sem("b_x_ready")
        hid_mm = sem("b_hidden_ready")
        gelu_ready = sem("b_gelu_ready")
        out_mm = sem("b_expert_out")
        spread_mm = sem("b_weights_spread")
        spread_kept = sem("b_spread_kept")
        weighted = sem("b_weighted")
        summed = sem("b_summed")
        bias_mm = sem("b_bias_ready")
        res_ready = sem("b_residual_ready")
        ln = Norm(sem, "b_ln")
        done = sem("b_chunk_done")
        UNITS = EXPERTS * FB
        CHUNKS = TOKENS // CH
        block = mem.enter_context(nc.Block())

        @block.sync
        def _(sp):
            sp.dma_start(wg[:, :], d["b_gate"]).then_inc(gate_loaded, 16)
            sp.dma_start(bg[:, :], d["b_gate_bias"]).then_inc(gate_loaded, 16)
            sp.dma_start(b1[:, :], d["b_b1"]).then_inc(loaded, 16)
            sp.dma_start(b2[:, :], d["b_b2"]).then_inc(loaded, 16)
            sp.dma_start(w1[:, :, :], d["b_w1"].rearrange("e p f -> p e f")).then_inc(loaded, 16)
            for e in range(EXPERTS):
                sp.dma_start(w2[:, e, :, :], d["b_w2"][e].rearrange("(f p) o -> p f o", p=P)).then_inc(loaded, 16)

        @block.gpsimd
        def _(pool):
            pool.memset(select[:, :, :], 1.0).then_inc(select_step, 1)
            pool.wait_ge(select_step, 1)
            pool.affine_select(out=select[:, :, :], in_=select[:, :, :], pattern=[[-1, EXPERTS], [0, P]],
                               compare_op=ALU.is_equal, fill=0.0, base=0, channel_multiplier=1).then_inc(select_step, 1)

        @block.tensor
        def _(pe):
            pe.wait_ge(gate_loaded, 32)
            logits = n_bank[0][:, 0:NT * G].rearrange("p (t g) -> p t g", g=G)
            for t in range(NT):
                ins = pe.matmul(logits[:, t, :], lhsT=X[:, t * P:t * P + P], rhs=wg[:, :], start=True, stop=True)
            ins.then_inc(logits_ready, 1)
            pe.wait_ge(gate_step, 11)
            for c in range(CHUNKS):
                if c >= 2:
                    pe.wait_ge(turned_kept, c - 1)
                for j in range(CH // P):
                    ins = pe.transpose(n_bank[c % 2][0:EXPERTS, j * P:j * P + P], wt[:, c * (CH // P) + j, :], ident)
                ins.then_inc(turned, 1)
            pe.wait_ge(loaded, 16 * (3 + EXPERTS))
            pe.wait_ge(select_step, 2)
            with pe.Fori(0, CHUNKS) as c:
                pe.wait_ge(x_ready, c * 2 + 2)

                def accumulate(u):
                    e, f = u // FB, u % FB
                    pe.wait_ge(gelu_ready, c * UNITS + (u + 1))
                    if f == 0 and e >= 2:
                        pe.wait_ge(weighted, c * EXPERTS + (e - 1))
                    pe.matmul(o_bank[e % 2][:, :], lhsT=w2[:, e, f, :], rhs=hid[:, u % 4, :], start=f == 0,
                              stop=f == FB - 1).then_inc(out_mm, 1)

                for u in range(UNITS):
                    e, f = u // FB, u % FB
                    if f == 0:
                        if e >= 1:
                            pe.wait_ge(spread_kept, c * EXPERTS + e)
                        pe.matmul(w_bank[:, :], lhsT=select[:, e, :], rhs=wc[:, :], start=True, stop=True).then_inc(spread_mm, 1)
                    if u >= 3:
                        pe.wait_ge(gelu_ready, c * UNITS + (u - 2))
                    pe.matmul(h_bank[u % 3][:, :], lhsT=w1[:, e, f * P:f * P + P], rhs=xs[:, :], start=True,
                              stop=True).then_inc(hid_mm, 1)
                    if u >= 2:
                        accumulate(u - 2)
                accumulate(UNITS - 2)
                accumulate(UNITS - 1)
                pe.matmul(n_bank[1][:, :], lhsT=b2[:, :], rhs=wc[:, :], start=True, stop=True).then_inc(bias_mm, 1)
                pe.wait_ge(res_ready, c * 2 + 2)
                norm_pe(pe, ln, c, mean_w, res[:, :], cent_sq[:, :], n_bank[0][:, :], n_bank[1][:, :])

        @block.scalar
        def _(act):
            act.wait_ge(gate_step, 3)
            act.activation(ex[:, :, :], ex[:, :, :], ACT.Exp).then_inc(gate_act, 1)
            act.activation(thr[:, :], logit[:, :, EXPERTS], ACT.Sigmoid).then_inc(gate_act, 1)
            for c in range(CHUNKS):
                act.wait_ge(turned, c + 1)
                act.activation(w_rows[:, c * CH:c * CH + CH], n_bank[c % 2][0:EXPERTS, :], ACT.Copy).then_inc(turned_kept, 1)
            act.wait_ge(turned_kept, CHUNKS)
            act.wait_ge(loaded, 16 * (3 + EXPERTS))
            with act.Fori(0, CHUNKS) as c:
                act.wait_ge(done, c)
                act.activation(xs[:, :], X[:, bass.ds(c * CH, CH)], ACT.Copy).then_inc(x_ready, 1)
                act.activation(wc[:, :], w_rows[:, bass.ds(c * CH, CH)], ACT.Copy).then_inc(x_ready, 1)
                for u in range(UNITS):
                    e, f = u // FB, u % FB
                    if f == 0:
                        act.wait_ge(spread_mm, c * EXPERTS + (e + 1))
                        if e >= 2:
                            act.wait_ge(weighted, c * EXPERTS + (e - 1))
                        act.activation(wb[:, e % 2, :], w_bank[:, :], ACT.Copy).then_inc(spread_kept, 1)
                    act.wait_ge(hid_mm, c * UNITS + (u + 1))
                    if u >= 4:
                        act.wait_ge(out_mm, c * UNITS + (u - 3))
                    act.activation(hid[:, u % 4, :], h_bank[u % 3][:, :], ACT.Gelu_apprx_tanh, bias=b1[:, u:u + 1]).then_inc(gelu_ready, 1)
                norm_act(act, ln, c, cent[:, :], cent_sq[:, :], n_bank[1][:, :], std[:, :], eps)

        @block.vector
        def _(dve):
            dve.wait_ge(logits_ready, 1)
            dve.tensor_tensor(logit[:, :, :], n_bank[0][:, 0:NT * G].rearrange("p (t g) -> p t g", g=G),
                              bg[:, :].unsqueeze(1).to_broadcast([P, NT, G]), ALU.add).then_inc(gate_step, 1)
            dve.wait_ge(gate_step, 1)
            dve.tensor_reduce(top[:, :], logit[:, :, 0:EXPERTS], AX.X, ALU.max).then_inc(gate_step, 1)
            dve.wait_ge(gate_step, 2)
            dve.tensor_tensor(ex[:, :, :], logit[:, :, 0:EXPERTS], top[:, :].unsqueeze(2).to_broadcast([P, NT, EXPERTS]),
                              ALU.subtract).then_inc(gate_step, 1)
            dve.wait_ge(gate_act, 2)
            dve.tensor_reduce(total[:, :], ex[:, :, :], AX.X, ALU.add).then_inc(gate_step, 1)
            dve.wait_ge(gate_step, 4)
            dve.reciprocal(inv[:, :], total[:, :]).then_inc(gate_step, 1)
            dve.wait_ge(gate_step, 5)
            dve.tensor_tensor(wt[:, :, :], ex[:, :, :], inv[:, :].unsqueeze(2).to_broadcast([P, NT, EXPERTS]), ALU.mult).then_inc(gate_step, 1)
            dve.wait_ge(gate_step, 6)
            dve.tensor_scalar(fix[:, :], thr[:, :], THRESHOLD, None, ALU.mult).then_inc(gate_step, 1)
            dve.wait_ge(gate_step, 7)
            dve.tensor_tensor(ex[:, :, :], wt[:, :, :], fix[:, :].unsqueeze(2).to_broadcast([P, NT, EXPERTS]),
                              ALU.subtract).then_inc(gate_step, 1)
            dve.wait_ge(gate_step, 8)
            dve.tensor_scalar(wt[:, :, :], ex[:, :, :], 0.0, None, ALU.max).then_inc(gate_step, 1)
            dve.wait_ge(gate_step, 9)
            dve.tensor_reduce(total[:, :], wt[:, :, :], AX.X, ALU.add).then_inc(gate_step, 1)
            dve.wait_ge(gate_step, 10)
            dve.scalar_tensor_tensor(fix[:, :], total[:, :], 0.0, total[:, :], ALU.is_equal, ALU.add).then_inc(gate_fix, 1)
            dve.wait_ge(gate_fix, 1)
            dve.reciprocal(inv[:, :], fix[:, :]).then_inc(gate_fix, 1)
            dve.wait_ge(gate_fix, 2)
            dve.tensor_tensor(wt[:, :, :], wt[:, :, :], inv[:, :].unsqueeze(2).to_broadcast([P, NT, EXPERTS]), ALU.mult).then_inc(gate_step, 1)
            with dve.Fori(0, CHUNKS) as c:
                for e in range(EXPERTS):
                    dve.wait_ge(out_mm, c * UNITS + (FB * e + FB))
                    dve.wait_ge(spread_kept, c * EXPERTS + (e + 1))
                    if e >= 2:
                        dve.wait_ge(summed, c * (EXPERTS - 1) + (e - 1))
                    dst = acc[:, :] if e == 0 else part[:, e % 2, :]
                    dve.tensor_tensor(dst, wb[:, e % 2, :], o_bank[e % 2][:, :], ALU.mult).then_inc(weighted, 1)
                    if e >= 1:
                        dve.wait_ge(weighted, c * EXPERTS + (e + 1))
                        dve.tensor_tensor(acc[:, :], acc[:, :], part[:, e % 2, :], ALU.add).then_inc(summed, 1)
                dve.wait_ge(bias_mm, c + 1)
                dve.wait_ge(summed, c * (EXPERTS - 1) + (EXPERTS - 1))
                dve.tensor_tensor(acc[:, :], acc[:, :], n_bank[1][:, :], ALU.add).then_inc(res_ready, 1)
                dve.wait_ge(res_ready, c * 2 + 1)
                dve.tensor_tensor(res[:, :], acc[:, :], xs[:, :], ALU.add).then_inc(res_ready, 1)
                dve.wait_ge(res_ready, c * 2 + 2)
                norm_dve(dve, ln, c, res[:, :], cent[:, :], std[:, :], rstd[:, :], n_bank[0][:, :])
                dve.tensor_tensor(X[:, bass.ds(c * CH, CH)], cent[:, :], rstd[:, :], ALU.mult).then_inc(done, 1)
                dve.wait_ge(done, c + 1)


HEADS = 16
HD = 8
GROUPS = 8
Q_PART = (0, 0, 1, 1, 0, 2, 1, 2)
K_PART = (0, 1, 0, 1, 2, 0, 2, 1)
KROWS = GROUPS * HD
QROWS = KROWS + 3
MASKED = -1e30
ROW_PIECES = [(i, lo, min(CH, P * (i + 1) - lo), lo + CH >= P * (i + 1)) for i in range(SEQ // P)
              for lo in range(0, P * (i + 1), CH)]
COL_PIECES = [(j, lo, CH - lo % CH) for j in range(SEQ // P) for lo in ([P * j, CH] if P * j < CH else [P * j])]
NP1 = len(ROW_PIECES)
NP2 = len(COL_PIECES)
TILES = SEQ // P
PROB_AT = [sum(SEQ - P * k for k in range(j)) for j in range(TILES + 1)]
PROB_COLS = PROB_AT[TILES]
HALF_HEADS = HEADS // 2
HALF_ROWS = HALF_HEADS * HD
OUT_ROWS = HALF_ROWS + HALF_HEADS


def mqa(nc, sem, X, X1, d, consts):
    ident, mean_w, eps = consts
    with ExitStack() as mem:
        def sb(label, shape, dt=F32):
            return mem.enter_context(nc.sbuf_tensor(f"q_{label}", shape, dt))

        def bank(label):
            return mem.enter_context(nc.psum_tensor(f"q_{label}", [P, CH], F32))

        wq = sb("wq", [P, DIM])
        wk = sb("wk", [P, KROWS])
        wv = sb("wv", [P, HD])
        bq = sb("bq", [P, 1])
        bk = sb("bk", [KROWS, 1])
        bv = sb("bv", [P, HD])
        k_pick = sb("k_pick", [KROWS, 3])
        w_out = sb("w_out", [HALF_ROWS, 2, DIM])
        b_out = sb("b_out", [P, 1])
        ident16 = sb("ident16", [P, P], BF16)
        mask_row = sb("mask_row", [P, P], BF16)
        mask_col = sb("mask_col", [P, P], BF16)
        mask_f = sb("mask_f", [P, P])
        qf = sb("q", [P, 2, CH])
        qr = sb("q_rest", [P, 2, CH])
        qp = sb("q_parts", [P, 2, 3, CH], BF16)
        kf = sb("k", [KROWS, CH])
        kr = sb("k_rest", [KROWS, 2, CH])
        kp = sb("k_parts", [KROWS, 3, CH], BF16)
        kt = sb("k_sum", [KROWS, 2, CH])
        keys = sb("keys", [QROWS, 2, TOKENS], BF16)
        vals = sb("values", [P, NT, HD])
        q_all = sb("q_all", [QROWS, HEADS, SEQ], BF16)
        k_now = sb("keys_now", [QROWS, 2, SEQ], BF16)
        v_all = sb("values_for_each_head", [P, TILES, OUT_ROWS])
        head_cols = sb("head_columns", [P, HALF_HEADS, OUT_ROWS])
        v_head = [sb(f"values_of_head{i}", [P, TILES, OUT_ROWS]) for i in range(2)]
        zeros16 = sb("zeros16", [P, CH], BF16)
        spread = sb("spread", [OUT_ROWS, HALF_HEADS, HD])
        piece_max = sb("piece_max", [P, NP1])
        pair_max = sb("pair_max", [P, TILES])
        neg_max = sb("neg_max", [P, 2, TILES])
        m_rest = sb("max_rest", [TILES, 2, P])
        m_part = sb("max_parts", [TILES, 2, 3, P], BF16)
        probs = [sb(f"probs{i}", [P, PROB_COLS]) for i in range(2)]
        upper = sb("attended_upper", [OUT_ROWS, TOKENS])
        attended = (X1, upper)
        att_n = sb("attended_normed", [HALF_ROWS, 2, 2, CH])
        s_bank = [bank(f"s_bank{i}") for i in range(2)]
        t_bank = [bank(f"t_bank{i}") for i in range(3)]
        o_bank = [bank(f"o_bank{i}") for i in range(2)]
        m_bank = bank("m_bank")
        parts_dram = nc.dram_tensor("q_parts_dram", (BATCH, 3, P, SEQ), BF16, kind="Internal").ap()

        loaded = sem("q_weights_loaded")
        mask_step = sem("q_mask_step")
        proj_mm = sem("q_projection_ready")
        proj_kept = sem("q_projection_kept")
        v_kept = sem("q_values_kept")
        q_step = sem("q_split_step")
        k_step = sem("q_key_split_step")
        stored = [sem(f"q_parts_stored{i}") for i in range(2)]
        CHUNKS = TOKENS // CH
        phase = ExitStack()
        block = phase.enter_context(nc.Block())

        @block.sync
        def _(sp):
            w = d["q_wqkv"]
            sp.dma_start(wq[:, :], w[:, 0:DIM]).then_inc(loaded, 16)
            for g in range(GROUPS):
                sp.dma_start(wk[:, g * HD:g * HD + HD], w[:, DIM:DIM + HD]).then_inc(loaded, 16)
                sp.dma_start(bk[g * HD:g * HD + HD, :], d["q_bias"][DIM:DIM + HD, :]).then_inc(loaded, 16)
            sp.dma_start(wv[:, :], w[:, DIM + HD:DIM + 2 * HD]).then_inc(loaded, 16)
            sp.dma_start(bq[:, :], d["q_bias"][0:DIM, :]).then_inc(loaded, 16)
            sp.dma_start(bv[:, :], d["q_value_bias"]).then_inc(loaded, 16)
            sp.dma_start(k_pick[:, :], d["q_key_pick"]).then_inc(loaded, 16)
            sp.dma_start(w_out[:, :, :], d["q_w_out"].rearrange("(s p) n -> p s n", p=HALF_ROWS)).then_inc(loaded, 16)
            sp.dma_start(b_out[:, :], d["q_b_out"]).then_inc(loaded, 16)
            for c in range(CHUNKS):
                sp.wait_ge(q_step, 5 * c + 5)
                sp.dma_start(parts_dram[c // 2, :, :, (c % 2) * CH:(c % 2) * CH + CH].rearrange("s p t -> p s t"),
                             qp[:, c % 2, :, :]).then_inc(stored[c % 2], 16)
            for slot in range(2):
                sp.wait_ge(stored[slot], 16 * CHUNKS // 2)

        @block.gpsimd
        def _(pool):
            pool.memset(mask_f[:, :], 0.0).then_inc(mask_step, 1)
            pool.wait_ge(mask_step, 1)
            pool.affine_select(out=mask_row[:, :], in_=mask_f[:, :], pattern=[[-1, P]], compare_op=ALU.is_ge, fill=MASKED,
                               base=0, channel_multiplier=1).then_inc(mask_step, 1)
            pool.memset(spread[:, :, :], 1.0).then_inc(mask_step, 1)
            pool.wait_ge(mask_step, 3)
            pool.affine_select(out=spread[:, :, :], in_=spread[:, :, :], pattern=[[-1, HALF_HEADS], [0, HD]],
                               compare_op=ALU.is_equal, fill=0.0, base=-HALF_ROWS, channel_multiplier=1).then_inc(mask_step, 1)
            pool.affine_select(out=mask_col[:, :], in_=mask_f[:, :], pattern=[[1, P]], compare_op=ALU.is_ge, fill=MASKED,
                               base=0, channel_multiplier=-1).then_inc(mask_step, 1)

        @block.tensor
        def _(pe):
            pe.wait_ge(loaded, 16 * (2 * GROUPS + 7))
            for c in range(CHUNKS):
                x = X[:, c * CH:c * CH + CH]
                if c >= 2:
                    pe.wait_ge(proj_kept, 2 * (c - 1))
                pe.matmul(s_bank[c % 2][:, :], lhsT=wq[:, :], rhs=x, start=True, stop=True).then_inc(proj_mm, 1)
                pe.matmul(o_bank[c % 2][0:KROWS, :], lhsT=wk[:, :], rhs=x, start=True, stop=True).then_inc(proj_mm, 1)
                if c >= 2:
                    pe.wait_ge(v_kept, c)
                for j in range(CH // P):
                    ins = pe.matmul(t_bank[c % 2][:, j * HD:j * HD + HD], lhsT=X[:, c * CH + j * P:c * CH + j * P + P], rhs=wv[:, :],
                                    start=True, stop=True)
                ins.then_inc(proj_mm, 1)

        @block.scalar
        def _(act):
            act.activation(ident16[:, :], ident, ACT.Copy)
            act.wait_ge(loaded, 16 * (2 * GROUPS + 7))
            for c in range(CHUNKS):
                act.wait_ge(proj_mm, 3 * c + 1)
                if c >= 2:
                    act.wait_ge(q_step, 5 * (c - 1))
                act.activation(qf[:, c % 2, :], s_bank[c % 2][:, :], ACT.Identity, bias=bq[:, :]).then_inc(proj_kept, 1)
                act.wait_ge(proj_mm, 3 * c + 2)
                if c >= 1:
                    act.wait_ge(k_step, 8 * c)
                act.activation(kf[:, :], o_bank[c % 2][0:KROWS, :], ACT.Identity, bias=bk[:, :]).then_inc(proj_kept, 1)

        @block.vector
        def _(dve):
            dve.memset(v_all[:, :, HALF_ROWS:OUT_ROWS], 1.0)
            dve.memset(zeros16[:, :], 0.0)
            dve.memset(head_cols[:, :, :], 0.0).then_inc(v_kept, 1)
            dve.wait_ge(v_kept, 1)
            for h in range(HALF_HEADS):
                dve.memset(head_cols[:, h, h * HD:h * HD + HD], 1.0)
                dve.memset(head_cols[:, h, HALF_ROWS + h:HALF_ROWS + h + 1], 1.0)
            dve.memset(keys[KROWS:QROWS, 0, :], 0.0)
            dve.memset(keys[KROWS:QROWS, 1, :], 1.0)
            dve.memset(q_all[KROWS:QROWS, :, :], 0.0)
            for c in range(CHUNKS):
                dve.wait_ge(proj_mm, 3 * c + 3)
                dve.tensor_tensor(vals[:, 4 * c:4 * c + 4, :], t_bank[c % 2][:, 0:4 * HD].rearrange("p (t v) -> p t v", v=HD),
                                  bv[:, :].unsqueeze(1).to_broadcast([P, 4, HD]), ALU.add).then_inc(v_kept, 1)
                q, r, s = qf[:, c % 2, :], qr, qp[:, c % 2]
                dve.wait_ge(proj_kept, 2 * c + 1)
                if c >= 2:
                    dve.wait_ge(stored[c % 2], 16 * (c // 2))
                dve.tensor_copy(s[:, 0, :], q).then_inc(q_step, 1)
                dve.wait_ge(q_step, 5 * c + 1)
                dve.tensor_tensor(r[:, 0, :], q, s[:, 0, :], ALU.subtract).then_inc(q_step, 1)
                dve.wait_ge(q_step, 5 * c + 2)
                dve.tensor_copy(s[:, 1, :], r[:, 0, :]).then_inc(q_step, 1)
                dve.wait_ge(q_step, 5 * c + 3)
                dve.tensor_tensor(r[:, 1, :], r[:, 0, :], s[:, 1, :], ALU.subtract).then_inc(q_step, 1)
                dve.wait_ge(q_step, 5 * c + 4)
                dve.tensor_copy(s[:, 2, :], r[:, 1, :]).then_inc(q_step, 1)
                dve.wait_ge(proj_kept, 2 * c + 2)
                dve.tensor_copy(kp[:, 0, :], kf[:, :]).then_inc(k_step, 1)
                dve.wait_ge(k_step, 8 * c + 1)
                dve.tensor_tensor(kr[:, 0, :], kf[:, :], kp[:, 0, :], ALU.subtract).then_inc(k_step, 1)
                dve.wait_ge(k_step, 8 * c + 2)
                dve.tensor_copy(kp[:, 1, :], kr[:, 0, :]).then_inc(k_step, 1)
                dve.wait_ge(k_step, 8 * c + 3)
                dve.tensor_tensor(kr[:, 1, :], kr[:, 0, :], kp[:, 1, :], ALU.subtract).then_inc(k_step, 1)
                dve.wait_ge(k_step, 8 * c + 4)
                dve.tensor_scalar(kt[:, 0, :], kp[:, 0, :], k_pick[:, 0:1], None, ALU.mult).then_inc(k_step, 1)
                dve.tensor_copy(kp[:, 2, :], kr[:, 1, :]).then_inc(k_step, 1)
                dve.wait_ge(k_step, 8 * c + 6)
                dve.scalar_tensor_tensor(kt[:, 1, :], kp[:, 1, :], k_pick[:, 1:2], kt[:, 0, :], ALU.mult, ALU.add).then_inc(k_step, 1)
                dve.wait_ge(k_step, 8 * c + 7)
                for slot in range(2):
                    ins = dve.scalar_tensor_tensor(keys[0:KROWS, slot, c * CH:c * CH + CH], kp[:, 2, :], k_pick[:, 2:3], kt[:, 1, :],
                                                   ALU.mult, ALU.add)
                ins.then_inc(k_step, 1)
                dve.wait_ge(k_step, 8 * c + 8)

        phase.close()

        q_landed = sem("q_queries_landed")
        batch_copied = sem("q_batch_copied")
        row_scores = sem("q_row_scores_ready")
        row_max = sem("q_piece_max_ready")
        neg_ready = sem("q_neg_max_ready")
        max_turned = sem("q_max_turned")
        max_step = sem("q_max_split_step")
        max_landed = sem("q_max_rows_landed")
        col_scores = sem("q_col_scores_ready")
        exp_ready = sem("q_exps_ready")
        v_ready = sem("q_head_values_ready")
        out_mm = sem("q_head_out_ready")
        evacuated = sem("q_half_kept")
        inverted = sem("q_sums_inverted")
        NMAX = 3

        def hcount(b, h, per, k):
            return b * (HEADS * per) + (h * per + k)

        phase = ExitStack()
        block = phase.enter_context(nc.Block())

        @block.sync
        def _(sp):
            with sp.Fori(0, BATCH) as b:
                sp.wait_ge(out_mm, b * HEADS)
                for g in range(GROUPS):
                    src = parts_dram[bass.ds(b, 1), Q_PART[g]].rearrange("o (h j) t -> j (o h) t", j=HD)
                    sp.dma_start(q_all[g * HD:g * HD + HD, :, :], src).then_inc(q_landed, 16)
                with sp.Fori(0, HEADS) as h:
                    sp.wait_ge(max_step, hcount(b, h, 5, 5))
                    for k in range(3):
                        sp.dma_start(q_all[KROWS + k:KROWS + k + 1, bass.ds(h, 1), :],
                                     m_part[:, 0, k, :]).then_inc(max_landed, 16)

        @block.tensor
        def _(pe):
            with pe.Fori(0, BATCH) as b:
                pe.wait_ge(batch_copied, b * 3 + 3)
                pe.wait_ge(q_landed, b * (16 * GROUPS) + 16 * GROUPS)

                def row_piece(h, n):
                    i, lo, size, last = ROW_PIECES[n]
                    pe.wait_ge(row_max, hcount(b, h, NP1, max(n - 1, 0)))
                    ins = pe.matmul(s_bank[n % 2][:, 0:size], lhsT=q_all[:, bass.ds(h, 1), i * P:i * P + P],
                                    rhs=k_now[:, 0, lo:lo + size], start=True, stop=not last)
                    if last:
                        ins = pe.matmul(s_bank[n % 2][:, size - P:size], lhsT=ident16[:, :], rhs=mask_row[:, :], start=False,
                                        stop=True)
                    ins.then_inc(row_scores, 1)

                def turn(h, slot):
                    pe.wait_ge(neg_ready, hcount(b, h, NMAX, NMAX))
                    pe.transpose(m_bank[0:TILES, 0:P], neg_max[:, slot, :], ident).then_inc(max_turned, 1)

                def cols(h, slot, turn_next, rows_next):
                    pe.wait_ge(max_landed, hcount(b, h, 48, 48))
                    pe.wait_ge(v_ready, hcount(b, h, 1, 1))

                    def product(n):
                        j, lo, size = COL_PIECES[n]
                        pe.wait_ge(exp_ready, hcount(b, h, NP2, n + 1))
                        at = PROB_AT[j] + lo - j * P
                        return pe.matmul(o_bank[lo // CH][0:OUT_ROWS, lo % CH:lo % CH + size], lhsT=v_head[slot][:, j, :],
                                         rhs=probs[slot][:, at:at + size], start=False, stop=True, skip_group_check=True)

                    for n, (j, lo, size) in enumerate(COL_PIECES):
                        pe.wait_ge(exp_ready, hcount(b, h, NP2, max(n - 2, 0)))
                        first = lo == j * P
                        ins = pe.matmul(t_bank[n % 3][:, 0:size], lhsT=k_now[:, 1, j * P:j * P + P],
                                        rhs=q_all[:, bass.ds(h, 1), lo:lo + size], start=True, stop=not first)
                        if first:
                            ins = pe.matmul(t_bank[n % 3][:, 0:P], lhsT=ident16[:, :], rhs=mask_col[:, :], start=False, stop=True)
                        ins.then_inc(col_scores, 1)
                        if rows_next:
                            row_piece(h + 2, n)
                        if n == 1 and turn_next:
                            turn(h + 1, 1 - slot)
                        if n >= 2:
                            product(n - 2)
                    product(NP2 - 2)
                    product(NP2 - 1).then_inc(out_mm, 1)

                def begin(half):
                    pe.wait_ge(evacuated, b * 4 + 2 * half)
                    for s in range(2):
                        pe.matmul(o_bank[s][0:OUT_ROWS, :], lhsT=zeros16[:, 0:OUT_ROWS], rhs=zeros16[:, :], start=True, stop=True)

                for n in range(NP1):
                    row_piece(0, n)
                turn(0, 0)
                for n in range(NP1):
                    row_piece(1, n)
                begin(0)
                with pe.Fori(0, HALF_HEADS // 2) as g:
                    cols(g * 2, 0, True, True)
                    cols(g * 2 + 1, 1, True, True)
                begin(1)
                with pe.Fori(HALF_HEADS // 2, HEADS // 2 - 1) as g:
                    cols(g * 2, 0, True, True)
                    cols(g * 2 + 1, 1, True, True)
                cols(HEADS - 2, 0, True, False)
                cols(HEADS - 1, 1, False, False)

        @block.scalar
        def _(act):
            with act.Fori(0, BATCH) as b:
                act.wait_ge(out_mm, b * HEADS)
                for slot in range(2):
                    act.activation(k_now[:, slot, :], keys[:, slot, bass.ds(b * SEQ, SEQ)], ACT.Copy).then_inc(batch_copied, 1)
                for h in range(HALF_HEADS):
                    ins = act.activation(v_all[:, :, h * HD:h * HD + HD], vals[:, bass.ds(b * TILES, TILES), :], ACT.Copy)
                ins.then_inc(batch_copied, 1)

                def exps(h, slot):
                    for n, (j, lo, size) in enumerate(COL_PIECES):
                        act.wait_ge(col_scores, hcount(b, h, NP2, n + 1))
                        at = PROB_AT[j] + lo - j * P
                        act.activation(probs[slot][:, at:at + size], t_bank[n % 3][:, 0:size], ACT.Exp,
                                       scale=float(HD) ** -0.5).then_inc(exp_ready, 1)

                for half in range(2):
                    with act.Fori(half * HALF_HEADS // 2, (half + 1) * HALF_HEADS // 2) as g:
                        exps(g * 2, 0)
                        exps(g * 2 + 1, 1)
                    for s in range(2):
                        act.wait_ge(out_mm, b * HEADS + (half + 1) * HALF_HEADS)
                        act.activation(attended[half][0:OUT_ROWS, bass.ds(b * SEQ + s * CH, CH)], o_bank[s][0:OUT_ROWS, :],
                                       ACT.Copy).then_inc(evacuated, 1)

        @block.vector
        def _(dve):
            with dve.Fori(0, BATCH) as b:
                def reduces(h, first, end):
                    for n in range(first, end):
                        dve.wait_ge(row_scores, hcount(b, h, NP1, n + 1))
                        dve.tensor_reduce(piece_max[:, n:n + 1], s_bank[n % 2][:, 0:ROW_PIECES[n][2]], AX.X, ALU.max).then_inc(row_max, 1)

                def negate(h, slot):
                    dve.wait_ge(row_max, hcount(b, h, NP1, NP1))
                    dve.tensor_scalar(neg_max[:, slot, 0:4], piece_max[:, 0:4], -1.0, None, ALU.mult).then_inc(neg_ready, 1)
                    two = piece_max[:, 4:NP1].rearrange("p (i s) -> p i s", s=2)
                    dve.tensor_tensor(pair_max[:, 4:TILES], two[:, :, 0], two[:, :, 1], ALU.max).then_inc(neg_ready, 1)
                    dve.wait_ge(neg_ready, hcount(b, h, NMAX, 2))
                    dve.tensor_scalar(neg_max[:, slot, 4:TILES], pair_max[:, 4:TILES], -1.0, None, ALU.mult).then_inc(neg_ready, 1)

                def split(h, slot):
                    dve.wait_ge(max_turned, hcount(b, h, 1, 1))
                    dve.wait_ge(max_landed, hcount(b, h, 48, 0))
                    m, r, s = m_bank[0:TILES, 0:P], m_rest, m_part[:, 0]
                    dve.tensor_copy(s[:, 0, :], m).then_inc(max_step, 1)
                    dve.wait_ge(max_step, hcount(b, h, 5, 1))
                    dve.tensor_tensor(r[:, 0, :], m, s[:, 0, :], ALU.subtract).then_inc(max_step, 1)
                    dve.wait_ge(max_step, hcount(b, h, 5, 2))
                    dve.tensor_copy(s[:, 1, :], r[:, 0, :]).then_inc(max_step, 1)
                    dve.wait_ge(max_step, hcount(b, h, 5, 3))
                    dve.tensor_tensor(r[:, 1, :], r[:, 0, :], s[:, 1, :], ALU.subtract).then_inc(max_step, 1)
                    dve.wait_ge(max_step, hcount(b, h, 5, 4))
                    dve.tensor_copy(s[:, 2, :], r[:, 1, :]).then_inc(max_step, 1)

                def values(h, slot, of):
                    dve.wait_ge(out_mm, hcount(b, h, 1, -1))
                    dve.tensor_tensor(v_head[slot][:, :, :], v_all[:, :, :],
                                      head_cols[:, bass.ds(of, 1), :].to_broadcast([P, TILES, OUT_ROWS]), ALU.mult).then_inc(v_ready, 1)

                def step(h, slot, of_next, rows_next):
                    if rows_next:
                        reduces(h + 2, 0, 2)
                    split(h + 1, 1 - slot)
                    values(h + 1, 1 - slot, of_next)
                    if rows_next:
                        reduces(h + 2, 2, NP1)
                        negate(h + 2, slot)

                def invert(half):
                    for s in range(2):
                        dve.wait_ge(evacuated, b * 4 + (2 * half + s + 1))
                        sums = attended[half][HALF_ROWS:OUT_ROWS, bass.ds(b * SEQ + s * CH, CH)]
                        dve.reciprocal(sums, sums).then_inc(inverted, 1)

                reduces(0, 0, NP1)
                negate(0, 0)
                dve.wait_ge(batch_copied, b * 3 + 3)
                dve.tensor_tensor(v_head[0][:, :, :], v_all[:, :, :], head_cols[:, 0:1, :].to_broadcast([P, TILES, OUT_ROWS]),
                                  ALU.mult).then_inc(v_ready, 1)
                split(0, 0)
                reduces(1, 0, NP1)
                negate(1, 1)
                with dve.Fori(0, HALF_HEADS // 2) as g:
                    step(g * 2, 0, g * 2 + 1, True)
                    step(g * 2 + 1, 1, (g * 2 + 2) % HALF_HEADS, True)
                invert(0)
                with dve.Fori(HALF_HEADS // 2, HEADS // 2 - 1) as g:
                    step(g * 2, 0, g * 2 + (1 - HALF_HEADS), True)
                    step(g * 2 + 1, 1, g * 2 + (2 - HALF_HEADS), True)
                step(HEADS - 2, 0, HALF_HEADS - 1, False)
                invert(1)

        phase.close()
        sums_spread = sem("q_sums_spread")
        normed = sem("q_att_normed")
        proj = sem("q_out_projected")
        x1_step = sem("q_x1_step")
        block = mem.enter_context(nc.Block())

        @block.tensor
        def _(pe):
            for c in range(CHUNKS):
                for half in range(2):
                    if c >= 1:
                        pe.wait_ge(normed, 2 * (c - 1) + half + 1)
                    pe.matmul(s_bank[half][0:HALF_ROWS, :], lhsT=spread[:, :, :].rearrange("r h v -> r (h v)"),
                              rhs=attended[half][0:OUT_ROWS, c * CH:c * CH + CH], start=True, stop=True).then_inc(sums_spread, 1)
                if c >= 2:
                    pe.wait_ge(x1_step, c - 1)
                for half in range(2):
                    pe.wait_ge(normed, 2 * c + half + 1)
                    ins = pe.matmul(t_bank[c % 2][:, :], lhsT=w_out[:, half, :], rhs=att_n[:, c % 2, half, :], start=half == 0,
                                    stop=half == 1)
                ins.then_inc(proj, 1)

        @block.vector
        def _(dve):
            def project(c):
                dve.wait_ge(proj, c + 1)
                x1 = X1[:, c * CH:c * CH + CH]
                dve.scalar_tensor_tensor(x1, t_bank[c % 2][:, :], b_out[:, 0:1], X[:, c * CH:c * CH + CH], ALU.add, ALU.add).then_inc(x1_step, 1)

            for c in range(CHUNKS):
                for half in range(2):
                    dve.wait_ge(sums_spread, 2 * c + half + 1)
                    dve.tensor_tensor(att_n[:, c % 2, half, :], attended[half][0:HALF_ROWS, c * CH:c * CH + CH],
                                      s_bank[half][0:HALF_ROWS, :], ALU.mult).then_inc(normed, 1)
                if c >= 1:
                    project(c - 1)
            project(CHUNKS - 1)


DEPTH = 6
LH = 16
LD = 64
INNER = LH * LD
WINDOW = 32
FFI = 341
FF_BLOCKS = ((0, P), (P, P), (2 * P, FFI - 2 * P))
HG = 4
NG = LH // HG
QK_SCALE = 8.0
NORM_SCALE = 2.0 ** 20
LANES = 8 * LD


def head_of(g, j):
    return g // 2 * 8 + 2 * j + g % 2


PLACES = [head_of(g, j) for g in range(NG) for j in range(HG)]


def rotary_tables():
    f = np.float32
    half = np.arange(0, LD, 2, dtype=f)
    inv_freq = (f(1.0) / np.power(f(10000.0), half / f(LD))).astype(f)
    t = np.arange(SEQ, dtype=f)
    freqs = (t[:, None] * inv_freq[None, :]).astype(f)
    base = ((half + f(0.4 * LD)) / f(1.4 * LD)).astype(f)
    power = ((t - SEQ // 2) / f(WINDOW // 2)).astype(f)
    scale = np.power(base[None, :], power[:, None]).astype(f)
    cos, sin = np.cos(freqs).astype(f), np.sin(freqs).astype(f)
    inv = (f(1.0) / scale).astype(f)
    both = lambda a, b: np.concatenate([a, b], axis=1)
    tables = np.stack([both(cos * scale, cos * scale), both(-sin * scale, sin * scale),
                       both(cos * inv, cos * inv), both(-sin * inv, sin * inv)], axis=1)
    return np.ascontiguousarray(tables.reshape(TILES, P, 4, LD).transpose(1, 0, 2, 3).astype(f))


def local_layers(nc, sem, Xp, X1p, d, consts):
    ident, mean_w, eps = consts
    X, X1 = Xp[:, 1:], X1p[:, 1:]
    with ExitStack() as mem:
        def sb(label, shape, dt=F32):
            return mem.enter_context(nc.sbuf_tensor(f"d_{label}", shape, dt))

        def bank(label):
            return mem.enter_context(nc.psum_tensor(f"d_{label}", [P, CH], F32))

        w_qkv = sb("w_qkv", [P, 3 * INNER])
        w_o = sb("w_o", [P, INNER // P, DIM])
        w_1 = sb("w_1", [P, 2 * FFI])
        w_2 = sb("w_2", [P, 3, DIM])
        b_1 = sb("b_1", [P, 6])
        vec = sb("vectors", [P, 3])
        base = sb("rotary", [P, TILES, 4, LD])
        table = sb("scaled_rotary", [P, TILES, 4, LD])
        qk_scale = sb("qk_scale", [P, 4, LD])
        ident16 = sb("ident16", [P, P], BF16)
        mask = sb("mask", [P, HG, P], BF16)
        mask_prev = sb("mask_prev", [WINDOW, LH, WINDOW], BF16)
        mask_now = sb("mask_now", [WINDOW, LH, WINDOW], BF16)
        shown = sb("shown", [P, NT])
        hidden = sb("hidden", [P, NT])
        norm_bias = sb("norm_bias", [P, 1])
        xs = [sb(f"x{i}", [P, P]) for i in range(2)]
        sq = sb("squares", [P, 2, 8, LD])
        t1 = sb("rotated1", [P, 4, 8, LD])
        t2 = sb("rotated2", [P, 4, 8, LD])
        ssq = sb("square_sums", [P, 4 * 8])
        ssq_c = sb("square_sums_guarded", [P, 4 * 8])
        ssq_l = sb("square_sums_log", [P, 4 * 8])
        inv_n = sb("inverse_norms", [P, 4 * 8])
        q_t = sb("q_turned", [P, LH // 2, P])
        k_t = [sb(f"k_turned{i}", [P, LH // 2, P]) for i in range(2)]
        v = [sb(f"v{i}", [P, LH, LD]) for i in range(2)]
        v_prev = [sb(f"v_prev{i}", [P, NG, HG, LD]) for i in range(2)]
        top = sb("top", [P, LH])
        top_prev = sb("top_prev", [WINDOW, LH])
        z = sb("exps", [P, NG, HG, P])
        z_prev = sb("exps_prev", [WINDOW, LH, WINDOW])
        pt = sb("probs_turned", [P, NG, HG, P])
        pt_prev = sb("probs_turned_prev", [P, NG, WINDOW])
        sums = sb("sums", [P, LH])
        sums_prev = sb("sums_prev", [WINDOW, LH])
        inv_s = sb("inverse_sums", [P, LH])
        att_t = sb("attended_turned", [P, INNER // P, P])
        flat = lambda t: t[:, :, :, :].rearrange("p a b c -> p (a b c)")
        f1, f2 = flat(t1), flat(t2)
        fx = [f1[:, i * CH:i * CH + CH] for i in range(2)]
        fc = [f1[:, (2 + i) * CH:(3 + i) * CH] for i in range(2)]
        fq = [f2[:, i * CH:i * CH + CH] for i in range(2)]
        fl = [f2[:, (2 + i) * CH:(3 + i) * CH] for i in range(2)]
        zf, pf = flat(z), flat(pt)
        fr = [zf[:, i * CH:i * CH + CH] for i in range(2)]
        fn = [zf[:, (2 + i) * CH:(3 + i) * CH] for i in range(2)]
        gl = [pf[:, i * CH:i * CH + CH] for i in range(2)]
        hh = [pf[:, (2 + i) * CH:(3 + i) * CH] for i in range(2)]
        hh += [flat(table)[:, 0:CH]]
        s_b = [bank(f"s_bank{i}") for i in range(3)]
        p_b = [bank(f"p_bank{i}") for i in range(2)]
        t_b = [bank(f"t_bank{i}") for i in range(2)]
        w_b = bank("w_bank")
        rotary = nc.inline_tensor(rotary_tables(), "rotary_tables").ap()
        kept_x = nc.dram_tensor("x_before_local", (P, TOKENS), F32, kind="Internal").ap()

        setup = sem("d_setup")
        setup_loads = sem("d_setup_loads")
        x_stored = sem("d_x_stored")
        qkv_loaded = sem("d_qkv_loaded")
        ffn_loaded = sem("d_ffn_loaded")
        table_step = sem("d_table_step")
        x_ready = sem("d_x_ready")
        proj = sem("d_projected")
        sq_ready = sem("d_squares_ready")
        rope_ready = sem("d_rope_ready")
        rope_sum = sem("d_rope_sum_ready")
        ssq_step = sem("d_square_sum_step")
        inv_step = sem("d_inverse_norm_step")
        q_unit = sem("d_unit_queries_ready")
        k_unit = sem("d_unit_keys_ready")
        v_kept = sem("d_v_kept")
        vp_landed = [sem(f"d_v_prev_landed{i}") for i in range(2)]
        qk_turned = sem("d_qk_turned")
        mask_ready = sem("d_mask_ready")
        even_done = sem("d_even_heads_done")
        scores = sem("d_scores_ready")
        max_step = sem("d_max_step")
        sub_ready = sem("d_less_max_ready")
        exp_ready = sem("d_exps_ready")
        sum_step = sem("d_sum_step")
        p_norm = sem("d_probs_normed")
        p_turned = sem("d_probs_turned")
        pp_turned = sem("d_prev_probs_turned")
        pp_kept = sem("d_prev_probs_kept")
        attended = sem("d_attended_ready")
        kept = sem("d_t_bank_kept")
        o_mm = sem("d_out_projected")
        x1_ready = sem("d_x1_ready")
        f_x = sem("d_ff_x_ready")
        f_mean = sem("d_ff_mean_ready")
        f_cent = sem("d_ff_centred_ready")
        f_sq = sem("d_ff_squares_ready")
        f_var = sem("d_ff_variance_ready")
        f_log = sem("d_ff_variance_log_ready")
        f_rstd = sem("d_ff_rstd_ready")
        f_norm = sem("d_ff_normed_step")
        f_gate = sem("d_ff_gate_ready")
        f_lin = sem("d_ff_linear_ready")
        f_gelu = sem("d_ff_gelu_ready")
        f_prod = sem("d_ff_product_ready")
        f_out = sem("d_ff_out_ready")
        f_done = sem("d_ff_chunk_done")
        b_step = sem("d_ff_bias_step")
        CHUNKS = TOKENS // CH
        TILE_JOBS = NG + 2 + 4
        LAYER_JOBS = NT * TILE_JOBS
        STEPS = NT
        QKV_LOADS = 16 * 3
        FFN_LOADS = 16 * 6

        with nc.Block() as block:
            @block.sync
            def _(sp):
                sp.dma_start(base[:, :, :, :], rotary).then_inc(setup_loads, 16)
                sp.dma_start(kept_x, X[:, 0:TOKENS]).then_inc(x_stored, 16)
                sp.wait_ge(setup_loads, 16)
                sp.wait_ge(x_stored, 16)

            @block.gpsimd
            def _(pool):
                step = [0]

                def after(ins):
                    ins.then_inc(setup, 1)
                    step[0] += 1
                    pool.wait_ge(setup, step[0])

                after(pool.memset(mask[:, :, :], 0.0))
                after(pool.affine_select(out=mask[:, :, :], in_=mask[:, :, :], pattern=[[0, HG], [-1, P]], compare_op=ALU.is_ge,
                                         fill=MASKED, base=0, channel_multiplier=1))
                after(pool.affine_select(out=mask[:, :, :], in_=mask[:, :, :], pattern=[[0, HG], [1, P]], compare_op=ALU.is_ge,
                                         fill=MASKED, base=WINDOW, channel_multiplier=-1))
                after(pool.memset(mask_prev[:, :, :], 0.0))
                after(pool.affine_select(out=mask_prev[:, :, :], in_=mask_prev[:, :, :], pattern=[[0, LH], [1, WINDOW]],
                                         compare_op=ALU.is_ge, fill=MASKED, base=0, channel_multiplier=-1))

            @block.vector
            def _(dve):
                dve.memset(shown[:, :], 1.0)
                dve.memset(hidden[:, :], 0.0)
                dve.memset(norm_bias[:, :], float(0.5 * np.log(NORM_SCALE)))
                for i in range(2):
                    dve.memset(v_prev[i][:, :, :, :], 0.0)
                    dve.memset(k_t[i][:, :, :], 0.0)
                dve.memset(Xp[:, 0:1], 0.0)
                dve.memset(X1p[:, 0:1], 0.0)
                dve.tensor_copy(ident16[:, :], ident).then_inc(table_step, 1)
                dve.wait_ge(table_step, 1)
                for b in range(BATCH):
                    dve.memset(shown[:, b * TILES:b * TILES + 1], 0.0)
                    ins = dve.memset(hidden[:, b * TILES:b * TILES + 1], MASKED)
                ins.then_inc(table_step, 1)

        def cnt(t, per, k):
            return t * per + k

        layers = ExitStack()
        block = layers.enter_context(nc.Block())

        @block.sync
        def _(sp):
            def attention_weights(one):
                sp.dma_start(w_qkv[:, :], d["d_wqkv"][one].rearrange("o p n -> p (o n)")).then_inc(qkv_loaded, 16)
                sp.dma_start(w_o[:, :, :], d["d_wo"][one].rearrange("o (k p) n -> p (o k) n", p=P)).then_inc(qkv_loaded, 16)
                sp.dma_start(qk_scale[:, :, :], d["d_scales"][one].rearrange("o p s n -> p (o s) n")).then_inc(qkv_loaded, 16)

            def layer(L):
                sp.wait_ge(f_done, L * CHUNKS)
                one = bass.ds(L, 1)
                sp.dma_start(b_1[:, :], d["d_b1"][one].rearrange("o p n -> p (o n)")).then_inc(ffn_loaded, 16)
                sp.dma_start(vec[:, :], d["d_ln"][one].rearrange("o p n -> p (o n)")).then_inc(ffn_loaded, 16)
                sp.dma_start(w_1[:, :], d["d_w1"][one].rearrange("o p n -> p (o n)")).then_inc(ffn_loaded, 16)
                for n, (lo, size) in enumerate(FF_BLOCKS):
                    sp.dma_start(w_2[0:size, n, :], d["d_w2"][one, lo:lo + size].rearrange("o p n -> p (o n)")).then_inc(ffn_loaded, 16)

                def prev_values(t, par):
                    sp.wait_ge(v_kept, cnt(t - 1, 2, 2))
                    sp.wait_ge(attended, t * 2 - 2)
                    src = v[1 - par][P - WINDOW:P, :, :].rearrange("p (g j) c -> p g j c", j=HG)
                    for j in range(HG):
                        sp.dma_start(v_prev[par][j * WINDOW:j * WINDOW + WINDOW, :, j, :], src[:, :, j, :]).then_inc(vp_landed[par], 16)

                prev_values(L * STEPS + 1, 1)
                with sp.Fori(1, NT // 2) as g:
                    prev_values(L * STEPS + g * 2, 0)
                    prev_values(L * STEPS + g * 2 + 1, 1)

            attention_weights(slice(0, 1))
            with sp.Fori(0, DEPTH - 1) as L:
                layer(L)
                sp.wait_ge(x1_ready, L * STEPS + STEPS)
                attention_weights(bass.ds(L + 1, 1))
            layer(DEPTH - 1)

        @block.gpsimd
        def _(pool):
            def add(L, i, n):
                t = L * STEPS + i
                pool.wait_ge(rope_ready, cnt(t, 4, n + 1))
                pool.tensor_tensor(t1[:, n, :, :], t1[:, n, :, :], t2[:, n, :, :], ALU.add).then_inc(rope_sum, 1)

            def unit(t, n):
                pool.wait_ge(inv_step, cnt(t, 2, 2))
                pool.wait_ge(rope_sum, cnt(t, 4, n + 1))
                pool.tensor_tensor(t1[:, n, :, :], t1[:, n, :, :], inv_n[:, 8 * n:8 * n + 8].unsqueeze(2).to_broadcast([P, 8, LD]),
                                   ALU.mult).then_inc(k_unit, 1)

            def normalise(t):
                pool.wait_ge(sum_step, t * 3 + 3)
                for g in range(NG):
                    pool.tensor_tensor(z[:, g, :, :], z[:, g, :, :], inv_s[:, g * HG:g * HG + HG].unsqueeze(2).to_broadcast([P, HG, P]),
                                       ALU.mult).then_inc(p_norm, 1)
                pool.tensor_tensor(z_prev[:, :, :], z_prev[:, :, :],
                                   inv_s[0:WINDOW, :].unsqueeze(2).to_broadcast([WINDOW, LH, WINDOW]), ALU.mult).then_inc(p_norm, 1)

            with pool.Fori(0, DEPTH) as L:
                for n in range(4):
                    add(L, 0, n)
                for n in range(2, 4):
                    unit(L * STEPS, n)
                with pool.Fori(1, NT) as i:
                    for n in range(4):
                        add(L, i, n)
                    for n in range(2, 4):
                        unit(L * STEPS + i, n)
                    normalise(L * STEPS + i - 1)
                normalise(L * STEPS + (NT - 1))

        def half(n):
            return t1[:, n, :, :].rearrange("p h c -> p (h c)")

        @block.tensor
        def _(pe):
            def project(t, par, n):
                if n == 0:
                    pe.wait_ge(x_ready, cnt(t, 2, 2))
                    pe.wait_ge(v_kept, t * 2)
                elif n >= 2:
                    pe.wait_ge(rope_ready, cnt(t, 4, n - 1))
                pe.matmul(p_b[n % 2][:, :], lhsT=xs[par][:, :], rhs=w_qkv[:, n * LANES:n * LANES + LANES], start=True,
                          stop=True).then_inc(proj, 1)

            def turn_qk(t, n, job):
                if n < 2:
                    pe.wait_ge(q_unit, cnt(t, 2, n + 1))
                else:
                    pe.wait_ge(k_unit, cnt(t, 2, n - 1))
                free_bank(job)
                for j in range(4):
                    ins = pe.transpose(t_b[n % 2][:, j * P:j * P + P], half(n)[:, j * P:j * P + P], ident)
                ins.then_inc(qk_turned, 1)

            def free_bank(job):
                if job is not None:
                    pe.wait_ge(kept, job - 1)

            def score(t, par, g):
                if g >= 2:
                    pe.wait_ge(sub_ready, cnt(t, 5, g - 1))
                b = s_b[g % 2]
                for j in range(HG):
                    h = head_of(g, j)
                    lo = (h % 2) * LD
                    pe.matmul(b[:, j * P:j * P + P], lhsT=q_t[lo:lo + LD, h // 2, :], rhs=k_t[par][lo:lo + LD, h // 2, :],
                              start=j == 0, stop=False, skip_group_check=True)
                pe.matmul(b[:, :], lhsT=ident16[:, :], rhs=mask[:, :, :].rearrange("p h c -> p (h c)"), start=False,
                          stop=True, skip_group_check=True).then_inc(scores, 1)

            def add_prev(par, odd):
                lo = odd * LD
                for g in (odd, 2 + odd):
                    for j in range(HG):
                        c = (g * HG + j) * WINDOW
                        h = head_of(g, j)
                        ins = pe.matmul(s_b[2][0:WINDOW, c:c + WINDOW], lhsT=q_t[lo:lo + LD, h // 2, 0:WINDOW],
                                        rhs=k_t[1 - par][lo:lo + LD, h // 2, P - WINDOW:P], start=c == 0, stop=False,
                                        skip_group_check=True)
                return ins

            def first_scores(t, par, masks, jobs):
                pe.wait_ge(kept, jobs)
                if par == 0:
                    pe.wait_ge(mask_ready, masks)
                pe.wait_ge(sub_ready, t * 5)
                score(t, par, 0)
                add_prev(par, 0).then_inc(even_done, 1)
                pe.wait_ge(even_done, t + 1)
                score(t, par, 1)
                add_prev(par, 1)
                m = mask_now if par == 0 else mask_prev
                pe.matmul(s_b[2][0:WINDOW, :], lhsT=ident16[0:WINDOW, 0:WINDOW], rhs=m[:, :, :].rearrange("p h c -> p (h c)"),
                          start=False, stop=True, skip_group_check=True).then_inc(scores, 1)

            def turn_probs(t, n, job):
                if n == NG - 1:
                    pe.wait_ge(x1_ready, t)
                    pe.wait_ge(p_norm, t * 5 + 5)
                else:
                    pe.wait_ge(p_norm, cnt(t, 5, n + 1))
                free_bank(job)
                for j in range(HG):
                    ins = pe.transpose(t_b[n % 2][:, j * P:j * P + P], z[:, n, j, :], ident)
                ins.then_inc(p_turned, 1)
                if n == NG - 1:
                    zp = z_prev[:, :, :].rearrange("p (g j) c -> p g (j c)", j=HG)
                    for g in range(NG):
                        ins = pe.transpose(w_b[:, P + g * WINDOW:P + (g + 1) * WINDOW], zp[:, g, :], ident[0:WINDOW, 0:WINDOW])
                    ins.then_inc(pp_turned, 1)

            def attend(t, par, n, landed, job):
                if n == 0:
                    pe.wait_ge(pp_kept, t + 1)
                    pe.wait_ge(v_kept, cnt(t, 2, 2))
                    pe.wait_ge(vp_landed[par], landed)
                pe.wait_ge(kept, job)
                for p in range(8 * n, 8 * n + 8):
                    g, j = p // HG, p % HG
                    lo, c = p % 2 * LD, (p - 8 * n) // 2 * P
                    pe.matmul(t_b[n][lo:lo + LD, c:c + WINDOW], lhsT=v_prev[par][:, g, j, :], rhs=pt_prev[:, g, :],
                              start=p < 8 * n + 2, stop=False, skip_group_check=True)
                    ins = pe.matmul(t_b[n][lo:lo + LD, c:c + P], lhsT=v[par][:, p, :], rhs=pt[:, g, j, :], start=False, stop=True,
                                    skip_group_check=True)
                ins.then_inc(attended, 1)

            def project_out(t, jobs):
                pe.wait_ge(kept, jobs)
                pe.wait_ge(x1_ready, t)
                for j in range(INNER // P):
                    ins = pe.matmul(w_b[:, 0:P], lhsT=w_o[:, j, :], rhs=att_t[:, j, :], start=j == 0, stop=j == INNER // P - 1)
                ins.then_inc(o_mm, 1)

            def step(L, i, par, has_c, has_a, landed_c, even, job):
                t = L * STEPS + i
                if has_a:
                    project(t + 1, 1 - par, 0)
                    project(t + 1, 1 - par, 1)
                first_scores(t, par, even, job)
                if has_c:
                    for n in range(NG):
                        turn_probs(t - 1, n, job + n)
                if has_a:
                    project(t + 1, 1 - par, 2)
                    project(t + 1, 1 - par, 3)
                score(t, par, 2)
                if has_c:
                    attend(t - 1, 1 - par, 0, landed_c, job + 4)
                score(t, par, 3)
                if has_c:
                    attend(t - 1, 1 - par, 1, landed_c, job + 4)
                if has_a:
                    project(t + 1, 1 - par, 4)
                    project(t + 1, 1 - par, 5)
                if has_c:
                    project_out(t - 1, job + 6)
                if has_a:
                    for n in range(4):
                        turn_qk(t + 1, n, job + (6 if has_c else 0) + n)

            with pe.Fori(0, DEPTH) as L:
                pe.wait_ge(qkv_loaded, L * QKV_LOADS + QKV_LOADS)
                job = L * LAYER_JOBS
                for n in range(6):
                    project(L * STEPS, 0, n)
                for n in range(4):
                    turn_qk(L * STEPS, n, job + n if n >= 2 else None)

                step(L, 0, 0, False, True, None, L * NT + 2, job + 4)
                with pe.Fori(0, NT // 2 - 1) as g:
                    step(L, g * 2 + 1, 1, True, True, L * (64 * (NT // 2 - 1)) + g * 64, None,
                         L * LAYER_JOBS + (g * (2 * TILE_JOBS) + 8))
                    step(L, g * 2 + 2, 0, True, True, L * (64 * (NT // 2)) + (g * 64 + 64), L * NT + (g * 2 + 4),
                         L * LAYER_JOBS + (g * (2 * TILE_JOBS) + 8 + TILE_JOBS))
                step(L, NT - 1, 1, True, False, L * (64 * (NT // 2 - 1)) + 64 * (NT // 2 - 1), None, job + (LAYER_JOBS - 12))
                t_last, job = L * STEPS + (NT - 1), L * LAYER_JOBS + (LAYER_JOBS - 6)
                for n in range(NG):
                    turn_probs(t_last, n, job + n)
                for n in range(2):
                    attend(t_last, 1, n, L * (64 * (NT // 2)) + 64 * (NT // 2), job + 4)
                project_out(t_last, job + 6)

                with pe.Fori(0, CHUNKS // 2) as g:
                    n = L * CHUNKS + g * 2
                    for s in range(2):
                        pe.wait_ge(f_x, n + (s + 1))
                        pe.wait_ge(f_cent, n)
                        pe.matmul(p_b[s][:, :], lhsT=mean_w, rhs=fx[s], start=True, stop=True).then_inc(f_mean, 1)
                    for s in range(2):
                        pe.wait_ge(f_sq, n + (s + 1))
                        pe.wait_ge(f_log, n)
                        pe.matmul(t_b[s][:, :], lhsT=mean_w, rhs=fq[s], start=True, stop=True).then_inc(f_var, 1)

                def feed(c, s):
                    n = L * CHUNKS + c
                    pe.wait_ge(ffn_loaded, L * FFN_LOADS + FFN_LOADS)
                    pe.wait_ge(f_norm, L * (CHUNKS * 2) + CHUNKS * 2)
                    x = X[:, bass.ds(c * CH, CH)]
                    for m, (lo, size) in enumerate(FF_BLOCKS):
                        pe.wait_ge(f_gelu, n * 3 + max(m - 1, 0))
                        pe.matmul(s_b[m % 2][0:size, :], lhsT=w_1[:, FFI + lo:FFI + lo + size], rhs=x, start=True,
                                  stop=True).then_inc(f_gate, 1)
                        pe.wait_ge(f_prod, n * 3 + max(m - 1, 0))
                        pe.matmul(p_b[m % 2][0:size, :], lhsT=w_1[:, lo:lo + size], rhs=x, start=True, stop=True).then_inc(f_lin, 1)
                    pe.wait_ge(f_done, n)
                    for m, (lo, size) in enumerate(FF_BLOCKS):
                        pe.wait_ge(f_prod, n * 3 + m + 1)
                        ins = pe.matmul(t_b[s][:, :], lhsT=w_2[0:size, m, :], rhs=hh[m][0:size, :], start=m == 0, stop=m == 2)
                    ins.then_inc(f_out, 1)

                with pe.Fori(0, CHUNKS // 2) as g:
                    feed(g * 2, 0)
                    feed(g * 2 + 1, 1)

        @block.scalar
        def _(act):
            def take(L, i, par, first=False):
                t = L * STEPS + i
                if first:
                    act.wait_ge(f_done, L * CHUNKS)
                act.wait_ge(proj, t * 6 if first else cnt(t, 6, -6))
                act.activation(xs[par][0:64, :], X[0:64, bass.ds(i * P, P)], ACT.Copy)
                act.activation(xs[par][64:P, :], Xp[64:P, bass.ds(i * P, P)], ACT.Copy).then_inc(x_ready, 1)
                act.wait_ge(x_ready, cnt(t, 2, 1))
                act.activation(xs[par][64:P, 0:1], xs[par][64:P, 0:1], ACT.Identity, scale=shown[64:P, bass.ds(i, 1)]).then_inc(x_ready, 1)

            def mask_for(L, i):
                act.wait_ge(scores, cnt(L * STEPS + i, 5, -5))
                act.activation(mask_now[:, :, :], mask_prev[:, :, :], ACT.Identity, bias=hidden[0:WINDOW, bass.ds(i, 1)]).then_inc(mask_ready, 1)

            def keys_for(L, i):
                act.wait_ge(scores, cnt(L * STEPS + i, 5, 0))
                before = k_t[1][:, :, P - WINDOW:P]
                act.activation(before, before, ACT.Identity, scale=shown[:, bass.ds(i, 1)]).then_inc(mask_ready, 1)

            def square(t, n):
                act.wait_ge(proj, cnt(t, 6, n + 1))
                act.wait_ge(ssq_step, cnt(t, 5, max(n - 1, 0)))
                act.activation(sq[:, n % 2, :, :].rearrange("p h c -> p (h c)"), p_b[n % 2][:, :], ACT.Square).then_inc(sq_ready, 1)

            def values(t, par, n, landed=None):
                if landed is not None:
                    act.wait_ge(vp_landed[1 - par], landed)
                act.wait_ge(proj, cnt(t, 6, n + 5))
                act.activation(v[par][:, 8 * n:8 * n + 8, 0:LD], p_b[n % 2][:, :].rearrange("p (h c) -> p h c", c=LD),
                               ACT.Copy).then_inc(v_kept, 1)

            def inverse_norms(t):
                act.wait_ge(ssq_step, cnt(t, 5, 5))
                act.activation(ssq_l[:, :], ssq_c[:, :], ACT.Ln, scale=NORM_SCALE).then_inc(inv_step, 1)
                act.wait_ge(inv_step, cnt(t, 2, 1))
                act.activation(inv_n[:, :], ssq_l[:, :], ACT.Exp, scale=-0.5, bias=norm_bias[:, 0:1]).then_inc(inv_step, 1)

            def keep_qk(t, par, n):
                act.wait_ge(qk_turned, cnt(t, 4, n + 1))
                dst = (q_t if n < 2 else k_t[par])[:, 4 * (n % 2):4 * (n % 2) + 4, :]
                act.activation(dst.rearrange("p j c -> p (j c)"), t_b[n % 2][:, :], ACT.Copy).then_inc(kept, 1)

            def exps(t, n):
                act.wait_ge(sub_ready, cnt(t, 5, n + 1))
                for j in range(HG):
                    p = n * HG + j
                    ins = act.activation(z[:, n, j, :], z[:, n, j, :], ACT.Exp, scale=QK_SCALE, accum_out=sums[:, p:p + 1])
                ins.then_inc(exp_ready, 1)

            def exps_prev(t):
                act.wait_ge(sub_ready, cnt(t, 5, 5))
                e = z_prev[:, :, :].rearrange("p h c -> p (h c)")
                act.activation(e, e, ACT.Exp, scale=QK_SCALE).then_inc(exp_ready, 1)

            def keep_probs(t, n):
                act.wait_ge(p_turned, cnt(t, 4, n + 1))
                act.activation(pt[:, n, :, :].rearrange("p h c -> p (h c)"), t_b[n % 2][:, :], ACT.Copy).then_inc(kept, 1)

            def keep_prev_probs(t):
                act.wait_ge(pp_turned, t + 1)
                act.activation(pt_prev[:, :, :], w_b[:, P:2 * P].rearrange("p (g c) -> p g c", c=WINDOW), ACT.Copy).then_inc(pp_kept, 1)

            def keep_attended(t, n):
                act.wait_ge(attended, cnt(t, 2, n + 1))
                act.activation(att_t[:, 4 * n:4 * n + 4, :].rearrange("p j c -> p (j c)"), t_b[n][:, :], ACT.Copy).then_inc(kept, 1)

            def step(L, i, par, has_c, has_a, takes, landed):
                t = L * STEPS + i
                if has_a:
                    square(t + 1, 0)
                    square(t + 1, 1)
                if has_c:
                    for n in range(NG):
                        keep_probs(t - 1, n)
                    keep_prev_probs(t - 1)
                if has_a:
                    square(t + 1, 2)
                    square(t + 1, 3)
                exps(t, 0)
                exps(t, 1)
                if has_c:
                    keep_attended(t - 1, 0)
                if takes:
                    take(L, i + 2, par)
                if has_a:
                    if par == 1:
                        mask_for(L, i + 1)
                    inverse_norms(t + 1)
                exps(t, 2)
                if has_c:
                    keep_attended(t - 1, 1)
                exps(t, 3)
                exps_prev(t)
                if has_a:
                    for n in range(2):
                        keep_qk(t + 1, 1 - par, n)
                    values(t + 1, 1 - par, 0, landed)
                    values(t + 1, 1 - par, 1)
                    for n in range(2, 4):
                        keep_qk(t + 1, 1 - par, n)
                    if par == 1:
                        keys_for(L, i + 1)

            act.preload_act_table_set("natural_log_exp_and_others")
            with act.Fori(0, DEPTH) as L:
                act.preload_act_table_set("natural_log_exp_and_others")
                t = L * STEPS
                take(L, 0, 0, first=True)
                act.wait_ge(f_done, L * CHUNKS)
                act.activation(mask_now[:, :, :], mask_prev[:, :, :], ACT.Identity, bias=hidden[0:WINDOW, 0:1]).then_inc(mask_ready, 1)
                keys_for(L, 0)
                take(L, 1, 1)
                for n in range(4):
                    square(t, n)
                for n in range(2):
                    values(t, 0, n)
                inverse_norms(t)
                for n in range(4):
                    keep_qk(t, 0, n)
                odd, even = L * (64 * (NT // 2)), L * (64 * (NT // 2 - 1))
                step(L, 0, 0, False, True, True, None)
                with act.Fori(0, NT // 2 - 2) as g:
                    step(L, g * 2 + 1, 1, True, True, True, odd + (g * 64 + 64))
                    step(L, g * 2 + 2, 0, True, True, True, even + (g * 64 + 64))
                step(L, NT - 3, 1, True, True, True, odd + 64 * (NT // 2 - 1))
                step(L, NT - 2, 0, True, True, False, even + 64 * (NT // 2 - 1))
                step(L, NT - 1, 1, True, False, False, None)
                t_last = L * STEPS + (NT - 1)
                for n in range(NG):
                    keep_probs(t_last, n)
                keep_prev_probs(t_last)
                for n in range(2):
                    keep_attended(t_last, n)
                act.wait_ge(x1_ready, L * STEPS + STEPS)

                def shifted(c):
                    n = L * CHUNKS + c
                    for s in range(2):
                        act.wait_ge(f_cent, n)
                        act.activation(fx[s][0:64, :], X1[0:64, bass.ds((c + s) * CH, CH)], ACT.Copy)
                        act.activation(fx[s][64:P, :], X1p[64:P, bass.ds((c + s) * CH, CH)], ACT.Copy).then_inc(b_step, 1)
                    for s in range(2):
                        act.wait_ge(b_step, n + (s + 1))
                        act.activation(fx[s][64:P, 0:1], fx[s][64:P, 0:1], ACT.Identity,
                                       scale=shown[64:P, bass.ds((c + s) * 4, 1)]).then_inc(f_x, 1)

                def norm_pair(c, last):
                    n = L * CHUNKS + c
                    for s in range(2):
                        act.wait_ge(f_cent, n + (s + 1))
                        act.activation(fq[s], fc[s], ACT.Square).then_inc(f_sq, 1)
                    if not last:
                        shifted(c + 2)
                    for s in range(2):
                        act.wait_ge(f_var, n + (s + 1))
                        act.activation(fl[s], t_b[s][:, :], ACT.Ln, bias=eps).then_inc(f_log, 1)
                    for s in range(2):
                        act.wait_ge(f_log, n + (s + 1))
                        act.wait_ge(f_norm, n * 2)
                        act.activation(fr[s], fl[s], ACT.Exp, scale=-0.5).then_inc(f_rstd, 1)

                shifted(0)
                with act.Fori(0, CHUNKS // 2 - 1) as g:
                    norm_pair(g * 2, False)
                norm_pair(CHUNKS - 2, True)

                def feed(c, s):
                    n = L * CHUNKS + c
                    for m, (lo, size) in enumerate(FF_BLOCKS):
                        act.wait_ge(f_gate, n * 3 + m + 1)
                        act.wait_ge(f_prod, n * 3 + max(m - 1, 0))
                        act.activation(gl[m % 2][0:size, :], s_b[m % 2][0:size, :], ACT.Gelu, bias=b_1[0:size, 3 + m:4 + m]).then_inc(f_gelu, 1)

                act.preload_act_table(ACT.Gelu)
                with act.Fori(0, CHUNKS // 2) as g:
                    feed(g * 2, 0)
                    feed(g * 2 + 1, 1)

        @block.vector
        def _(dve):
            def rope(t, i8, n):
                dve.wait_ge(sq_ready, cnt(t, 4, n + 1))
                x = p_b[n % 2][:, :].rearrange("p (h c) -> p h c", c=LD)
                which = 0 if n < 2 else 2
                cos = table[:, bass.ds(i8, 1), which, :].to_broadcast([P, 8, LD])
                sin = table[:, bass.ds(i8, 1), which + 1, :]
                dve.tensor_tensor(t1[:, n, :, :], x, cos, ALU.mult)
                H = LD // 2
                dve.tensor_tensor(t2[:, n, :, 0:H], x[:, :, H:LD], sin[:, :, 0:H].to_broadcast([P, 8, H]), ALU.mult)
                dve.tensor_tensor(t2[:, n, :, H:LD], x[:, :, 0:H], sin[:, :, H:LD].to_broadcast([P, 8, H]), ALU.mult).then_inc(rope_ready, 1)

            def square_sum(t, n):
                dve.tensor_reduce(ssq[:, 8 * n:8 * n + 8], sq[:, n % 2, :, :], AX.X, ALU.add).then_inc(ssq_step, 1)

            def guard(t):
                dve.wait_ge(ssq_step, cnt(t, 5, 4))
                dve.tensor_scalar(ssq_c[:, :], ssq[:, :], 1e-24, None, ALU.max).then_inc(ssq_step, 1)

            def unit(t, n):
                if n == 0:
                    dve.wait_ge(inv_step, cnt(t, 2, 2))
                dve.wait_ge(rope_sum, cnt(t, 4, n + 1))
                dve.tensor_tensor(t1[:, n, :, :], t1[:, n, :, :], inv_n[:, 8 * n:8 * n + 8].unsqueeze(2).to_broadcast([P, 8, LD]),
                                  ALU.mult).then_inc(q_unit, 1)

            def max_prev(t):
                dve.wait_ge(scores, cnt(t, 5, 3))
                dve.tensor_reduce(top_prev[:, :], s_b[2][0:WINDOW, :].rearrange("p (h c) -> p h c", c=WINDOW), AX.X,
                                  ALU.max).then_inc(max_step, 1)

            def less_max(t, g, prior):
                dve.wait_ge(scores, cnt(t, 5, g + 2 if g >= 2 else g + 1))
                if prior:
                    dve.wait_ge(p_turned, cnt(t - 1, 4, g + 1))
                s = s_b[g % 2][:, :].rearrange("p (h c) -> p h c", c=P)
                hs = slice(g * HG, g * HG + HG)
                dve.tensor_reduce(top[:, hs], s, AX.X, ALU.max).then_inc(max_step, 1)
                dve.wait_ge(max_step, cnt(t, 9, 2 + 2 * g))
                dve.tensor_tensor(top[0:WINDOW, hs], top[0:WINDOW, hs], top_prev[:, hs], ALU.max).then_inc(max_step, 1)
                dve.wait_ge(max_step, cnt(t, 9, 3 + 2 * g))
                dve.tensor_tensor(z[:, g, :, :], s, top[:, hs].unsqueeze(2).to_broadcast([P, HG, P]), ALU.subtract).then_inc(sub_ready, 1)

            def less_max_prev(t):
                dve.wait_ge(pp_turned, t)
                s = s_b[2][0:WINDOW, :].rearrange("p (h c) -> p h c", c=WINDOW)
                dve.tensor_tensor(z_prev[:, :, :], s, top[0:WINDOW, :].unsqueeze(2).to_broadcast([WINDOW, LH, WINDOW]),
                                  ALU.subtract).then_inc(sub_ready, 1)

            def inverse_sums(t):
                dve.wait_ge(exp_ready, t * 5 + 5)
                dve.tensor_reduce(sums_prev[:, :], z_prev[:, :, :], AX.X, ALU.add).then_inc(sum_step, 1)
                dve.wait_ge(sum_step, cnt(t, 3, 1))
                dve.tensor_tensor(sums[0:WINDOW, :], sums[0:WINDOW, :], sums_prev[:, :], ALU.add).then_inc(sum_step, 1)
                dve.wait_ge(sum_step, cnt(t, 3, 2))
                dve.reciprocal(inv_s[:, :], sums[:, :]).then_inc(sum_step, 1)

            def add_x(L, i):
                t = L * STEPS + i
                dve.wait_ge(o_mm, t + 1)
                dve.tensor_tensor(X1[:, bass.ds(i * P, P)], X[:, bass.ds(i * P, P)], w_b[:, 0:P], ALU.add).then_inc(x1_ready, 1)

            def step(L, i, has_c, has_a):
                t = L * STEPS + i
                i8 = (i + 1) % TILES
                if has_a:
                    for n in range(2):
                        rope(t + 1, i8, n)
                        square_sum(t + 1, n)
                max_prev(t)
                less_max(t, 0, has_c)
                less_max(t, 1, has_c)
                if has_a:
                    for n in range(2, 4):
                        rope(t + 1, i8, n)
                        square_sum(t + 1, n)
                    guard(t + 1)
                less_max(t, 2, has_c)
                less_max(t, 3, has_c)
                less_max_prev(t)
                if has_a:
                    for n in range(2):
                        unit(t + 1, n)
                inverse_sums(t)
                if has_c:
                    add_x(L, i - 1)

            with dve.Fori(0, DEPTH) as L:
                dve.wait_ge(qkv_loaded, L * QKV_LOADS + QKV_LOADS)
                dve.wait_ge(f_done, L * CHUNKS)
                for k in range(4):
                    ins = dve.tensor_tensor(table[:, :, k, :], base[:, :, k, :], qk_scale[:, k, :].unsqueeze(1).to_broadcast([P, TILES, LD]),
                                            ALU.mult)
                ins.then_inc(table_step, 1)
                dve.wait_ge(table_step, L + 3)
                t = L * STEPS
                for n in range(4):
                    rope(t, 0, n)
                    square_sum(t, n)
                guard(t)
                for n in range(2):
                    unit(t, n)
                step(L, 0, False, True)
                with dve.Fori(0, NT // 2 - 1) as g:
                    step(L, g * 2 + 1, True, True)
                    step(L, g * 2 + 2, True, True)
                step(L, NT - 1, True, False)
                add_x(L, NT - 1)

                with dve.Fori(0, CHUNKS // 2) as g:
                    n = L * CHUNKS + g * 2
                    dve.wait_ge(ffn_loaded, L * FFN_LOADS + FFN_LOADS)
                    for s in range(2):
                        dve.wait_ge(f_mean, n + (s + 1))
                        dve.wait_ge(f_sq, n)
                        dve.tensor_tensor(fc[s], fx[s], p_b[s][:, :], ALU.subtract).then_inc(f_cent, 1)
                    for s in range(2):
                        dve.wait_ge(f_rstd, n + (s + 1))
                        dve.tensor_tensor(fn[s], fc[s], fr[s], ALU.mult).then_inc(f_norm, 1)
                    for s in range(2):
                        dve.wait_ge(f_norm, n * 2 + (s + 1))
                        dve.tensor_scalar(X[:, bass.ds((g * 2 + s) * CH, CH)], fn[s], vec[:, 0:1], vec[:, 1:2], ALU.mult,
                                          ALU.add).then_inc(f_norm, 1)

                def feed(c, s):
                    n = L * CHUNKS + c
                    for m, (lo, size) in enumerate(FF_BLOCKS):
                        dve.wait_ge(f_lin, n * 3 + m + 1)
                        dve.wait_ge(f_gelu, n * 3 + m + 1)
                        if m == 0:
                            dve.wait_ge(f_out, n)
                        dve.scalar_tensor_tensor(hh[m][0:size, :], p_b[m % 2][0:size, :], b_1[0:size, m:m + 1], gl[m % 2][0:size, :],
                                                 ALU.add, ALU.mult).then_inc(f_prod, 1)
                    dve.wait_ge(f_out, n + 1)
                    dve.scalar_tensor_tensor(X[:, bass.ds(c * CH, CH)], t_b[s][:, :], vec[:, 2:3], X1[:, bass.ds(c * CH, CH)], ALU.add,
                                             ALU.add).then_inc(f_done, 1)

                with dve.Fori(0, CHUNKS // 2) as g:
                    feed(g * 2, 0)
                    feed(g * 2 + 1, 1)

        layers.close()

        landed = [sem(f"d_x_landed{i}") for i in range(2)]
        e_sum = sem("d_end_sum_ready")
        e_ln = Norm(sem, "d_end_ln")
        e_done = sem("d_end_done")
        with nc.Block() as block:
            @block.sync
            def _(sp):
                for c in range(CHUNKS):
                    if c >= 2:
                        sp.wait_ge(e_sum, c - 1)
                    sp.dma_start(fx[c % 2], kept_x[:, c * CH:c * CH + CH]).then_inc(landed[c % 2], 16)

            @block.tensor
            def _(pe):
                for c in range(CHUNKS):
                    pe.wait_ge(e_sum, c + 1)
                    norm_pe(pe, e_ln, c, mean_w, X[:, c * CH:c * CH + CH], fq[0], p_b[0][:, :], p_b[1][:, :])

            @block.scalar
            def _(act):
                for c in range(CHUNKS):
                    norm_act(act, e_ln, c, fc[0], fq[0], p_b[1][:, :], fl[0], eps)

            @block.vector
            def _(dve):
                for c in range(CHUNKS):
                    x = X[:, c * CH:c * CH + CH]
                    dve.wait_ge(landed[c % 2], 16 * (c // 2) + 16)
                    dve.tensor_tensor(x, x, fx[c % 2], ALU.add).then_inc(e_sum, 1)
                    dve.wait_ge(e_sum, c + 1)
                    norm_dve(dve, e_ln, c, x, fc[0], fl[0], fr[0], p_b[0][:, :])
                    dve.tensor_tensor(x, fc[0], fr[0], ALU.mult).then_inc(e_done, 1)


def build(nc, d, out):
    with ExitStack() as ctx:
        def sem(label):
            return ctx.enter_context(nc.semaphore(label))

        Xp = ctx.enter_context(nc.sbuf_tensor("X", [P, 1 + TOKENS], F32))
        X1p = ctx.enter_context(nc.sbuf_tensor("X1", [P, 1 + TOKENS], F32))
        X, X1 = Xp[:, 1:], X1p[:, 1:]
        ident = ctx.enter_context(nc.sbuf_tensor("ident", [P, P], F32))
        mean_w = ctx.enter_context(nc.sbuf_tensor("mean_weights", [P, P], F32))
        eps = ctx.enter_context(nc.sbuf_tensor("eps", [P, 1], F32))
        const_step = sem("const_step")
        with nc.Block() as block:
            @block.gpsimd
            def _(pool):
                pool.memset(mean_w[:, :], 1.0 / DIM)
                pool.memset(eps[:, :], EPS)
                pool.memset(ident[:, :], 0.0).then_inc(const_step, 1)
                pool.wait_ge(const_step, 1)
                pool.affine_select(out=ident[:, :], in_=ident[:, :], pattern=[[-1, P]], compare_op=ALU.not_equal, fill=1.0,
                                   base=0, channel_multiplier=1)
        consts = (ident[:, :], mean_w[:, :], eps[:, 0:1])
        def stage_sem(label):
            return nc.alloc_semaphore(name=label)

        with nc.cleanup_on_exit():
            load_tokens(nc, stage_sem, d["x"], X, ident[:, :])
        with nc.cleanup_on_exit():
            mamba(nc, stage_sem, "a", X, X1, dict(in_proj=d["a_in_proj"], conv=d["a_conv"], x_proj=d["a_x_proj"], dt=d["a_dt"],
                                                  out_proj=d["a_out_proj"], vectors=d["a_vectors"]), consts)
        with nc.cleanup_on_exit():
            experts(nc, stage_sem, X, d, consts)
        with nc.cleanup_on_exit():
            mqa(nc, stage_sem, X, X1, d, consts)
        with nc.cleanup_on_exit():
            mamba(nc, stage_sem, "c", X, X1, dict(in_proj=d["c_w_in"], taps=d["c_conv_w"], x_proj=d["c_w_xproj"], dt=d["c_w_dt"],
                                                  out_proj=d["c_w_out"], vectors=d["c_vectors"], a_log=d["c_a_log"]), consts)
        with nc.cleanup_on_exit():
            local_layers(nc, stage_sem, Xp, X1p, d, consts)
    with nc.cleanup_on_exit():
        store_tokens(nc, stage_sem, out, X, ident[:, :])


def layout(i):
    def t(a):
        return np.ascontiguousarray(np.transpose(a))

    def cols(*vs):
        parts = [v.reshape(-1, P).T for v in vs]
        n = sum(p.shape[1] for p in parts)
        parts.append(np.zeros((P, 8 - n), np.float32))
        return np.ascontiguousarray(np.concatenate(parts, axis=1))

    swap = np.concatenate([np.arange(LD // 2, LD), np.arange(LD // 2)])
    q, k = i["L1_ffn_q_scale"], i["L1_ffn_k_scale"]
    scales = np.broadcast_to(np.stack([q, q[:, swap], k, k[:, swap]], axis=1)[:, None], (DEPTH, P, 4, LD))
    b1 = np.zeros((DEPTH, P, 6), np.float32)
    for m, (lo, size) in enumerate(FF_BLOCKS):
        b1[:, :size, m] = i["L1_ffn_b1"][:, lo:lo + size]
        b1[:, :size, 3 + m] = i["L1_ffn_b1"][:, FFI + lo:FFI + lo + size]
    wqkv = i["L1_ffn_Wqkv"].reshape(DEPTH, DIM, 3, LH, LD).copy()
    wqkv[:, :, 2] = wqkv[:, :, 2][:, :, PLACES]
    wo = i["L1_ffn_Wo"].reshape(DEPTH, LH, LD, DIM)[:, PLACES].reshape(DEPTH, INNER, DIM)
    return {
        "x": i["L0_attn_x"],
        "a_in_proj": t(i["L0_attn_in_proj_w"]),
        "a_conv": np.ascontiguousarray(np.transpose(i["L0_attn_conv_w"], (2, 1, 0))),
        "a_x_proj": t(i["L0_attn_x_proj_w"]),
        "a_dt": t(i["L0_attn_dt_w"]),
        "a_out_proj": t(i["L0_attn_out_proj_w"]),
        "a_vectors": cols(i["L0_attn_conv_b"], i["L0_attn_dt_b"], i["L0_attn_norm_w"], i["L0_attn_norm_b"]),
        "b_gate": np.ascontiguousarray(np.concatenate([i["L0_ffn_Wg"], i["L0_ffn_Wt"]], axis=1)),
        "b_gate_bias": np.ascontiguousarray(np.broadcast_to(np.concatenate([i["L0_ffn_bg"], i["L0_ffn_bt"]]), (P, 9))),
        "b_w1": i["L0_ffn_W1"],
        "b_b1": np.ascontiguousarray(i["L0_ffn_b1"].reshape(8, 4, P).transpose(2, 0, 1).reshape(P, 32)),
        "b_w2": i["L0_ffn_W2"],
        "b_b2": i["L0_ffn_b2"],
        "q_wqkv": i["L1_attn_wqkv"],
        "q_bias": np.ascontiguousarray(i["L1_attn_bqkv"].reshape(-1, 1)),
        "q_value_bias": np.ascontiguousarray(np.broadcast_to(i["L1_attn_bqkv"][DIM + HD:], (P, HD))),
        "q_key_pick": np.ascontiguousarray(np.repeat(np.array([[k == p for p in range(3)] for k in K_PART], np.float32), HD, axis=0)),
        "q_w_out": i["L1_attn_w_attn_out"],
        "q_b_out": np.ascontiguousarray(i["L1_attn_b_attn_out"].reshape(-1, 1)),
        "c_w_in": i["L1_attn_w_in"],
        "c_conv_w": i["L1_attn_conv_w"],
        "c_w_xproj": i["L1_attn_w_xproj"],
        "c_w_dt": i["L1_attn_w_dt"],
        "c_w_out": i["L1_attn_w_out"],
        "c_a_log": i["L1_attn_A_log"],
        "c_vectors": cols(i["L1_attn_conv_b"], i["L1_attn_b_dt"], np.zeros(2 * P, np.float32), i["L1_attn_Dp"]),
        "d_wqkv": wqkv.reshape(DEPTH, DIM, 3 * INNER),
        "d_wo": wo,
        "d_w1": i["L1_ffn_W1"],
        "d_w2": i["L1_ffn_W2"],
        "d_scales": scales,
        "d_b1": b1,
        "d_ln": np.ascontiguousarray(np.stack([i["L1_ffn_ln_g"], i["L1_ffn_ln_b"], i["L1_ffn_b2"]], axis=2)),
    }


def kernel(**inputs):
    import numpy as _np
    import concourse.bacc as _bacc
    from concourse import mybir as _mybir
    from concourse.bass_utils import run_bass_kernel_spmd as _run

    nc = _bacc.Bacc("TRN2", target_bir_lowering=False, num_devices=1)
    arrays, aps = {}, {}
    for name, a in layout({k: _np.asarray(v) for k, v in inputs.items()}).items():
        a = _np.ascontiguousarray(a)
        arrays[f"in_{name}"] = a
        aps[name] = nc.dram_tensor(f"in_{name}", a.shape, _mybir.dt.from_np(a.dtype), kind="ExternalInput").ap()
    out = nc.dram_tensor("out_0", (BATCH, SEQ, DIM), F32, kind="ExternalOutput").ap()
    build(nc, aps, out)
    r = _run(nc, [arrays], core_ids=[0])
    return r.results[0]["out_0"]
```

```python
from contextlib import ExitStack

import concourse.bass as bass
import numpy as np
from concourse import mybir

F32 = mybir.dt.float32
BF16 = mybir.dt.bfloat16
ALU = mybir.AluOpType
ACT = mybir.ActivationFunctionType
AX = mybir.AxisListType

P = 128
DIM = 128
BATCH = 4
SEQ = 1024
TOKENS = BATCH * SEQ
CH = 512
HALVES = SEQ // CH
NT = TOKENS // P
D_INNER = 256
DB = D_INNER // P
STATES = 16
TAPS = 4
EPS = 1e-5
LOG1P_DEGREE = 10


def log1p_coefficients():
    fit = np.polynomial.chebyshev.Chebyshev.interpolate(lambda x: np.log1p(x + 1e-12) / (x + 1e-12), LOG1P_DEGREE, domain=[0, 1])
    return [float(c) for c in fit.convert(kind=np.polynomial.Polynomial).coef]


class Norm:

    def __init__(self, sem, name):
        self.mean = sem(f"{name}_mean_ready")
        self.cent = sem(f"{name}_centred_ready")
        self.sq = sem(f"{name}_squares_ready")
        self.var = sem(f"{name}_variance_ready")
        self.std = sem(f"{name}_std_ready")
        self.rstd = sem(f"{name}_rstd_ready")


def norm_mean(pe, ln, mean_w, x, mean_bank):
    pe.matmul(mean_bank, lhsT=mean_w, rhs=x, start=True, stop=True).then_inc(ln.mean, 1)


def norm_var(pe, ln, n, mean_w, cent_sq, var_bank):
    pe.wait_ge(ln.sq, n + 1)
    pe.matmul(var_bank, lhsT=mean_w, rhs=cent_sq, start=True, stop=True).then_inc(ln.var, 1)


def norm_pe(pe, ln, n, mean_w, x, cent_sq, mean_bank, var_bank):
    norm_mean(pe, ln, mean_w, x, mean_bank)
    norm_var(pe, ln, n, mean_w, cent_sq, var_bank)


def norm_squares(act, ln, n, cent, cent_sq):
    act.wait_ge(ln.cent, n + 1)
    act.activation(cent_sq, cent, ACT.Square).then_inc(ln.sq, 1)


def norm_std(act, ln, n, var_bank, std, eps):
    act.wait_ge(ln.var, n + 1)
    act.activation(std, var_bank, ACT.Sqrt, bias=eps).then_inc(ln.std, 1)


def norm_act(act, ln, n, cent, cent_sq, var_bank, std, eps):
    norm_squares(act, ln, n, cent, cent_sq)
    norm_std(act, ln, n, var_bank, std, eps)


def norm_centre(dve, ln, n, x, cent, mean_bank):
    dve.wait_ge(ln.mean, n + 1)
    dve.tensor_tensor(cent, x, mean_bank, ALU.subtract).then_inc(ln.cent, 1)


def norm_inverse(dve, ln, n, std, rstd):
    dve.wait_ge(ln.std, n + 1)
    dve.reciprocal(rstd, std).then_inc(ln.rstd, 1)
    dve.wait_ge(ln.rstd, n + 1)


def norm_dve(dve, ln, n, x, cent, std, rstd, mean_bank):
    norm_centre(dve, ln, n, x, cent, mean_bank)
    norm_inverse(dve, ln, n, std, rstd)


def load_tokens(nc, sem, x_dram, X, ident):
    with ExitStack() as mem:
        raw = mem.enter_context(nc.sbuf_tensor("raw_tokens", [P, NT, DIM], F32))
        bank = [mem.enter_context(nc.psum_tensor(f"load_bank{i}", [P, CH], F32)) for i in range(2)]
        landed = [sem(f"tokens_landed{b}") for b in range(BATCH)]
        turned = sem("tokens_turned")
        kept = sem("tokens_kept")
        per = CH // P
        block = mem.enter_context(nc.Block())

        @block.sync
        def _(sp):
            for b in range(BATCH):
                sp.dma_start(raw[:, b * 8:b * 8 + 8, :], x_dram[b].rearrange("(t p) d -> p t d", p=P)).then_inc(landed[b], 16)

        @block.tensor
        def _(pe):
            for g in range(NT // per):
                if g % 2 == 0:
                    pe.wait_ge(landed[g // 2], 16)
                if g >= 2:
                    pe.wait_ge(kept, g - 1)
                for j in range(per):
                    ins = pe.transpose(bank[g % 2][:, j * P:j * P + P], raw[:, g * per + j, :], ident)
                ins.then_inc(turned, 1)

        @block.scalar
        def _(act):
            for g in range(NT // per):
                act.wait_ge(turned, g + 1)
                act.activation(X[:, g * CH:g * CH + CH], bank[g % 2][:, :], ACT.Copy).then_inc(kept, 1)


def store_tokens(nc, sem, out_dram, X, ident):
    with ExitStack() as mem:
        raw = mem.enter_context(nc.sbuf_tensor("out_tokens", [P, NT, DIM], F32))
        bank = [mem.enter_context(nc.psum_tensor(f"store_bank{i}", [P, CH], F32)) for i in range(2)]
        turned = sem("out_turned")
        kept = sem("out_kept")
        stored = sem("out_stored")
        per = CH // P
        block = mem.enter_context(nc.Block())

        @block.tensor
        def _(pe):
            for g in range(NT // per):
                if g >= 2:
                    pe.wait_ge(kept, g - 1)
                for j in range(per):
                    t = g * per + j
                    ins = pe.transpose(bank[g % 2][:, j * P:j * P + P], X[:, t * P:t * P + P], ident)
                ins.then_inc(turned, 1)

        @block.scalar
        def _(act):
            for g in range(NT // per):
                act.wait_ge(turned, g + 1)
                act.activation(raw[:, g * per:g * per + per, :], bank[g % 2][:, :].rearrange("p (t d) -> p t d", t=per),
                               ACT.Copy).then_inc(kept, 1)

        @block.sync
        def _(sp):
            for b in range(BATCH):
                sp.wait_ge(kept, 2 * b + 2)
                sp.dma_start(out_dram[b].rearrange("(t p) d -> p t d", p=P), raw[:, b * 8:b * 8 + 8, :]).then_inc(stored, 16)
            sp.wait_ge(stored, 16 * BATCH)


def norm_all(nc, sem, ln, X, out, vec, mean_w, eps, vectors, banks, mem):
    chunks = TOKENS // CH
    mean_bank, var_bank = banks
    buf = [[mem.enter_context(nc.sbuf_tensor(f"norm_{k}{i}", [P, CH], F32)) for k in ("cent", "cent_sq", "std", "rstd")]
           for i in range(2)]
    loaded = sem("norm_vectors_loaded")
    scaled = sem("norm_scaled")
    done = sem("norm_done")
    with nc.Block() as block:
        @block.sync
        def _(sp):
            sp.dma_start(vec[:, :], vectors).then_inc(loaded, 16)
            sp.wait_ge(loaded, 16)

        @block.tensor
        def _(pe):
            def var(c):
                norm_var(pe, ln, c, mean_w, buf[c % 2][1][:, :], var_bank[c % 2][:, :])

            for c in range(chunks):
                if c >= 2:
                    pe.wait_ge(ln.cent, c - 1)
                norm_mean(pe, ln, mean_w, X[:, c * CH:c * CH + CH], mean_bank[c % 2][:, :])
                if c >= 1:
                    var(c - 1)
            var(chunks - 1)

        @block.scalar
        def _(act):
            for c in range(chunks):
                norm_squares(act, ln, c, buf[c % 2][0][:, :], buf[c % 2][1][:, :])
                if c >= 2:
                    act.wait_ge(ln.rstd, c - 1)
                norm_std(act, ln, c, var_bank[c % 2][:, :], buf[c % 2][2][:, :], eps)

        @block.vector
        def _(dve):
            def finish(c):
                cent, _, std, rstd = buf[c % 2]
                norm_inverse(dve, ln, c, std[:, :], rstd[:, :])
                dve.tensor_tensor(cent[:, :], cent[:, :], rstd[:, :], ALU.mult).then_inc(scaled, 1)
                dve.wait_ge(scaled, c + 1)
                dve.tensor_scalar(out[:, c * CH:c * CH + CH], cent[:, :], vec[:, 4:5], vec[:, 5:6], ALU.mult, ALU.add).then_inc(done, 1)

            dve.wait_ge(loaded, 16)
            for c in range(chunks):
                if c >= 2:
                    dve.wait_ge(done, c - 1)
                norm_centre(dve, ln, c, X[:, c * CH:c * CH + CH], buf[c % 2][0][:, :], mean_bank[c % 2][:, :])
                if c >= 1:
                    finish(c - 1)
            finish(chunks - 1)


def mamba(nc, sem, name, X, X1, w, consts):
    first = name == "a"
    ident, mean_w, eps = consts
    low = 1 if first else 8
    LOW = 3 * 2 * STATES
    rows = LOW + low
    with ExitStack() as mem:
        def sb(label, shape, dt=F32):
            return mem.enter_context(nc.sbuf_tensor(f"{name}_{label}", shape, dt))

        def bank(label):
            return mem.enter_context(nc.psum_tensor(f"{name}_{label}", [P, CH], F32))

        w_in = sb("w_in", [P, 2 * D_INNER])
        w_conv = sb("w_conv", [P, TAPS, DB, D_INNER]) if first else None
        taps = None if first else sb("taps", [P, DB, TAPS])
        diag = None if first else sb("diag", [P, DB, TAPS, P])
        w_x = sb("w_x", [P, DB, rows])
        w_dt = sb("w_dt", [rows, D_INNER])
        w_out = sb("w_out", [P, DB, DIM])
        vec = sb("vectors", [P, 8])
        neg_dt = sb("neg_dt_bias", [P, DB])
        a_log = None if first else sb("a_log", [P, DB, STATES])
        a_neg = None if first else sb("a_neg", [P, DB, STATES])
        select = sb("select", [LOW, 2 * STATES, P], BF16)
        ln2_buf = [sb(f"ln2_{k}", [P, CH]) for k in ("cent", "cent_sq", "std", "rstd")]
        x_in = sb("x_in", [P, DB, TAPS - 1 + SEQ])
        gate = [sb(f"gate{i}", [P, DB, CH]) for i in range(2)]
        u = [sb(f"u{i}", [P, DB, CH]) for i in range(2)]
        du = u if first else [sb(f"du{i}", [P, DB, CH]) for i in range(2)]
        dec = [sb(f"decay_or_delta{i}", [P, DB, CH]) for i in range(2)]
        parts = [sb(f"ssm_parts{i}", [LOW, CH], BF16) for i in range(2)]
        part2 = sb("ssm_second_part", [LOW, CH], BF16)
        rest = sb("ssm_rest", [LOW, 2, CH])
        soft = None if first else sb("soft", [P, DB, 3, CH])
        ssm = sb("ssm", [rows, CH])
        c_sb = sb("c_rows", [P, 2, CH])
        bu = sb("b_times_u", [P, 2, DB, CH])
        h = sb("state", [P, 2, DB, CH])
        hc = sb("state_times_c", [P, 2, DB, CH])
        a_ring = None if first else sb("decays", [P, 2, DB, CH])
        carry = sb("carry", [P, STATES, DB])
        g = sb("gated", [P, DB, CH])
        yd = None if first else sb("y_plus_skip", [P, DB, CH])
        r = sb("residual", [P, CH])
        r2 = sb("residual2", [P, CH])
        b_bank = [bank(f"b_bank{i}") for i in range(2)]
        c_bank = bank("c_bank")
        y_bank = [bank(f"y_bank{i}") for i in range(DB)]
        p_bank = [bank(f"p_bank{i}") for i in range(2)]
        o_bank = bank("o_bank")

        loaded = sem(f"{name}_weights_loaded")
        setup = sem(f"{name}_setup_done")
        select_step = sem(f"{name}_select_step")
        ln1 = Norm(sem, f"{name}_ln1") if first else None
        ln2 = Norm(sem, f"{name}_ln2")
        pre_mm = sem(f"{name}_projection_ready")
        pre_ev = sem(f"{name}_projection_kept")
        soft_step = sem(f"{name}_softplus_step")
        poly_step = sem(f"{name}_log1p_step")
        log1p = log1p_coefficients()
        taps_at = ((4, 5), (6, 7)) if first else ((4,), (5,))
        u_at = (7, 9) if first else (6, 7)
        rows_at = 9 if first else 7
        delta_ready = sem(f"{name}_delta_ready")
        part_step = sem(f"{name}_part_step")
        rest_step = sem(f"{name}_rest_step")
        b_ready = sem(f"{name}_b_ready")
        c_ready = sem(f"{name}_c_ready")
        c_kept = sem(f"{name}_c_kept")
        a_ready = sem(f"{name}_decay_ready")
        bu_ready = sem(f"{name}_bu_ready")
        h_ready = sem(f"{name}_state_ready")
        carried = sem(f"{name}_state_carried")
        hc_ready = sem(f"{name}_hc_ready")
        summed = sem(f"{name}_hc_summed")
        skip_ready = sem(f"{name}_skip_added")
        g_ready = sem(f"{name}_gated_ready")
        out_ready = sem(f"{name}_out_ready")
        res_ready = sem(f"{name}_residual_ready")
        done = sem(f"{name}_chunk_done")
        LOADS = 16 * (9 if first else 7)
        SETUP = 3 if first else 12
        source = X if first else X1
        x_op = X1
        PRE = 9
        if first:
            norm_all(nc, sem, ln1, X, X1, vec, mean_w, eps, w["vectors"], [b_bank, y_bank], mem)
        block = mem.enter_context(nc.Block())

        def at(b, half, per, k):
            return b * (HALVES * per) + (half * per + k)

        def cols(b, half):
            return bass.ds(b * SEQ + half * CH, CH)

        @block.sync
        def _(sp):
            sp.dma_start(w_in[:, :], w["in_proj"]).then_inc(loaded, 16)
            if first:
                for k in range(TAPS):
                    sp.dma_start(w_conv[:, k, :, :], w["conv"][k].rearrange("(e p) o -> p e o", p=P)).then_inc(loaded, 16)
            else:
                sp.dma_start(taps[:, :, :], w["taps"].rearrange("(d p) k -> p d k", p=P)).then_inc(loaded, 16)
                sp.dma_start(a_log[:, :, :], w["a_log"].rearrange("(d p) n -> p d n", p=P)).then_inc(loaded, 16)
            sp.dma_start(w_x[:, :, :], w["x_proj"].rearrange("(e p) r -> p e r", p=P)).then_inc(loaded, 16)
            sp.dma_start(w_dt[LOW:rows, :], w["dt"]).then_inc(loaded, 16)
            sp.dma_start(w_out[:, :, :], w["out_proj"].rearrange("(e p) o -> p e o", p=P)).then_inc(loaded, 16)
            sp.dma_start(vec[:, :], w["vectors"]).then_inc(loaded, 16)

        def schedule(eng, body):
            body(0, 0, False, True)
            with eng.Fori(0, BATCH - 1) as g:
                body(g, 1, True, True)
                body(g + 1, 0, True, True)
            body(BATCH - 1, 1, True, False)

        def before(b, half):
            return (b, 0) if half else (b - 1, 1)

        def after(b, half):
            return (b + 1, 0) if half else (b, 1)

        @block.tensor
        def _(pe):
            def project(b, half, m):
                pe.wait_ge(pre_ev, at(b, half, PRE, m - 1 if m >= 2 else 0))
                x = x_op[:, cols(b, half)]
                pe.matmul(p_bank[m % 2][:, :], lhsT=w_in[:, m * P:m * P + P], rhs=x, start=True, stop=True).then_inc(pre_mm, 1)

            def convolve(b, half, d, part, n_parts):
                t0 = half * CH
                if part == 0:
                    pe.wait_ge(pre_ev, at(b, half, PRE, 3 + d))
                pairs = [(k, e) for k in range(TAPS) for e in (range(DB) if first else (d,))]
                size = len(pairs) // n_parts
                for i in range(part * size, part * size + size):
                    k, e = pairs[i]
                    w = w_conv[:, k, e, d * P:d * P + P] if first else diag[:, d, k, :]
                    ins = pe.matmul(p_bank[d][:, :], lhsT=w, rhs=x_in[:, e, t0 + k:t0 + k + CH], start=i == 0, stop=i == len(pairs) - 1)
                if part == n_parts - 1:
                    ins.then_inc(pre_mm, 1)

            def project_x(b, half):
                pe.wait_ge(pre_ev, at(b, half, PRE, 6))
                for e in range(DB):
                    ins = pe.matmul(p_bank[0][0:rows, :], lhsT=w_x[:, e, :], rhs=u[half][:, e, :], start=e == 0, stop=e == DB - 1)
                ins.then_inc(pre_mm, 1)

            def project_step(b, half):
                pe.wait_ge(pre_ev, at(b, half, PRE, 7))
                for d in range(DB):
                    pe.matmul(p_bank[1 - d][:, :], lhsT=w_dt[LOW:rows, d * P:d * P + P], rhs=ssm[LOW:rows, :], start=True,
                              stop=True).then_inc(pre_mm, 1)

            def spread(b, half, s, prior):
                if s < 2:
                    pe.wait_ge(part_step, at(b, half, 4, 4))
                if prior:
                    pe.wait_ge(bu_ready, at(b, half, 2 * STATES, 2 * (s - 1)))
                pe.matmul(b_bank[s % 2][:, :], lhsT=select[:, s, :], rhs=parts[half][:, :], start=True, stop=True).then_inc(b_ready, 1)
                if prior or s == 1:
                    pe.wait_ge(c_kept, at(b, half, STATES, s))
                pe.matmul(c_bank[:, :], lhsT=select[:, STATES + s, :], rhs=parts[half][:, :], start=True,
                          stop=True).then_inc(c_ready, 1)

            def project_out(b, half):
                for d in range(DB):
                    pe.wait_ge(g_ready, at(b, half, DB, d + 1))
                    ins = pe.matmul(o_bank[:, :], lhsT=w_out[:, d, :], rhs=g[:, d, :], start=d == 0, stop=d == DB - 1)
                ins.then_inc(out_ready, 1)

            def ln2_mean(b, half):
                pe.wait_ge(res_ready, at(b, half, 2, 2))
                norm_mean(pe, ln2, mean_w, r2[:, :], o_bank[:, :])

            def ln2_var(b, half):
                norm_var(pe, ln2, at(b, half, 1, 0), mean_w, ln2_buf[1][:, :], o_bank[:, :])

            def pre(b, half, k):
                if k in (0, 2):
                    project(b, half, k)
                    project(b, half, k + 1)
                for d in range(DB):
                    if k in taps_at[d]:
                        convolve(b, half, d, taps_at[d].index(k), len(taps_at[d]))
                if k == rows_at:
                    project_x(b, half)
                if k == rows_at + 2:
                    project_step(b, half)

            def post(b, half, k):
                if k == 1:
                    project_out(b, half)
                if k == 3:
                    ln2_mean(b, half)
                if k == 6:
                    ln2_var(b, half)

            def body(b, half, has_post, has_pre):
                for s in range(STATES):
                    if s == 0 and has_post:
                        pe.wait_ge(g_ready, at(b, half, DB, 0))
                    for d in range(DB):
                        pe.wait_ge(hc_ready, at(b, half, 2 * STATES, 2 * s + d + 1))
                        pe.matmul(y_bank[d][:, :], lhsT=ident, rhs=hc[:, s % 2, d, :], start=s == 0,
                                  stop=s == STATES - 1).then_inc(summed, 1)
                    if s + 2 < STATES:
                        spread(b, half, s + 2, True)
                    elif has_pre:
                        spread(*after(b, half), s + 2 - STATES, True)
                    if has_post:
                        post(*before(b, half), s)
                    if has_pre:
                        pre(*after(b, half), s)

            pe.wait_ge(loaded, LOADS)
            pe.wait_ge(setup, SETUP)
            for k in range(STATES):
                pre(0, 0, k)
            spread(0, 0, 0, False)
            spread(0, 0, 1, False)
            schedule(pe, body)
            project_out(BATCH - 1, 1)
            ln2_mean(BATCH - 1, 1)
            ln2_var(BATCH - 1, 1)

        @block.scalar
        def _(act):
            def keep_x(b, half, m):
                t0 = TAPS - 1 + half * CH
                act.wait_ge(pre_mm, at(b, half, PRE, m + 1))
                act.activation(x_in[:, m, t0:t0 + CH], p_bank[m][:, :], ACT.Copy).then_inc(pre_ev, 1)

            def keep_gate(b, half, m):
                act.wait_ge(pre_mm, at(b, half, PRE, m + 3))
                act.activation(gate[half][:, m, :], p_bank[m][:, :], ACT.Silu).then_inc(pre_ev, 1)

            def keep_u(b, half, d):
                act.wait_ge(pre_mm, at(b, half, PRE, 5 + d))
                act.activation(u[half][:, d, :], p_bank[d][:, :], ACT.Silu, bias=vec[:, d:d + 1]).then_inc(pre_ev, 1)

            def keep_rows(b, half):
                act.wait_ge(pre_mm, at(b, half, PRE, 7))
                act.activation(ssm[:, :], p_bank[0][0:rows, :], ACT.Copy).then_inc(pre_ev, 1)
                act.wait_ge(pre_ev, at(b, half, PRE, 7))
                act.activation(parts[half][:, :], ssm[0:LOW, :], ACT.Copy).then_inc(part_step, 1)

            def keep_parts(b, half, k):
                if k == 0:
                    act.wait_ge(rest_step, at(b, half, 2, 1))
                    act.activation(part2[:, :], rest[:, 0, :], ACT.Copy).then_inc(part_step, 1)
                    act.activation(parts[half][32:64, :], rest[32:64, 0, :], ACT.Copy).then_inc(part_step, 1)
                else:
                    act.wait_ge(rest_step, at(b, half, 2, 2))
                    act.activation(parts[half][64:96, :], rest[64:96, 1, :], ACT.Copy).then_inc(part_step, 1)

            def keep_step(b, half):
                for d in range(DB):
                    act.wait_ge(pre_mm, at(b, half, PRE, 8 + d))
                    if first:
                        act.activation(dec[half][:, d, :], p_bank[1 - d][:, :], ACT.Sigmoid, bias=neg_dt[:, d:d + 1],
                                       scale=-1.0).then_inc(pre_ev, 1)
                    else:
                        act.activation(soft[:, d, 0, :], p_bank[1 - d][:, :], ACT.Identity, bias=vec[:, 2 + d:3 + d]).then_inc(pre_ev, 1)
                if not first:
                    act.wait_ge(pre_ev, at(b, half, PRE, 9))
                    act.activation(soft[:, :, 1, :], soft[:, :, 0, :], ACT.Abs).then_inc(soft_step, 1)
                    act.wait_ge(soft_step, at(b, half, 2, 1))
                    act.activation(soft[:, :, 2, :], soft[:, :, 1, :], ACT.Exp, scale=-1.0).then_inc(soft_step, 1)

            def decays(b, half, s, prior):
                if s == 0:
                    act.wait_ge(delta_ready, at(b, half, 2, 1))
                for d in range(DB):
                    if prior:
                        act.wait_ge(h_ready, at(b, half, 2 * STATES, 2 * (s - 2) + d + 1))
                    act.activation(a_ring[:, s % 2, d, :], dec[half][:, d, :], ACT.Exp, scale=a_neg[:, d, s:s + 1]).then_inc(a_ready, 1)

            def pre(b, half, k):
                if k == 2:
                    keep_x(b, half, 0)
                    keep_x(b, half, 1)
                if k == 4:
                    keep_gate(b, half, 0)
                    keep_gate(b, half, 1)
                for d in range(DB):
                    if k == u_at[d]:
                        keep_u(b, half, d)
                if k == rows_at + 2:
                    keep_rows(b, half)
                if k in (rows_at + 3, rows_at + 4):
                    keep_parts(b, half, k - rows_at - 3)
                if k == rows_at + 4:
                    keep_step(b, half)

            def post(b, half, k):
                if k == 6:
                    norm_squares(act, ln2, at(b, half, 1, 0), ln2_buf[0][:, :], ln2_buf[1][:, :])
                if k == 8:
                    norm_std(act, ln2, at(b, half, 1, 0), o_bank[:, :], ln2_buf[2][:, :], eps)

            def body(b, half, has_post, has_pre):
                for s in range(STATES):
                    act.wait_ge(c_ready, at(b, half, STATES, s + 1))
                    if s >= 2 or has_post:
                        act.wait_ge(hc_ready, at(b, half, 2 * STATES, 2 * (s - 1)))
                    act.activation(c_sb[:, s % 2, :], c_bank[:, :], ACT.Copy).then_inc(c_kept, 1)
                    if not first:
                        if s + 1 < STATES:
                            decays(b, half, s + 1, s >= 1 or has_post)
                        elif has_pre:
                            decays(*after(b, half), 0, True)
                    if has_post:
                        post(*before(b, half), s)
                    if has_pre:
                        pre(*after(b, half), s)
                    if half == 0:
                        for d in range(DB):
                            act.wait_ge(h_ready, at(b, half, 2 * STATES, 2 * s + d + 1))
                            act.activation(carry[:, s, d:d + 1], h[:, s % 2, d, CH - 1:CH], ACT.Copy).then_inc(carried, 1)

            if not first:
                act.wait_ge(loaded, LOADS)
                act.activation(a_neg[:, :, :], a_log[:, :, :], ACT.Exp).then_inc(setup, 1)
            act.wait_ge(setup, SETUP)
            for k in range(STATES):
                pre(0, 0, k)
            if not first:
                decays(0, 0, 0, False)
            schedule(act, body)
            for k in range(STATES):
                post(BATCH - 1, 1, k)

        @block.gpsimd
        def _(pool):
            def body(b, half, has_post, has_pre):
                for s in range(STATES):
                    pool.wait_ge(c_kept, at(b, half, STATES, s + 1))
                    for d in range(DB):
                        pool.wait_ge(h_ready, at(b, half, 2 * STATES, 2 * s + d + 1))
                        if s >= 2 or has_post:
                            pool.wait_ge(summed, at(b, half, 2 * STATES, 2 * (s - 2) + d + 1))
                        pool.tensor_tensor(hc[:, s % 2, d, :], h[:, s % 2, d, :], c_sb[:, s % 2, :], ALU.mult).then_inc(hc_ready, 1)

            pool.memset(x_in[:, :, 0:TAPS - 1], 0.0).then_inc(setup, 1)
            pool.memset(select[:, :, :], 0.0).then_inc(select_step, 1)
            for k in range(3):
                pool.wait_ge(select_step, k + 1)
                pool.affine_select(out=select[:, :, :], in_=select[:, :, :], pattern=[[-1, 2 * STATES], [0, P]],
                                   compare_op=ALU.not_equal, fill=1.0, base=-2 * STATES * k,
                                   channel_multiplier=1).then_inc(setup if k == 2 else select_step, 1)
            schedule(pool, body)

        @block.vector
        def _(dve):
            def rests(b, half, k):
                if k == 0:
                    dve.wait_ge(part_step, at(b, half, 4, 1))
                    dve.tensor_tensor(rest[:, 0, :], ssm[0:LOW, :], parts[half][:, :], ALU.subtract).then_inc(rest_step, 1)
                else:
                    dve.wait_ge(part_step, at(b, half, 4, 2))
                    dve.tensor_tensor(rest[:, 1, :], rest[:, 0, :], part2[:, :], ALU.subtract).then_inc(rest_step, 1)

            def softplus(b, half, first_k, end_k):
                e, q = soft[:, :, 2, :], soft[:, :, 1, :]
                for k in range(first_k, end_k):
                    if k == 0:
                        dve.wait_ge(soft_step, at(b, half, 2, 2))
                        dve.tensor_scalar(q, e, log1p[LOG1P_DEGREE], None, ALU.mult).then_inc(poly_step, 1)
                    elif k <= LOG1P_DEGREE:
                        dve.wait_ge(poly_step, at(b, half, LOG1P_DEGREE + 1, k))
                        dve.scalar_tensor_tensor(q, q, log1p[LOG1P_DEGREE - k], e, ALU.add, ALU.mult).then_inc(poly_step, 1)
                    else:
                        dve.wait_ge(poly_step, at(b, half, LOG1P_DEGREE + 1, LOG1P_DEGREE + 1))
                        dve.scalar_tensor_tensor(dec[half][:, :, :], soft[:, :, 0, :], 0.0, soft[:, :, 1, :], ALU.max,
                                                 ALU.add).then_inc(delta_ready, 1)
                        dve.wait_ge(delta_ready, at(b, half, 2, 1))
                        dve.tensor_tensor(du[half][:, :, :], dec[half][:, :, :], u[half][:, :, :], ALU.mult).then_inc(delta_ready, 1)

            def pre(b, half, k):
                if k in (rows_at + 2, rows_at + 3):
                    rests(b, half, k - rows_at - 2)
                if not first and k > rows_at + 4:
                    at_k = 3 * (k - rows_at - 5)
                    softplus(b, half, min(at_k, LOG1P_DEGREE + 2), min(at_k + 3, LOG1P_DEGREE + 2))

            def gated(b, half):
                dve.wait_ge(summed, at(b, half, 2 * STATES, 2 * STATES))
                for d in range(DB):
                    if first:
                        dve.tensor_tensor(g[:, d, :], gate[half][:, d, :], y_bank[d][:, :], ALU.mult).then_inc(g_ready, 1)
                    else:
                        dve.scalar_tensor_tensor(yd[:, d, :], u[half][:, d, :], vec[:, 6 + d:7 + d], y_bank[d][:, :], ALU.mult,
                                                 ALU.add).then_inc(skip_ready, 1)
                        dve.wait_ge(skip_ready, at(b, half, DB, d + 1))
                        dve.tensor_tensor(g[:, d, :], gate[half][:, d, :], yd[:, d, :], ALU.mult).then_inc(g_ready, 1)

            def post(b, half, k):
                n = at(b, half, 1, 0)
                if k == 0:
                    gated(b, half)
                if k == 3:
                    dve.wait_ge(out_ready, at(b, half, 1, 1))
                    dve.tensor_tensor(r[:, :], source[:, cols(b, half)], o_bank[:, :], ALU.add).then_inc(res_ready, 1)
                    dve.wait_ge(res_ready, at(b, half, 2, 1))
                    dve.tensor_tensor(r2[:, :], r[:, :], X[:, cols(b, half)], ALU.add).then_inc(res_ready, 1)
                if k == 5:
                    dve.wait_ge(res_ready, at(b, half, 2, 2))
                    norm_centre(dve, ln2, n, r2[:, :], ln2_buf[0][:, :], o_bank[:, :])
                if k == 9:
                    norm_inverse(dve, ln2, n, ln2_buf[2][:, :], ln2_buf[3][:, :])
                    dve.tensor_tensor(X[:, cols(b, half)], ln2_buf[0][:, :], ln2_buf[3][:, :], ALU.mult).then_inc(done, 1)

            def body(b, half, has_post, has_pre):
                for s in range(STATES):
                    prior = s >= 2 or has_post
                    dve.wait_ge(b_ready, at(b, half, STATES, s + 1))
                    if s == 0:
                        if first:
                            dve.wait_ge(pre_ev, at(b, half, PRE, 9))
                        else:
                            dve.wait_ge(delta_ready, at(b, half, 2, 2))
                    for d in range(DB):
                        if prior:
                            dve.wait_ge(h_ready, at(b, half, 2 * STATES, 2 * (s - 2) + d + 1))
                        dve.tensor_tensor(bu[:, s % 2, d, :], du[half][:, d, :], b_bank[s % 2][:, :], ALU.mult).then_inc(bu_ready, 1)
                    for d in range(DB):
                        dve.wait_ge(bu_ready, at(b, half, 2 * STATES, 2 * s + d + 1))
                        if prior:
                            dve.wait_ge(hc_ready, at(b, half, 2 * STATES, 2 * (s - 2) + d + 1))
                        if half == 0 and s >= 2:
                            dve.wait_ge(carried, b * 2 * STATES + (2 * (s - 2) + d + 1))
                        elif half == 1 and s < 2:
                            dve.wait_ge(carried, b * 2 * STATES + 2 * STATES)
                        if not first:
                            dve.wait_ge(a_ready, at(b, half, 2 * STATES, 2 * s + d + 1))
                        decay = dec[half][:, d, :] if first else a_ring[:, s % 2, d, :]
                        start = 0.0 if half == 0 else carry[:, s, d:d + 1]
                        dve.tensor_tensor_scan(h[:, s % 2, d, :], decay, bu[:, s % 2, d, :], start, ALU.mult,
                                               ALU.add).then_inc(h_ready, 1)
                    if has_post:
                        post(*before(b, half), s)
                    if has_pre:
                        pre(*after(b, half), s)

            dve.wait_ge(loaded, LOADS)
            if first:
                dve.tensor_scalar(neg_dt[:, :], vec[:, 2:4], -1.0, None, ALU.mult).then_inc(setup, 1)
            else:
                for d in range(DB):
                    for k in range(TAPS):
                        dve.tensor_scalar(diag[:, d, k, :], ident, taps[:, d, k:k + 1], None, ALU.mult).then_inc(setup, 1)
                dve.wait_ge(setup, SETUP - 1)
                dve.tensor_scalar(a_neg[:, :, :], a_neg[:, :, :], -1.0, None, ALU.mult).then_inc(setup, 1)
            for k in range(STATES):
                pre(0, 0, k)
            schedule(dve, body)
            for k in range(STATES):
                post(BATCH - 1, 1, k)


EXPERTS = 8
FF = 512
FB = FF // P
THRESHOLD = 0.125


def experts(nc, sem, X, d, consts):
    ident, mean_w, eps = consts
    G = EXPERTS + 1
    with ExitStack() as mem:
        def sb(label, shape, dt=F32):
            return mem.enter_context(nc.sbuf_tensor(f"b_{label}", shape, dt))

        def bank(label):
            return mem.enter_context(nc.psum_tensor(f"b_{label}", [P, CH], F32))

        w1 = sb("w1", [P, EXPERTS, FF])
        w2 = sb("w2", [P, EXPERTS, FB, DIM])
        b1 = sb("b1", [P, EXPERTS * FB])
        b2 = sb("b2", [EXPERTS, DIM])
        wg = sb("w_gate", [P, G])
        bg = sb("gate_bias", [P, G])
        select = sb("select", [EXPERTS, EXPERTS, P])
        logit = sb("logit", [P, NT, G])
        top = sb("top", [P, NT])
        ex = sb("exps", [P, NT, EXPERTS])
        total = sb("total", [P, NT])
        inv = sb("inverse", [P, NT])
        thr = sb("threshold", [P, NT])
        fix = sb("zero_fix", [P, NT])
        wt = sb("weights", [P, NT, EXPERTS])
        w_rows = sb("weight_rows", [EXPERTS, TOKENS])
        wb = sb("spread_weights", [P, 2, CH])
        hid = sb("hidden", [P, 4, CH])
        part = sb("weighted", [P, 2, CH])
        acc = sb("acc", [P, CH])
        res = sb("residual", [P, CH])
        cent = sb("cent", [P, CH])
        cent_sq = sb("cent_sq", [P, CH])
        std = sb("std", [P, CH])
        rstd = sb("rstd", [P, CH])
        h_bank = [bank(f"h_bank{i}") for i in range(3)]
        o_bank = [bank(f"o_bank{i}") for i in range(2)]
        w_bank = bank("w_bank")
        n_bank = [bank(f"n_bank{i}") for i in range(2)]

        loaded = sem("b_weights_loaded")
        gate_loaded = sem("b_gate_loaded")
        select_step = sem("b_select_step")
        logits_ready = sem("b_logits_ready")
        gate_step = sem("b_gate_step")
        gate_act = sem("b_gate_exps")
        gate_fix = sem("b_zero_sum_step")
        turned = sem("b_weights_turned")
        turned_kept = sem("b_weight_rows_kept")
        hid_mm = sem("b_hidden_ready")
        gelu_ready = sem("b_gelu_ready")
        out_mm = sem("b_expert_out")
        spread_mm = sem("b_weights_spread")
        spread_kept = sem("b_spread_kept")
        weighted = sem("b_weighted")
        summed = sem("b_summed")
        bias_mm = sem("b_bias_ready")
        res_ready = sem("b_residual_ready")
        ln = Norm(sem, "b_ln")
        done = sem("b_chunk_done")
        UNITS = EXPERTS * FB
        CHUNKS = TOKENS // CH
        block = mem.enter_context(nc.Block())

        @block.sync
        def _(sp):
            sp.dma_start(wg[:, :], d["b_gate"]).then_inc(gate_loaded, 16)
            sp.dma_start(bg[:, :], d["b_gate_bias"]).then_inc(gate_loaded, 16)
            sp.dma_start(b1[:, :], d["b_b1"]).then_inc(loaded, 16)
            sp.dma_start(b2[:, :], d["b_b2"]).then_inc(loaded, 16)
            sp.dma_start(w1[:, :, :], d["b_w1"].rearrange("e p f -> p e f")).then_inc(loaded, 16)
            for e in range(EXPERTS):
                sp.dma_start(w2[:, e, :, :], d["b_w2"][e].rearrange("(f p) o -> p f o", p=P)).then_inc(loaded, 16)

        @block.gpsimd
        def _(pool):
            pool.memset(select[:, :, :], 1.0).then_inc(select_step, 1)
            pool.wait_ge(select_step, 1)
            pool.affine_select(out=select[:, :, :], in_=select[:, :, :], pattern=[[-1, EXPERTS], [0, P]],
                               compare_op=ALU.is_equal, fill=0.0, base=0, channel_multiplier=1).then_inc(select_step, 1)

        @block.tensor
        def _(pe):
            pe.wait_ge(gate_loaded, 32)
            logits = n_bank[0][:, 0:NT * G].rearrange("p (t g) -> p t g", g=G)
            for t in range(NT):
                ins = pe.matmul(logits[:, t, :], lhsT=X[:, t * P:t * P + P], rhs=wg[:, :], start=True, stop=True)
            ins.then_inc(logits_ready, 1)
            pe.wait_ge(gate_step, 11)
            for c in range(CHUNKS):
                if c >= 2:
                    pe.wait_ge(turned_kept, c - 1)
                for j in range(CH // P):
                    ins = pe.transpose(n_bank[c % 2][0:EXPERTS, j * P:j * P + P], wt[:, c * (CH // P) + j, :], ident)
                ins.then_inc(turned, 1)
            pe.wait_ge(loaded, 16 * (3 + EXPERTS))
            pe.wait_ge(select_step, 2)

            def tail(c, u):
                if u == 1:
                    norm_mean(pe, ln, mean_w, res[:, :], n_bank[0][:, :])
                if u == 5:
                    norm_var(pe, ln, c, mean_w, cent_sq[:, :], n_bank[1][:, :])

            def chunk(c, has_tail):
                def accumulate(u):
                    e, f = u // FB, u % FB
                    pe.wait_ge(gelu_ready, c * UNITS + (u + 1))
                    if f == 0 and e >= 2:
                        pe.wait_ge(weighted, c * EXPERTS + (e - 1))
                    pe.matmul(o_bank[e % 2][:, :], lhsT=w2[:, e, f, :], rhs=hid[:, u % 4, :], start=f == 0,
                              stop=f == FB - 1).then_inc(out_mm, 1)

                for u in range(UNITS):
                    e, f = u // FB, u % FB
                    if f == 0:
                        if e >= 1:
                            pe.wait_ge(spread_kept, c * EXPERTS + e)
                    if u >= 3:
                        pe.wait_ge(gelu_ready, c * UNITS + (u - 2))
                    pe.matmul(h_bank[u % 3][:, :], lhsT=w1[:, e, f * P:f * P + P], rhs=X[:, bass.ds(c * CH, CH)], start=True,
                              stop=True).then_inc(hid_mm, 1)
                    if f == 0:
                        pe.matmul(w_bank[:, :], lhsT=select[:, e, :], rhs=w_rows[:, bass.ds(c * CH, CH)], start=True,
                                  stop=True).then_inc(spread_mm, 1)
                    if u >= 2:
                        accumulate(u - 2)
                    if has_tail:
                        tail(c - 1, u)
                if has_tail:
                    pe.wait_ge(ln.std, c)
                accumulate(UNITS - 2)
                accumulate(UNITS - 1)
                pe.matmul(n_bank[1][:, :], lhsT=b2[:, :], rhs=w_rows[:, bass.ds(c * CH, CH)], start=True, stop=True).then_inc(bias_mm, 1)
                pe.wait_ge(res_ready, c * 2 + 2)

            pe.wait_ge(turned_kept, CHUNKS)
            chunk(0, False)
            with pe.Fori(1, CHUNKS) as c:
                chunk(c, True)
            norm_pe(pe, ln, CHUNKS - 1, mean_w, res[:, :], cent_sq[:, :], n_bank[0][:, :], n_bank[1][:, :])

        @block.scalar
        def _(act):
            act.wait_ge(gate_step, 3)
            act.activation(ex[:, :, :], ex[:, :, :], ACT.Exp).then_inc(gate_act, 1)
            act.activation(thr[:, :], logit[:, :, EXPERTS], ACT.Sigmoid).then_inc(gate_act, 1)
            for c in range(CHUNKS):
                act.wait_ge(turned, c + 1)
                act.activation(w_rows[:, c * CH:c * CH + CH], n_bank[c % 2][0:EXPERTS, :], ACT.Copy).then_inc(turned_kept, 1)
            act.wait_ge(turned_kept, CHUNKS)
            act.wait_ge(loaded, 16 * (3 + EXPERTS))

            def chunk(c, has_tail):
                for u in range(UNITS):
                    e, f = u // FB, u % FB
                    if f == 0:
                        act.wait_ge(spread_mm, c * EXPERTS + (e + 1))
                        if e >= 2 or has_tail:
                            act.wait_ge(weighted, c * EXPERTS + (e - 1))
                        act.activation(wb[:, e % 2, :], w_bank[:, :], ACT.Copy).then_inc(spread_kept, 1)
                    act.wait_ge(hid_mm, c * UNITS + (u + 1))
                    if u >= 4 or has_tail:
                        act.wait_ge(out_mm, c * UNITS + (u - 3))
                    act.activation(hid[:, u % 4, :], h_bank[u % 3][:, :], ACT.Gelu_apprx_tanh, bias=b1[:, u:u + 1]).then_inc(gelu_ready, 1)
                    if has_tail and u == 4:
                        norm_squares(act, ln, c - 1, cent[:, :], cent_sq[:, :])
                    if has_tail and u == 8:
                        norm_std(act, ln, c - 1, n_bank[1][:, :], std[:, :], eps)

            chunk(0, False)
            with act.Fori(1, CHUNKS) as c:
                chunk(c, True)
            norm_act(act, ln, CHUNKS - 1, cent[:, :], cent_sq[:, :], n_bank[1][:, :], std[:, :], eps)

        @block.vector
        def _(dve):
            dve.wait_ge(logits_ready, 1)
            dve.tensor_tensor(logit[:, :, :], n_bank[0][:, 0:NT * G].rearrange("p (t g) -> p t g", g=G),
                              bg[:, :].unsqueeze(1).to_broadcast([P, NT, G]), ALU.add).then_inc(gate_step, 1)
            dve.wait_ge(gate_step, 1)
            dve.tensor_reduce(top[:, :], logit[:, :, 0:EXPERTS], AX.X, ALU.max).then_inc(gate_step, 1)
            dve.wait_ge(gate_step, 2)
            dve.tensor_tensor(ex[:, :, :], logit[:, :, 0:EXPERTS], top[:, :].unsqueeze(2).to_broadcast([P, NT, EXPERTS]),
                              ALU.subtract).then_inc(gate_step, 1)
            dve.wait_ge(gate_act, 2)
            dve.tensor_reduce(total[:, :], ex[:, :, :], AX.X, ALU.add).then_inc(gate_step, 1)
            dve.wait_ge(gate_step, 4)
            dve.reciprocal(inv[:, :], total[:, :]).then_inc(gate_step, 1)
            dve.wait_ge(gate_step, 5)
            dve.tensor_tensor(wt[:, :, :], ex[:, :, :], inv[:, :].unsqueeze(2).to_broadcast([P, NT, EXPERTS]), ALU.mult).then_inc(gate_step, 1)
            dve.wait_ge(gate_step, 6)
            dve.tensor_scalar(fix[:, :], thr[:, :], THRESHOLD, None, ALU.mult).then_inc(gate_step, 1)
            dve.wait_ge(gate_step, 7)
            dve.tensor_tensor(ex[:, :, :], wt[:, :, :], fix[:, :].unsqueeze(2).to_broadcast([P, NT, EXPERTS]),
                              ALU.subtract).then_inc(gate_step, 1)
            dve.wait_ge(gate_step, 8)
            dve.tensor_scalar(wt[:, :, :], ex[:, :, :], 0.0, None, ALU.max).then_inc(gate_step, 1)
            dve.wait_ge(gate_step, 9)
            dve.tensor_reduce(total[:, :], wt[:, :, :], AX.X, ALU.add).then_inc(gate_step, 1)
            dve.wait_ge(gate_step, 10)
            dve.scalar_tensor_tensor(fix[:, :], total[:, :], 0.0, total[:, :], ALU.is_equal, ALU.add).then_inc(gate_fix, 1)
            dve.wait_ge(gate_fix, 1)
            dve.reciprocal(inv[:, :], fix[:, :]).then_inc(gate_fix, 1)
            dve.wait_ge(gate_fix, 2)
            dve.tensor_tensor(wt[:, :, :], wt[:, :, :], inv[:, :].unsqueeze(2).to_broadcast([P, NT, EXPERTS]), ALU.mult).then_inc(gate_step, 1)

            def normalise(c):
                norm_inverse(dve, ln, c, std[:, :], rstd[:, :])
                dve.tensor_tensor(X[:, bass.ds(c * CH, CH)], cent[:, :], rstd[:, :], ALU.mult).then_inc(done, 1)

            def chunk(c, has_tail):
                if has_tail:
                    norm_centre(dve, ln, c - 1, res[:, :], cent[:, :], n_bank[0][:, :])
                for e in range(EXPERTS):
                    dve.wait_ge(out_mm, c * UNITS + (FB * e + FB))
                    dve.wait_ge(spread_kept, c * EXPERTS + (e + 1))
                    if e >= 2:
                        dve.wait_ge(summed, c * (EXPERTS - 1) + (e - 1))
                    dst = acc[:, :] if e == 0 else part[:, e % 2, :]
                    dve.tensor_tensor(dst, wb[:, e % 2, :], o_bank[e % 2][:, :], ALU.mult).then_inc(weighted, 1)
                    if e >= 1:
                        dve.wait_ge(weighted, c * EXPERTS + (e + 1))
                        dve.tensor_tensor(acc[:, :], acc[:, :], part[:, e % 2, :], ALU.add).then_inc(summed, 1)
                    if has_tail and e == 2:
                        normalise(c - 1)
                dve.wait_ge(bias_mm, c + 1)
                dve.wait_ge(summed, c * (EXPERTS - 1) + (EXPERTS - 1))
                dve.tensor_tensor(acc[:, :], acc[:, :], n_bank[1][:, :], ALU.add).then_inc(res_ready, 1)
                dve.wait_ge(res_ready, c * 2 + 1)
                dve.tensor_tensor(res[:, :], acc[:, :], X[:, bass.ds(c * CH, CH)], ALU.add).then_inc(res_ready, 1)
                dve.wait_ge(res_ready, c * 2 + 2)

            chunk(0, False)
            with dve.Fori(1, CHUNKS) as c:
                chunk(c, True)
            norm_centre(dve, ln, CHUNKS - 1, res[:, :], cent[:, :], n_bank[0][:, :])
            normalise(CHUNKS - 1)


HEADS = 16
HD = 8
GROUPS = 8
Q_PART = (0, 0, 1, 1, 0, 2, 1, 2)
K_PART = (0, 1, 0, 1, 2, 0, 2, 1)
KROWS = GROUPS * HD
QROWS = KROWS + 3
MASKED = -1e30
ROW_PIECES = [(i, lo, min(CH, P * (i + 1) - lo), lo + CH >= P * (i + 1)) for i in range(SEQ // P)
              for lo in range(0, P * (i + 1), CH)]
COL_PIECES = [(j, lo, CH - lo % CH) for j in range(SEQ // P) for lo in ([P * j, CH] if P * j < CH else [P * j])]
NP1 = len(ROW_PIECES)
NP2 = len(COL_PIECES)
TILES = SEQ // P
PROB_AT = [sum(SEQ - P * k for k in range(j)) for j in range(TILES + 1)]
PROB_COLS = PROB_AT[TILES]
HALF_HEADS = HEADS // 2
HALF_ROWS = HALF_HEADS * HD
OUT_ROWS = HALF_ROWS + HALF_HEADS


def mqa(nc, sem, X, X1, d, consts):
    ident = consts[0]
    with ExitStack() as mem:
        def sb(label, shape, dt=F32):
            return mem.enter_context(nc.sbuf_tensor(f"q_{label}", shape, dt))

        def bank(label):
            return mem.enter_context(nc.psum_tensor(f"q_{label}", [P, CH], F32))

        wq = sb("wq", [P, DIM])
        wk = sb("wk", [P, KROWS])
        wv = sb("wv", [P, HD])
        bq = sb("bq", [P, 1])
        bk = sb("bk", [KROWS, 1])
        bv = sb("bv", [P, HD])
        k_pick = sb("k_pick", [KROWS, 3])
        w_out = sb("w_out", [HALF_ROWS, 2, DIM])
        b_out = sb("b_out", [P, 1])
        ident16 = sb("ident16", [P, P], BF16)
        mask_row = sb("mask_row", [P, P], BF16)
        mask_col = sb("mask_col", [P, P], BF16)
        mask_f = sb("mask_f", [P, P])
        qf = sb("q", [P, 2, CH])
        qr = sb("q_rest", [P, 2, CH])
        qp = sb("q_parts", [P, 2, 3, CH], BF16)
        kf = sb("k", [KROWS, CH])
        kr = sb("k_rest", [KROWS, 2, CH])
        kp = sb("k_parts", [KROWS, 3, CH], BF16)
        kt = sb("k_sum", [KROWS, 2, CH])
        keys = sb("keys", [QROWS, 2, TOKENS], BF16)
        vals = sb("values", [P, NT, HD])
        q_all = sb("q_all", [QROWS, HEADS, SEQ], BF16)
        k_now = sb("keys_now", [QROWS, 2, SEQ], BF16)
        v_all = sb("values_for_each_head", [P, TILES, OUT_ROWS])
        head_cols = sb("head_columns", [P, HALF_HEADS, OUT_ROWS])
        v_head = [sb(f"values_of_head{i}", [P, TILES, OUT_ROWS]) for i in range(2)]
        zeros16 = sb("zeros16", [P, CH], BF16)
        spread = sb("spread", [OUT_ROWS, HALF_HEADS, HD])
        piece_max = sb("piece_max", [P, NP1])
        pair_max = sb("pair_max", [P, TILES])
        neg_max = sb("neg_max", [P, 2, TILES])
        m_rest = sb("max_rest", [TILES, 2, P])
        m_part = sb("max_parts", [TILES, 2, 3, P], BF16)
        probs = [sb(f"probs{i}", [P, PROB_COLS]) for i in range(2)]
        upper = sb("attended_upper", [OUT_ROWS, TOKENS])
        attended = (X1, upper)
        att_n = sb("attended_normed", [HALF_ROWS, 2, 2, CH])
        s_bank = [bank(f"s_bank{i}") for i in range(2)]
        t_bank = [bank(f"t_bank{i}") for i in range(3)]
        o_bank = [bank(f"o_bank{i}") for i in range(2)]
        m_bank = bank("m_bank")
        parts_dram = nc.dram_tensor("q_parts_dram", (BATCH, 3, P, SEQ), BF16, kind="Internal").ap()

        loaded = sem("q_weights_loaded")
        mask_step = sem("q_mask_step")
        proj_mm = sem("q_projection_ready")
        proj_kept = sem("q_projection_kept")
        v_kept = sem("q_values_kept")
        q_step = sem("q_split_step")
        k_step = sem("q_key_split_step")
        stored = [sem(f"q_parts_stored{i}") for i in range(2)]
        CHUNKS = TOKENS // CH
        phase = ExitStack()
        block = phase.enter_context(nc.Block())

        @block.sync
        def _(sp):
            w = d["q_wqkv"]
            sp.dma_start(wq[:, :], w[:, 0:DIM]).then_inc(loaded, 16)
            for g in range(GROUPS):
                sp.dma_start(wk[:, g * HD:g * HD + HD], w[:, DIM:DIM + HD]).then_inc(loaded, 16)
                sp.dma_start(bk[g * HD:g * HD + HD, :], d["q_bias"][DIM:DIM + HD, :]).then_inc(loaded, 16)
            sp.dma_start(wv[:, :], w[:, DIM + HD:DIM + 2 * HD]).then_inc(loaded, 16)
            sp.dma_start(bq[:, :], d["q_bias"][0:DIM, :]).then_inc(loaded, 16)
            sp.dma_start(bv[:, :], d["q_value_bias"]).then_inc(loaded, 16)
            sp.dma_start(k_pick[:, :], d["q_key_pick"]).then_inc(loaded, 16)
            sp.dma_start(w_out[:, :, :], d["q_w_out"].rearrange("(s p) n -> p s n", p=HALF_ROWS)).then_inc(loaded, 16)
            sp.dma_start(b_out[:, :], d["q_b_out"]).then_inc(loaded, 16)
            for c in range(CHUNKS):
                sp.wait_ge(q_step, 5 * c + 5)
                sp.dma_start(parts_dram[c // 2, :, :, (c % 2) * CH:(c % 2) * CH + CH].rearrange("s p t -> p s t"),
                             qp[:, c % 2, :, :]).then_inc(stored[c % 2], 16)
            for slot in range(2):
                sp.wait_ge(stored[slot], 16 * CHUNKS // 2)

        @block.gpsimd
        def _(pool):
            pool.memset(mask_f[:, :], 0.0).then_inc(mask_step, 1)
            pool.wait_ge(mask_step, 1)
            pool.affine_select(out=mask_row[:, :], in_=mask_f[:, :], pattern=[[-1, P]], compare_op=ALU.is_ge, fill=MASKED,
                               base=0, channel_multiplier=1).then_inc(mask_step, 1)
            pool.memset(spread[:, :, :], 1.0).then_inc(mask_step, 1)
            pool.wait_ge(mask_step, 3)
            pool.affine_select(out=spread[:, :, :], in_=spread[:, :, :], pattern=[[-1, HALF_HEADS], [0, HD]],
                               compare_op=ALU.is_equal, fill=0.0, base=-HALF_ROWS, channel_multiplier=1).then_inc(mask_step, 1)
            pool.affine_select(out=mask_col[:, :], in_=mask_f[:, :], pattern=[[1, P]], compare_op=ALU.is_ge, fill=MASKED,
                               base=0, channel_multiplier=-1).then_inc(mask_step, 1)

        @block.tensor
        def _(pe):
            pe.wait_ge(loaded, 16 * (2 * GROUPS + 7))
            for c in range(CHUNKS):
                x = X[:, c * CH:c * CH + CH]
                if c >= 2:
                    pe.wait_ge(proj_kept, 2 * (c - 1))
                pe.matmul(s_bank[c % 2][:, :], lhsT=wq[:, :], rhs=x, start=True, stop=True).then_inc(proj_mm, 1)
                pe.matmul(o_bank[c % 2][0:KROWS, :], lhsT=wk[:, :], rhs=x, start=True, stop=True).then_inc(proj_mm, 1)
                if c >= 2:
                    pe.wait_ge(v_kept, c)
                for j in range(CH // P):
                    ins = pe.matmul(t_bank[c % 2][:, j * HD:j * HD + HD], lhsT=X[:, c * CH + j * P:c * CH + j * P + P], rhs=wv[:, :],
                                    start=True, stop=True)
                ins.then_inc(proj_mm, 1)

        @block.scalar
        def _(act):
            act.activation(ident16[:, :], ident, ACT.Copy)
            act.wait_ge(loaded, 16 * (2 * GROUPS + 7))
            for c in range(CHUNKS):
                act.wait_ge(proj_mm, 3 * c + 1)
                if c >= 2:
                    act.wait_ge(q_step, 5 * (c - 1))
                act.activation(qf[:, c % 2, :], s_bank[c % 2][:, :], ACT.Identity, bias=bq[:, :]).then_inc(proj_kept, 1)
                act.wait_ge(proj_mm, 3 * c + 2)
                if c >= 1:
                    act.wait_ge(k_step, 8 * c)
                act.activation(kf[:, :], o_bank[c % 2][0:KROWS, :], ACT.Identity, bias=bk[:, :]).then_inc(proj_kept, 1)

        @block.vector
        def _(dve):
            dve.memset(v_all[:, :, HALF_ROWS:OUT_ROWS], 1.0)
            dve.memset(zeros16[:, :], 0.0)
            dve.memset(head_cols[:, :, :], 0.0).then_inc(v_kept, 1)
            dve.wait_ge(v_kept, 1)
            for h in range(HALF_HEADS):
                dve.memset(head_cols[:, h, h * HD:h * HD + HD], 1.0)
                dve.memset(head_cols[:, h, HALF_ROWS + h:HALF_ROWS + h + 1], 1.0)
            dve.memset(keys[KROWS:QROWS, 0, :], 0.0)
            dve.memset(keys[KROWS:QROWS, 1, :], 1.0)
            dve.memset(q_all[KROWS:QROWS, :, :], 0.0)
            for c in range(CHUNKS):
                dve.wait_ge(proj_mm, 3 * c + 3)
                dve.tensor_tensor(vals[:, 4 * c:4 * c + 4, :], t_bank[c % 2][:, 0:4 * HD].rearrange("p (t v) -> p t v", v=HD),
                                  bv[:, :].unsqueeze(1).to_broadcast([P, 4, HD]), ALU.add).then_inc(v_kept, 1)
                q, r, s = qf[:, c % 2, :], qr, qp[:, c % 2]
                dve.wait_ge(proj_kept, 2 * c + 1)
                if c >= 2:
                    dve.wait_ge(stored[c % 2], 16 * (c // 2))
                dve.tensor_copy(s[:, 0, :], q).then_inc(q_step, 1)
                dve.wait_ge(q_step, 5 * c + 1)
                dve.tensor_tensor(r[:, 0, :], q, s[:, 0, :], ALU.subtract).then_inc(q_step, 1)
                dve.wait_ge(q_step, 5 * c + 2)
                dve.tensor_copy(s[:, 1, :], r[:, 0, :]).then_inc(q_step, 1)
                dve.wait_ge(q_step, 5 * c + 3)
                dve.tensor_tensor(r[:, 1, :], r[:, 0, :], s[:, 1, :], ALU.subtract).then_inc(q_step, 1)
                dve.wait_ge(q_step, 5 * c + 4)
                dve.tensor_copy(s[:, 2, :], r[:, 1, :]).then_inc(q_step, 1)
                dve.wait_ge(proj_kept, 2 * c + 2)
                dve.tensor_copy(kp[:, 0, :], kf[:, :]).then_inc(k_step, 1)
                dve.wait_ge(k_step, 8 * c + 1)
                dve.tensor_tensor(kr[:, 0, :], kf[:, :], kp[:, 0, :], ALU.subtract).then_inc(k_step, 1)
                dve.wait_ge(k_step, 8 * c + 2)
                dve.tensor_copy(kp[:, 1, :], kr[:, 0, :]).then_inc(k_step, 1)
                dve.wait_ge(k_step, 8 * c + 3)
                dve.tensor_tensor(kr[:, 1, :], kr[:, 0, :], kp[:, 1, :], ALU.subtract).then_inc(k_step, 1)
                dve.wait_ge(k_step, 8 * c + 4)
                dve.tensor_scalar(kt[:, 0, :], kp[:, 0, :], k_pick[:, 0:1], None, ALU.mult).then_inc(k_step, 1)
                dve.tensor_copy(kp[:, 2, :], kr[:, 1, :]).then_inc(k_step, 1)
                dve.wait_ge(k_step, 8 * c + 6)
                dve.scalar_tensor_tensor(kt[:, 1, :], kp[:, 1, :], k_pick[:, 1:2], kt[:, 0, :], ALU.mult, ALU.add).then_inc(k_step, 1)
                dve.wait_ge(k_step, 8 * c + 7)
                for slot in range(2):
                    ins = dve.scalar_tensor_tensor(keys[0:KROWS, slot, c * CH:c * CH + CH], kp[:, 2, :], k_pick[:, 2:3], kt[:, 1, :],
                                                   ALU.mult, ALU.add)
                ins.then_inc(k_step, 1)
                dve.wait_ge(k_step, 8 * c + 8)

        phase.close()

        q_landed = sem("q_queries_landed")
        batch_copied = sem("q_batch_copied")
        row_scores = sem("q_row_scores_ready")
        row_max = sem("q_piece_max_ready")
        neg_ready = sem("q_neg_max_ready")
        max_turned = sem("q_max_turned")
        max_step = sem("q_max_split_step")
        max_landed = sem("q_max_rows_landed")
        col_scores = sem("q_col_scores_ready")
        exp_ready = sem("q_exps_ready")
        v_ready = sem("q_head_values_ready")
        out_mm = sem("q_head_out_ready")
        evacuated = sem("q_half_kept")
        inverted = sem("q_sums_inverted")
        NMAX = 3

        def hcount(b, h, per, k):
            return b * (HEADS * per) + (h * per + k)

        phase = ExitStack()
        block = phase.enter_context(nc.Block())

        @block.sync
        def _(sp):
            with sp.Fori(0, BATCH) as b:
                sp.wait_ge(out_mm, b * HEADS)
                for g in range(GROUPS):
                    src = parts_dram[bass.ds(b, 1), Q_PART[g]].rearrange("o (h j) t -> j (o h) t", j=HD)
                    sp.dma_start(q_all[g * HD:g * HD + HD, :, :], src).then_inc(q_landed, 16)
                with sp.Fori(0, HEADS) as h:
                    sp.wait_ge(max_step, hcount(b, h, 5, 5))
                    for k in range(3):
                        sp.dma_start(q_all[KROWS + k:KROWS + k + 1, bass.ds(h, 1), :],
                                     m_part[:, 0, k, :]).then_inc(max_landed, 16)

        @block.tensor
        def _(pe):
            with pe.Fori(0, BATCH) as b:
                pe.wait_ge(batch_copied, b * 3 + 3)
                pe.wait_ge(q_landed, b * (16 * GROUPS) + 16 * GROUPS)

                def row_piece(h, n):
                    i, lo, size, last = ROW_PIECES[n]
                    pe.wait_ge(row_max, hcount(b, h, NP1, max(n - 1, 0)))
                    ins = pe.matmul(s_bank[n % 2][:, 0:size], lhsT=q_all[:, bass.ds(h, 1), i * P:i * P + P],
                                    rhs=k_now[:, 0, lo:lo + size], start=True, stop=not last)
                    if last:
                        ins = pe.matmul(s_bank[n % 2][:, size - P:size], lhsT=ident16[:, :], rhs=mask_row[:, :], start=False,
                                        stop=True)
                    ins.then_inc(row_scores, 1)

                def turn(h, slot):
                    pe.wait_ge(neg_ready, hcount(b, h, NMAX, NMAX))
                    pe.transpose(m_bank[0:TILES, 0:P], neg_max[:, slot, :], ident).then_inc(max_turned, 1)

                def cols(h, slot, turn_next, rows_next):
                    pe.wait_ge(max_landed, hcount(b, h, 48, 48))
                    pe.wait_ge(v_ready, hcount(b, h, 1, 1))

                    def product(n):
                        j, lo, size = COL_PIECES[n]
                        pe.wait_ge(exp_ready, hcount(b, h, NP2, n + 1))
                        at = PROB_AT[j] + lo - j * P
                        return pe.matmul(o_bank[lo // CH][0:OUT_ROWS, lo % CH:lo % CH + size], lhsT=v_head[slot][:, j, :],
                                         rhs=probs[slot][:, at:at + size], start=False, stop=True, skip_group_check=True)

                    for n, (j, lo, size) in enumerate(COL_PIECES):
                        pe.wait_ge(exp_ready, hcount(b, h, NP2, max(n - 2, 0)))
                        first = lo == j * P
                        ins = pe.matmul(t_bank[n % 3][:, 0:size], lhsT=k_now[:, 1, j * P:j * P + P],
                                        rhs=q_all[:, bass.ds(h, 1), lo:lo + size], start=True, stop=not first)
                        if first:
                            ins = pe.matmul(t_bank[n % 3][:, 0:P], lhsT=ident16[:, :], rhs=mask_col[:, :], start=False, stop=True)
                        ins.then_inc(col_scores, 1)
                        if rows_next:
                            row_piece(h + 2, n)
                        if n == 1 and turn_next:
                            turn(h + 1, 1 - slot)
                        if n >= 2:
                            product(n - 2)
                    product(NP2 - 2)
                    product(NP2 - 1).then_inc(out_mm, 1)

                def begin(half):
                    pe.wait_ge(evacuated, b * 4 + 2 * half)
                    for s in range(2):
                        pe.matmul(o_bank[s][0:OUT_ROWS, :], lhsT=zeros16[:, 0:OUT_ROWS], rhs=zeros16[:, :], start=True, stop=True)

                for n in range(NP1):
                    row_piece(0, n)
                turn(0, 0)
                for n in range(NP1):
                    row_piece(1, n)
                begin(0)
                with pe.Fori(0, HALF_HEADS // 2) as g:
                    cols(g * 2, 0, True, True)
                    cols(g * 2 + 1, 1, True, True)
                begin(1)
                with pe.Fori(HALF_HEADS // 2, HEADS // 2 - 1) as g:
                    cols(g * 2, 0, True, True)
                    cols(g * 2 + 1, 1, True, True)
                cols(HEADS - 2, 0, True, False)
                cols(HEADS - 1, 1, False, False)

        @block.scalar
        def _(act):
            with act.Fori(0, BATCH) as b:
                act.wait_ge(out_mm, b * HEADS)
                for slot in range(2):
                    act.activation(k_now[:, slot, :], keys[:, slot, bass.ds(b * SEQ, SEQ)], ACT.Copy).then_inc(batch_copied, 1)
                for h in range(HALF_HEADS):
                    ins = act.activation(v_all[:, :, h * HD:h * HD + HD], vals[:, bass.ds(b * TILES, TILES), :], ACT.Copy)
                ins.then_inc(batch_copied, 1)

                def exps(h, slot):
                    for n, (j, lo, size) in enumerate(COL_PIECES):
                        act.wait_ge(col_scores, hcount(b, h, NP2, n + 1))
                        at = PROB_AT[j] + lo - j * P
                        act.activation(probs[slot][:, at:at + size], t_bank[n % 3][:, 0:size], ACT.Exp,
                                       scale=float(HD) ** -0.5).then_inc(exp_ready, 1)

                for half in range(2):
                    with act.Fori(half * HALF_HEADS // 2, (half + 1) * HALF_HEADS // 2) as g:
                        exps(g * 2, 0)
                        exps(g * 2 + 1, 1)
                    for s in range(2):
                        act.wait_ge(out_mm, b * HEADS + (half + 1) * HALF_HEADS)
                        act.activation(attended[half][0:OUT_ROWS, bass.ds(b * SEQ + s * CH, CH)], o_bank[s][0:OUT_ROWS, :],
                                       ACT.Copy).then_inc(evacuated, 1)

        @block.vector
        def _(dve):
            with dve.Fori(0, BATCH) as b:
                def reduces(h, first, end):
                    for n in range(first, end):
                        dve.wait_ge(row_scores, hcount(b, h, NP1, n + 1))
                        dve.tensor_reduce(piece_max[:, n:n + 1], s_bank[n % 2][:, 0:ROW_PIECES[n][2]], AX.X, ALU.max).then_inc(row_max, 1)

                def negate(h, slot):
                    dve.wait_ge(row_max, hcount(b, h, NP1, NP1))
                    dve.tensor_scalar(neg_max[:, slot, 0:4], piece_max[:, 0:4], -1.0, None, ALU.mult).then_inc(neg_ready, 1)
                    two = piece_max[:, 4:NP1].rearrange("p (i s) -> p i s", s=2)
                    dve.tensor_tensor(pair_max[:, 4:TILES], two[:, :, 0], two[:, :, 1], ALU.max).then_inc(neg_ready, 1)
                    dve.wait_ge(neg_ready, hcount(b, h, NMAX, 2))
                    dve.tensor_scalar(neg_max[:, slot, 4:TILES], pair_max[:, 4:TILES], -1.0, None, ALU.mult).then_inc(neg_ready, 1)

                def split(h, slot):
                    dve.wait_ge(max_turned, hcount(b, h, 1, 1))
                    dve.wait_ge(max_landed, hcount(b, h, 48, 0))
                    m, r, s = m_bank[0:TILES, 0:P], m_rest, m_part[:, 0]
                    dve.tensor_copy(s[:, 0, :], m).then_inc(max_step, 1)
                    dve.wait_ge(max_step, hcount(b, h, 5, 1))
                    dve.tensor_tensor(r[:, 0, :], m, s[:, 0, :], ALU.subtract).then_inc(max_step, 1)
                    dve.wait_ge(max_step, hcount(b, h, 5, 2))
                    dve.tensor_copy(s[:, 1, :], r[:, 0, :]).then_inc(max_step, 1)
                    dve.wait_ge(max_step, hcount(b, h, 5, 3))
                    dve.tensor_tensor(r[:, 1, :], r[:, 0, :], s[:, 1, :], ALU.subtract).then_inc(max_step, 1)
                    dve.wait_ge(max_step, hcount(b, h, 5, 4))
                    dve.tensor_copy(s[:, 2, :], r[:, 1, :]).then_inc(max_step, 1)

                def values(h, slot, of):
                    dve.wait_ge(out_mm, hcount(b, h, 1, -1))
                    dve.tensor_tensor(v_head[slot][:, :, :], v_all[:, :, :],
                                      head_cols[:, bass.ds(of, 1), :].to_broadcast([P, TILES, OUT_ROWS]), ALU.mult).then_inc(v_ready, 1)

                def step(h, slot, of_next, rows_next):
                    if rows_next:
                        reduces(h + 2, 0, 2)
                    split(h + 1, 1 - slot)
                    values(h + 1, 1 - slot, of_next)
                    if rows_next:
                        reduces(h + 2, 2, NP1)
                        negate(h + 2, slot)

                def invert(half):
                    for s in range(2):
                        dve.wait_ge(evacuated, b * 4 + (2 * half + s + 1))
                        sums = attended[half][HALF_ROWS:OUT_ROWS, bass.ds(b * SEQ + s * CH, CH)]
                        dve.reciprocal(sums, sums).then_inc(inverted, 1)

                reduces(0, 0, NP1)
                negate(0, 0)
                dve.wait_ge(batch_copied, b * 3 + 3)
                dve.tensor_tensor(v_head[0][:, :, :], v_all[:, :, :], head_cols[:, 0:1, :].to_broadcast([P, TILES, OUT_ROWS]),
                                  ALU.mult).then_inc(v_ready, 1)
                split(0, 0)
                reduces(1, 0, NP1)
                negate(1, 1)
                with dve.Fori(0, HALF_HEADS // 2) as g:
                    step(g * 2, 0, g * 2 + 1, True)
                    step(g * 2 + 1, 1, (g * 2 + 2) % HALF_HEADS, True)
                invert(0)
                with dve.Fori(HALF_HEADS // 2, HEADS // 2 - 1) as g:
                    step(g * 2, 0, g * 2 + (1 - HALF_HEADS), True)
                    step(g * 2 + 1, 1, g * 2 + (2 - HALF_HEADS), True)
                step(HEADS - 2, 0, HALF_HEADS - 1, False)
                invert(1)

        phase.close()
        sums_spread = sem("q_sums_spread")
        normed = sem("q_att_normed")
        proj = sem("q_out_projected")
        x1_step = sem("q_x1_step")
        block = mem.enter_context(nc.Block())

        @block.tensor
        def _(pe):
            for c in range(CHUNKS):
                for half in range(2):
                    if c >= 1:
                        pe.wait_ge(normed, 2 * (c - 1) + half + 1)
                    pe.matmul(s_bank[half][0:HALF_ROWS, :], lhsT=spread[:, :, :].rearrange("r h v -> r (h v)"),
                              rhs=attended[half][0:OUT_ROWS, c * CH:c * CH + CH], start=True, stop=True).then_inc(sums_spread, 1)
                if c >= 2:
                    pe.wait_ge(x1_step, c - 1)
                for half in range(2):
                    pe.wait_ge(normed, 2 * c + half + 1)
                    ins = pe.matmul(t_bank[c % 2][:, :], lhsT=w_out[:, half, :], rhs=att_n[:, c % 2, half, :], start=half == 0,
                                    stop=half == 1)
                ins.then_inc(proj, 1)

        @block.vector
        def _(dve):
            def project(c):
                dve.wait_ge(proj, c + 1)
                x1 = X1[:, c * CH:c * CH + CH]
                dve.scalar_tensor_tensor(x1, t_bank[c % 2][:, :], b_out[:, 0:1], X[:, c * CH:c * CH + CH], ALU.add, ALU.add).then_inc(x1_step, 1)

            for c in range(CHUNKS):
                for half in range(2):
                    dve.wait_ge(sums_spread, 2 * c + half + 1)
                    dve.tensor_tensor(att_n[:, c % 2, half, :], attended[half][0:HALF_ROWS, c * CH:c * CH + CH],
                                      s_bank[half][0:HALF_ROWS, :], ALU.mult).then_inc(normed, 1)
                if c >= 1:
                    project(c - 1)
            project(CHUNKS - 1)


DEPTH = 6
LH = 16
LD = 64
INNER = LH * LD
WINDOW = 32
FFI = 341
FF_BLOCKS = ((0, P), (P, P), (2 * P, FFI - 2 * P))
HG = 4
NG = LH // HG
QK_SCALE = 8.0
NORM_SCALE = 2.0 ** 20
LANES = 8 * LD


def head_of(g, j):
    return g // 2 * 8 + 2 * j + g % 2


PLACES = [head_of(g, j) for g in range(NG) for j in range(HG)]


def rotary_tables():
    f = np.float32
    half = np.arange(0, LD, 2, dtype=f)
    inv_freq = (f(1.0) / np.power(f(10000.0), half / f(LD))).astype(f)
    t = np.arange(SEQ, dtype=f)
    freqs = (t[:, None] * inv_freq[None, :]).astype(f)
    base = ((half + f(0.4 * LD)) / f(1.4 * LD)).astype(f)
    power = ((t - SEQ // 2) / f(WINDOW // 2)).astype(f)
    scale = np.power(base[None, :], power[:, None]).astype(f)
    cos, sin = np.cos(freqs).astype(f), np.sin(freqs).astype(f)
    inv = (f(1.0) / scale).astype(f)
    both = lambda a, b: np.concatenate([a, b], axis=1)
    tables = np.stack([both(cos * scale, cos * scale), both(-sin * scale, sin * scale),
                       both(cos * inv, cos * inv), both(-sin * inv, sin * inv)], axis=1)
    return np.ascontiguousarray(tables.reshape(TILES, P, 4, LD).transpose(1, 0, 2, 3).astype(f))


def local_layers(nc, sem, Xp, X1p, d, consts):
    ident, mean_w, eps = consts
    X, X1 = Xp[:, 1:], X1p[:, 1:]
    with ExitStack() as mem:
        def sb(label, shape, dt=F32):
            return mem.enter_context(nc.sbuf_tensor(f"d_{label}", shape, dt))

        def bank(label):
            return mem.enter_context(nc.psum_tensor(f"d_{label}", [P, CH], F32))

        w_qkv = sb("w_qkv", [P, 3 * INNER])
        w_o = sb("w_o", [P, INNER // P, DIM])
        w_1 = sb("w_1", [P, 2 * FFI])
        w_2 = sb("w_2", [P, 3, DIM])
        b_1 = sb("b_1", [P, 6])
        vec = sb("vectors", [P, 3])
        base = sb("rotary", [P, TILES, 4, LD])
        table = sb("scaled_rotary", [P, TILES, 4, LD])
        qk_scale = sb("qk_scale", [P, 4, LD])
        ident16 = sb("ident16", [P, P], BF16)
        mask = sb("mask", [P, HG, P], BF16)
        mask_prev = sb("mask_prev", [WINDOW, LH, WINDOW], BF16)
        mask_now = sb("mask_now", [WINDOW, LH, WINDOW], BF16)
        shown = sb("shown", [P, NT])
        hidden = sb("hidden", [P, NT])
        norm_bias = sb("norm_bias", [P, 1])
        xs = [sb(f"x{i}", [P, P]) for i in range(2)]
        sq = sb("squares", [P, 2, 8, LD])
        t1 = sb("rotated1", [P, 4, 8, LD])
        t2 = sb("rotated2", [P, 4, 8, LD])
        ssq = sb("square_sums", [P, 4 * 8])
        ssq_c = sb("square_sums_guarded", [P, 4 * 8])
        ssq_l = sb("square_sums_log", [P, 4 * 8])
        inv_n = sb("inverse_norms", [P, 4 * 8])
        q_t = sb("q_turned", [P, LH // 2, P])
        k_t = [sb(f"k_turned{i}", [P, LH // 2, P]) for i in range(2)]
        v = [sb(f"v{i}", [P, LH, LD]) for i in range(2)]
        v_prev = [sb(f"v_prev{i}", [P, NG, HG, LD]) for i in range(2)]
        top = sb("top", [P, LH])
        top_prev = sb("top_prev", [WINDOW, LH])
        z = sb("exps", [P, NG, HG, P])
        z_prev = sb("exps_prev", [WINDOW, LH, WINDOW])
        pt = sb("probs_turned", [P, NG, HG, P])
        pt_prev = sb("probs_turned_prev", [P, NG, WINDOW])
        sums = sb("sums", [P, LH])
        sums_prev = sb("sums_prev", [WINDOW, LH])
        inv_s = sb("inverse_sums", [P, LH])
        att_t = sb("attended_turned", [P, INNER // P, P])
        flat = lambda t: t[:, :, :, :].rearrange("p a b c -> p (a b c)")
        f1, f2 = flat(t1), flat(t2)
        fx = [f1[:, i * CH:i * CH + CH] for i in range(2)]
        fc = [f1[:, (2 + i) * CH:(3 + i) * CH] for i in range(2)]
        fq = [f2[:, i * CH:i * CH + CH] for i in range(2)]
        fl = [f2[:, (2 + i) * CH:(3 + i) * CH] for i in range(2)]
        zf, pf = flat(z), flat(pt)
        fr = [zf[:, i * CH:i * CH + CH] for i in range(2)]
        fn = [zf[:, (2 + i) * CH:(3 + i) * CH] for i in range(2)]
        gl = [pf[:, i * CH:i * CH + CH] for i in range(2)]
        hh = [pf[:, (2 + i) * CH:(3 + i) * CH] for i in range(2)]
        hh += [flat(table)[:, 0:CH]]
        s_b = [bank(f"s_bank{i}") for i in range(3)]
        p_b = [bank(f"p_bank{i}") for i in range(2)]
        t_b = [bank(f"t_bank{i}") for i in range(2)]
        w_b = bank("w_bank")
        rotary = nc.inline_tensor(rotary_tables(), "rotary_tables").ap()
        kept_x = nc.dram_tensor("x_before_local", (P, TOKENS), F32, kind="Internal").ap()

        setup = sem("d_setup")
        setup_loads = sem("d_setup_loads")
        x_stored = sem("d_x_stored")
        qkv_loaded = sem("d_qkv_loaded")
        ffn_loaded = sem("d_ffn_loaded")
        table_step = sem("d_table_step")
        x_ready = sem("d_x_ready")
        proj = sem("d_projected")
        sq_ready = sem("d_squares_ready")
        rope_ready = sem("d_rope_ready")
        rope_sum = sem("d_rope_sum_ready")
        ssq_step = sem("d_square_sum_step")
        inv_step = sem("d_inverse_norm_step")
        q_unit = sem("d_unit_queries_ready")
        k_unit = sem("d_unit_keys_ready")
        v_kept = sem("d_v_kept")
        vp_landed = [sem(f"d_v_prev_landed{i}") for i in range(2)]
        qk_turned = sem("d_qk_turned")
        mask_ready = sem("d_mask_ready")
        even_done = sem("d_even_heads_done")
        scores = sem("d_scores_ready")
        max_step = sem("d_max_step")
        sub_ready = sem("d_less_max_ready")
        exp_ready = sem("d_exps_ready")
        sum_step = sem("d_sum_step")
        p_norm = sem("d_probs_normed")
        p_turned = sem("d_probs_turned")
        pp_turned = sem("d_prev_probs_turned")
        pp_kept = sem("d_prev_probs_kept")
        attended = sem("d_attended_ready")
        kept = sem("d_t_bank_kept")
        o_mm = sem("d_out_projected")
        x1_ready = sem("d_x1_ready")
        f_x = sem("d_ff_x_ready")
        f_mean = sem("d_ff_mean_ready")
        f_cent = sem("d_ff_centred_ready")
        f_sq = sem("d_ff_squares_ready")
        f_var = sem("d_ff_variance_ready")
        f_log = sem("d_ff_variance_log_ready")
        f_rstd = sem("d_ff_rstd_ready")
        f_norm = sem("d_ff_normed_step")
        f_gate = sem("d_ff_gate_ready")
        f_lin = sem("d_ff_linear_ready")
        f_gelu = sem("d_ff_gelu_ready")
        f_prod = sem("d_ff_product_ready")
        f_out = sem("d_ff_out_ready")
        f_done = sem("d_ff_chunk_done")
        b_step = sem("d_ff_bias_step")
        CHUNKS = TOKENS // CH
        TILE_JOBS = NG + 2 + 4
        LAYER_JOBS = NT * TILE_JOBS
        STEPS = NT
        QKV_LOADS = 16 * 3
        FFN_LOADS = 16 * 6

        with nc.Block() as block:
            @block.sync
            def _(sp):
                sp.dma_start(base[:, :, :, :], rotary).then_inc(setup_loads, 16)
                sp.dma_start(kept_x, X[:, 0:TOKENS]).then_inc(x_stored, 16)
                sp.wait_ge(setup_loads, 16)
                sp.wait_ge(x_stored, 16)

            @block.gpsimd
            def _(pool):
                step = [0]

                def after(ins):
                    ins.then_inc(setup, 1)
                    step[0] += 1
                    pool.wait_ge(setup, step[0])

                after(pool.memset(mask[:, :, :], 0.0))
                after(pool.affine_select(out=mask[:, :, :], in_=mask[:, :, :], pattern=[[0, HG], [-1, P]], compare_op=ALU.is_ge,
                                         fill=MASKED, base=0, channel_multiplier=1))
                after(pool.affine_select(out=mask[:, :, :], in_=mask[:, :, :], pattern=[[0, HG], [1, P]], compare_op=ALU.is_ge,
                                         fill=MASKED, base=WINDOW, channel_multiplier=-1))
                after(pool.memset(mask_prev[:, :, :], 0.0))
                after(pool.affine_select(out=mask_prev[:, :, :], in_=mask_prev[:, :, :], pattern=[[0, LH], [1, WINDOW]],
                                         compare_op=ALU.is_ge, fill=MASKED, base=0, channel_multiplier=-1))

            @block.vector
            def _(dve):
                dve.memset(shown[:, :], 1.0)
                dve.memset(hidden[:, :], 0.0)
                dve.memset(norm_bias[:, :], float(0.5 * np.log(NORM_SCALE)))
                for i in range(2):
                    dve.memset(v_prev[i][:, :, :, :], 0.0)
                    dve.memset(k_t[i][:, :, :], 0.0)
                dve.memset(Xp[:, 0:1], 0.0)
                dve.memset(X1p[:, 0:1], 0.0)
                dve.tensor_copy(ident16[:, :], ident).then_inc(table_step, 1)
                dve.wait_ge(table_step, 1)
                for b in range(BATCH):
                    dve.memset(shown[:, b * TILES:b * TILES + 1], 0.0)
                    ins = dve.memset(hidden[:, b * TILES:b * TILES + 1], MASKED)
                ins.then_inc(table_step, 1)

        def cnt(t, per, k):
            return t * per + k

        layers = ExitStack()
        block = layers.enter_context(nc.Block())

        @block.sync
        def _(sp):
            def attention_weights(one):
                sp.dma_start(w_qkv[:, :], d["d_wqkv"][one].rearrange("o p n -> p (o n)")).then_inc(qkv_loaded, 16)
                sp.dma_start(w_o[:, :, :], d["d_wo"][one].rearrange("o (k p) n -> p (o k) n", p=P)).then_inc(qkv_loaded, 16)
                sp.dma_start(qk_scale[:, :, :], d["d_scales"][one].rearrange("o p s n -> p (o s) n")).then_inc(qkv_loaded, 16)

            def layer(L):
                sp.wait_ge(f_done, L * CHUNKS)
                one = bass.ds(L, 1)
                sp.dma_start(b_1[:, :], d["d_b1"][one].rearrange("o p n -> p (o n)")).then_inc(ffn_loaded, 16)
                sp.dma_start(vec[:, :], d["d_ln"][one].rearrange("o p n -> p (o n)")).then_inc(ffn_loaded, 16)
                sp.dma_start(w_1[:, :], d["d_w1"][one].rearrange("o p n -> p (o n)")).then_inc(ffn_loaded, 16)
                for n, (lo, size) in enumerate(FF_BLOCKS):
                    sp.dma_start(w_2[0:size, n, :], d["d_w2"][one, lo:lo + size].rearrange("o p n -> p (o n)")).then_inc(ffn_loaded, 16)

                def prev_values(t, par):
                    sp.wait_ge(v_kept, cnt(t - 1, 2, 2))
                    sp.wait_ge(attended, t * 2 - 2)
                    src = v[1 - par][P - WINDOW:P, :, :].rearrange("p (g j) c -> p g j c", j=HG)
                    for j in range(HG):
                        sp.dma_start(v_prev[par][j * WINDOW:j * WINDOW + WINDOW, :, j, :], src[:, :, j, :]).then_inc(vp_landed[par], 16)

                prev_values(L * STEPS + 1, 1)
                with sp.Fori(1, NT // 2) as g:
                    prev_values(L * STEPS + g * 2, 0)
                    prev_values(L * STEPS + g * 2 + 1, 1)

            attention_weights(slice(0, 1))
            with sp.Fori(0, DEPTH - 1) as L:
                layer(L)
                sp.wait_ge(x1_ready, L * STEPS + STEPS)
                attention_weights(bass.ds(L + 1, 1))
            layer(DEPTH - 1)

        @block.gpsimd
        def _(pool):
            def add(L, i, n):
                t = L * STEPS + i
                pool.wait_ge(rope_ready, cnt(t, 4, n + 1))
                pool.tensor_tensor(t1[:, n, :, :], t1[:, n, :, :], t2[:, n, :, :], ALU.add).then_inc(rope_sum, 1)

            def unit(t, n):
                pool.wait_ge(inv_step, cnt(t, 2, 2))
                pool.wait_ge(rope_sum, cnt(t, 4, n + 1))
                pool.tensor_tensor(t1[:, n, :, :], t1[:, n, :, :], inv_n[:, 8 * n:8 * n + 8].unsqueeze(2).to_broadcast([P, 8, LD]),
                                   ALU.mult).then_inc(k_unit, 1)

            def normalise(t):
                pool.wait_ge(sum_step, t * 3 + 3)
                for g in range(NG):
                    pool.tensor_tensor(z[:, g, :, :], z[:, g, :, :], inv_s[:, g * HG:g * HG + HG].unsqueeze(2).to_broadcast([P, HG, P]),
                                       ALU.mult).then_inc(p_norm, 1)
                pool.tensor_tensor(z_prev[:, :, :], z_prev[:, :, :],
                                   inv_s[0:WINDOW, :].unsqueeze(2).to_broadcast([WINDOW, LH, WINDOW]), ALU.mult).then_inc(p_norm, 1)

            with pool.Fori(0, DEPTH) as L:
                for n in range(4):
                    add(L, 0, n)
                for n in range(2, 4):
                    unit(L * STEPS, n)
                with pool.Fori(1, NT) as i:
                    for n in range(4):
                        add(L, i, n)
                    for n in range(2, 4):
                        unit(L * STEPS + i, n)
                    normalise(L * STEPS + i - 1)
                normalise(L * STEPS + (NT - 1))

        def half(n):
            return t1[:, n, :, :].rearrange("p h c -> p (h c)")

        @block.tensor
        def _(pe):
            def project(t, par, n):
                if n == 0:
                    pe.wait_ge(x_ready, cnt(t, 2, 2))
                    pe.wait_ge(v_kept, t * 2)
                elif n >= 2:
                    pe.wait_ge(rope_ready, cnt(t, 4, n - 1))
                pe.matmul(p_b[n % 2][:, :], lhsT=xs[par][:, :], rhs=w_qkv[:, n * LANES:n * LANES + LANES], start=True,
                          stop=True).then_inc(proj, 1)

            def turn_qk(t, n, job):
                if n < 2:
                    pe.wait_ge(q_unit, cnt(t, 2, n + 1))
                else:
                    pe.wait_ge(k_unit, cnt(t, 2, n - 1))
                free_bank(job)
                for j in range(4):
                    ins = pe.transpose(t_b[n % 2][:, j * P:j * P + P], half(n)[:, j * P:j * P + P], ident)
                ins.then_inc(qk_turned, 1)

            def free_bank(job):
                if job is not None:
                    pe.wait_ge(kept, job - 1)

            def score(t, par, g, even=False):
                if g >= 2:
                    pe.wait_ge(sub_ready, cnt(t, 5, g - 1))
                b = s_b[g % 2]
                for j in range(HG):
                    h = head_of(g, j)
                    lo = (h % 2) * LD
                    pe.matmul(b[:, j * P:j * P + P], lhsT=q_t[lo:lo + LD, h // 2, :], rhs=k_t[par][lo:lo + LD, h // 2, :],
                              start=j == 0, stop=False, skip_group_check=True)
                if even:
                    pe.wait_ge(even_done, t + 1)
                pe.matmul(b[:, :], lhsT=ident16[:, :], rhs=mask[:, :, :].rearrange("p h c -> p (h c)"), start=False,
                          stop=True, skip_group_check=True).then_inc(scores, 1)

            def add_prev(par, odd):
                lo = odd * LD
                for g in (odd, 2 + odd):
                    for j in range(HG):
                        c = (g * HG + j) * WINDOW
                        h = head_of(g, j)
                        ins = pe.matmul(s_b[2][0:WINDOW, c:c + WINDOW], lhsT=q_t[lo:lo + LD, h // 2, 0:WINDOW],
                                        rhs=k_t[1 - par][lo:lo + LD, h // 2, P - WINDOW:P], start=c == 0, stop=False,
                                        skip_group_check=True)
                return ins

            def first_scores(t, par, masks, jobs):
                pe.wait_ge(kept, jobs)
                if par == 0:
                    pe.wait_ge(mask_ready, masks)
                pe.wait_ge(sub_ready, t * 5)
                score(t, par, 0)
                add_prev(par, 0).then_inc(even_done, 1)
                score(t, par, 1, even=True)
                add_prev(par, 1)
                m = mask_now if par == 0 else mask_prev
                pe.matmul(s_b[2][0:WINDOW, :], lhsT=ident16[0:WINDOW, 0:WINDOW], rhs=m[:, :, :].rearrange("p h c -> p (h c)"),
                          start=False, stop=True, skip_group_check=True).then_inc(scores, 1)

            def turn_probs(t, n, job):
                if n == NG - 1:
                    pe.wait_ge(x1_ready, t)
                    pe.wait_ge(p_norm, t * 5 + 5)
                else:
                    pe.wait_ge(p_norm, cnt(t, 5, n + 1))
                free_bank(job)
                for j in range(HG):
                    ins = pe.transpose(t_b[n % 2][:, j * P:j * P + P], z[:, n, j, :], ident)
                ins.then_inc(p_turned, 1)
                if n == NG - 1:
                    zp = z_prev[:, :, :].rearrange("p (g j) c -> p g (j c)", j=HG)
                    for g in range(NG):
                        ins = pe.transpose(w_b[:, P + g * WINDOW:P + (g + 1) * WINDOW], zp[:, g, :], ident[0:WINDOW, 0:WINDOW])
                    ins.then_inc(pp_turned, 1)

            def attend(t, par, n, landed, job):
                if n == 0:
                    pe.wait_ge(pp_kept, t + 1)
                    pe.wait_ge(v_kept, cnt(t, 2, 2))
                    pe.wait_ge(vp_landed[par], landed)
                pe.wait_ge(kept, job)
                for p in range(8 * n, 8 * n + 8):
                    g, j = p // HG, p % HG
                    lo, c = p % 2 * LD, (p - 8 * n) // 2 * P
                    pe.matmul(t_b[n][lo:lo + LD, c:c + WINDOW], lhsT=v_prev[par][:, g, j, :], rhs=pt_prev[:, g, :],
                              start=p < 8 * n + 2, stop=False, skip_group_check=True)
                    ins = pe.matmul(t_b[n][lo:lo + LD, c:c + P], lhsT=v[par][:, p, :], rhs=pt[:, g, j, :], start=False, stop=True,
                                    skip_group_check=True)
                ins.then_inc(attended, 1)

            def project_out(t, jobs):
                pe.wait_ge(kept, jobs)
                pe.wait_ge(x1_ready, t)
                for j in range(INNER // P):
                    ins = pe.matmul(w_b[:, 0:P], lhsT=w_o[:, j, :], rhs=att_t[:, j, :], start=j == 0, stop=j == INNER // P - 1)
                ins.then_inc(o_mm, 1)

            def step(L, i, par, has_c, has_a, landed_c, even, job):
                t = L * STEPS + i
                if has_a:
                    project(t + 1, 1 - par, 0)
                    project(t + 1, 1 - par, 1)
                first_scores(t, par, even, job)
                if has_c:
                    turn_probs(t - 1, 0, job)
                    turn_probs(t - 1, 1, job + 1)
                if has_a:
                    project(t + 1, 1 - par, 2)
                if has_c:
                    turn_probs(t - 1, 2, job + 2)
                    turn_probs(t - 1, 3, job + 3)
                if has_a:
                    project(t + 1, 1 - par, 3)
                score(t, par, 2)
                if has_c:
                    attend(t - 1, 1 - par, 0, landed_c, job + 4)
                score(t, par, 3)
                if has_c:
                    attend(t - 1, 1 - par, 1, landed_c, job + 4)
                if has_a:
                    project(t + 1, 1 - par, 4)
                if has_c:
                    project_out(t - 1, job + 6)
                if has_a:
                    job = job + (6 if has_c else 0)
                    turn_qk(t + 1, 0, job)
                    turn_qk(t + 1, 1, job + 1)
                    project(t + 1, 1 - par, 5)
                    turn_qk(t + 1, 2, job + 2)
                    turn_qk(t + 1, 3, job + 3)

            with pe.Fori(0, DEPTH) as L:
                pe.wait_ge(qkv_loaded, L * QKV_LOADS + QKV_LOADS)
                job = L * LAYER_JOBS
                for n in range(6):
                    project(L * STEPS, 0, n)
                for n in range(4):
                    turn_qk(L * STEPS, n, job + n if n >= 2 else None)

                step(L, 0, 0, False, True, None, L * NT + 2, job + 4)
                with pe.Fori(0, NT // 2 - 1) as g:
                    step(L, g * 2 + 1, 1, True, True, L * (64 * (NT // 2 - 1)) + g * 64, None,
                         L * LAYER_JOBS + (g * (2 * TILE_JOBS) + 8))
                    step(L, g * 2 + 2, 0, True, True, L * (64 * (NT // 2)) + (g * 64 + 64), L * NT + (g * 2 + 4),
                         L * LAYER_JOBS + (g * (2 * TILE_JOBS) + 8 + TILE_JOBS))
                step(L, NT - 1, 1, True, False, L * (64 * (NT // 2 - 1)) + 64 * (NT // 2 - 1), None, job + (LAYER_JOBS - 12))
                t_last, job = L * STEPS + (NT - 1), L * LAYER_JOBS + (LAYER_JOBS - 6)
                for n in range(NG):
                    turn_probs(t_last, n, job + n)
                for n in range(2):
                    attend(t_last, 1, n, L * (64 * (NT // 2)) + 64 * (NT // 2), job + 4)
                project_out(t_last, job + 6)

                with pe.Fori(0, CHUNKS // 2) as g:
                    n = L * CHUNKS + g * 2
                    for s in range(2):
                        pe.wait_ge(f_x, n + (s + 1))
                        pe.wait_ge(f_cent, n)
                        pe.matmul(p_b[s][:, :], lhsT=mean_w, rhs=fx[s], start=True, stop=True).then_inc(f_mean, 1)
                    for s in range(2):
                        pe.wait_ge(f_sq, n + (s + 1))
                        pe.wait_ge(f_log, n)
                        pe.matmul(t_b[s][:, :], lhsT=mean_w, rhs=fq[s], start=True, stop=True).then_inc(f_var, 1)

                def feed(c, s):
                    n = L * CHUNKS + c
                    pe.wait_ge(ffn_loaded, L * FFN_LOADS + FFN_LOADS)
                    pe.wait_ge(f_norm, L * (CHUNKS * 2) + CHUNKS * 2)
                    x = X[:, bass.ds(c * CH, CH)]
                    for m, (lo, size) in enumerate(FF_BLOCKS):
                        pe.wait_ge(f_gelu, n * 3 + max(m - 1, 0))
                        pe.matmul(s_b[m % 2][0:size, :], lhsT=w_1[:, FFI + lo:FFI + lo + size], rhs=x, start=True,
                                  stop=True).then_inc(f_gate, 1)
                        pe.wait_ge(f_prod, n * 3 + max(m - 1, 0))
                        pe.matmul(p_b[m % 2][0:size, :], lhsT=w_1[:, lo:lo + size], rhs=x, start=True, stop=True).then_inc(f_lin, 1)
                    pe.wait_ge(f_done, n)
                    for m, (lo, size) in enumerate(FF_BLOCKS):
                        pe.wait_ge(f_prod, n * 3 + m + 1)
                        ins = pe.matmul(t_b[s][:, :], lhsT=w_2[0:size, m, :], rhs=hh[m][0:size, :], start=m == 0, stop=m == 2)
                    ins.then_inc(f_out, 1)

                with pe.Fori(0, CHUNKS // 2) as g:
                    feed(g * 2, 0)
                    feed(g * 2 + 1, 1)

        @block.scalar
        def _(act):
            def take(L, i, par, first=False):
                t = L * STEPS + i
                if first:
                    act.wait_ge(f_done, L * CHUNKS)
                act.wait_ge(proj, t * 6 if first else cnt(t, 6, -6))
                act.activation(xs[par][0:64, :], X[0:64, bass.ds(i * P, P)], ACT.Copy)
                act.activation(xs[par][64:P, :], Xp[64:P, bass.ds(i * P, P)], ACT.Copy).then_inc(x_ready, 1)
                act.wait_ge(x_ready, cnt(t, 2, 1))
                act.activation(xs[par][64:P, 0:1], xs[par][64:P, 0:1], ACT.Identity, scale=shown[64:P, bass.ds(i, 1)]).then_inc(x_ready, 1)

            def mask_for(L, i):
                act.wait_ge(scores, cnt(L * STEPS + i, 5, -5))
                act.activation(mask_now[:, :, :], mask_prev[:, :, :], ACT.Identity, bias=hidden[0:WINDOW, bass.ds(i, 1)]).then_inc(mask_ready, 1)

            def keys_for(L, i):
                act.wait_ge(scores, cnt(L * STEPS + i, 5, 0))
                before = k_t[1][:, :, P - WINDOW:P]
                act.activation(before, before, ACT.Identity, scale=shown[:, bass.ds(i, 1)]).then_inc(mask_ready, 1)

            def square(t, n):
                act.wait_ge(proj, cnt(t, 6, n + 1))
                act.wait_ge(ssq_step, cnt(t, 5, max(n - 1, 0)))
                act.activation(sq[:, n % 2, :, :].rearrange("p h c -> p (h c)"), p_b[n % 2][:, :], ACT.Square).then_inc(sq_ready, 1)

            def values(t, par, n, landed=None):
                if landed is not None:
                    act.wait_ge(vp_landed[1 - par], landed)
                act.wait_ge(proj, cnt(t, 6, n + 5))
                act.activation(v[par][:, 8 * n:8 * n + 8, 0:LD], p_b[n % 2][:, :].rearrange("p (h c) -> p h c", c=LD),
                               ACT.Copy).then_inc(v_kept, 1)

            def inverse_norms(t):
                act.wait_ge(ssq_step, cnt(t, 5, 5))
                act.activation(ssq_l[:, :], ssq_c[:, :], ACT.Ln, scale=NORM_SCALE).then_inc(inv_step, 1)
                act.wait_ge(inv_step, cnt(t, 2, 1))
                act.activation(inv_n[:, :], ssq_l[:, :], ACT.Exp, scale=-0.5, bias=norm_bias[:, 0:1]).then_inc(inv_step, 1)

            def keep_qk(t, par, n):
                act.wait_ge(qk_turned, cnt(t, 4, n + 1))
                dst = (q_t if n < 2 else k_t[par])[:, 4 * (n % 2):4 * (n % 2) + 4, :]
                act.activation(dst.rearrange("p j c -> p (j c)"), t_b[n % 2][:, :], ACT.Copy).then_inc(kept, 1)

            def exps(t, n):
                act.wait_ge(sub_ready, cnt(t, 5, n + 1))
                for j in range(HG):
                    p = n * HG + j
                    ins = act.activation(z[:, n, j, :], z[:, n, j, :], ACT.Exp, scale=QK_SCALE, accum_out=sums[:, p:p + 1])
                ins.then_inc(exp_ready, 1)

            def exps_prev(t):
                act.wait_ge(sub_ready, cnt(t, 5, 5))
                e = z_prev[:, :, :].rearrange("p h c -> p (h c)")
                act.activation(e, e, ACT.Exp, scale=QK_SCALE).then_inc(exp_ready, 1)

            def keep_probs(t, n):
                act.wait_ge(p_turned, cnt(t, 4, n + 1))
                act.activation(pt[:, n, :, :].rearrange("p h c -> p (h c)"), t_b[n % 2][:, :], ACT.Copy).then_inc(kept, 1)

            def keep_prev_probs(t):
                act.wait_ge(pp_turned, t + 1)
                act.activation(pt_prev[:, :, :], w_b[:, P:2 * P].rearrange("p (g c) -> p g c", c=WINDOW), ACT.Copy).then_inc(pp_kept, 1)

            def keep_attended(t, n):
                act.wait_ge(attended, cnt(t, 2, n + 1))
                act.activation(att_t[:, 4 * n:4 * n + 4, :].rearrange("p j c -> p (j c)"), t_b[n][:, :], ACT.Copy).then_inc(kept, 1)

            def step(L, i, par, has_c, has_a, takes, landed):
                t = L * STEPS + i
                if has_a:
                    square(t + 1, 0)
                    square(t + 1, 1)
                if has_c:
                    keep_probs(t - 1, 0)
                    keep_probs(t - 1, 1)
                if has_a:
                    square(t + 1, 2)
                if has_c:
                    keep_probs(t - 1, 2)
                    keep_probs(t - 1, 3)
                    keep_prev_probs(t - 1)
                if has_a:
                    square(t + 1, 3)
                exps(t, 0)
                exps(t, 1)
                if has_c:
                    keep_attended(t - 1, 0)
                if takes:
                    take(L, i + 2, par)
                if has_a:
                    if par == 1:
                        mask_for(L, i + 1)
                    inverse_norms(t + 1)
                if has_c:
                    keep_attended(t - 1, 1)
                exps(t, 2)
                exps(t, 3)
                if has_a:
                    for n in range(2):
                        keep_qk(t + 1, 1 - par, n)
                exps_prev(t)
                if has_a:
                    values(t + 1, 1 - par, 0, landed)
                    values(t + 1, 1 - par, 1)
                    for n in range(2, 4):
                        keep_qk(t + 1, 1 - par, n)
                    if par == 1:
                        keys_for(L, i + 1)

            act.preload_act_table_set("natural_log_exp_and_others")
            with act.Fori(0, DEPTH) as L:
                act.preload_act_table_set("natural_log_exp_and_others")
                t = L * STEPS
                take(L, 0, 0, first=True)
                act.wait_ge(f_done, L * CHUNKS)
                act.activation(mask_now[:, :, :], mask_prev[:, :, :], ACT.Identity, bias=hidden[0:WINDOW, 0:1]).then_inc(mask_ready, 1)
                keys_for(L, 0)
                take(L, 1, 1)
                for n in range(4):
                    square(t, n)
                for n in range(2):
                    values(t, 0, n)
                inverse_norms(t)
                for n in range(4):
                    keep_qk(t, 0, n)
                odd, even = L * (64 * (NT // 2)), L * (64 * (NT // 2 - 1))
                step(L, 0, 0, False, True, True, None)
                with act.Fori(0, NT // 2 - 2) as g:
                    step(L, g * 2 + 1, 1, True, True, True, odd + (g * 64 + 64))
                    step(L, g * 2 + 2, 0, True, True, True, even + (g * 64 + 64))
                step(L, NT - 3, 1, True, True, True, odd + 64 * (NT // 2 - 1))
                step(L, NT - 2, 0, True, True, False, even + 64 * (NT // 2 - 1))
                step(L, NT - 1, 1, True, False, False, None)
                t_last = L * STEPS + (NT - 1)
                for n in range(NG):
                    keep_probs(t_last, n)
                keep_prev_probs(t_last)
                for n in range(2):
                    keep_attended(t_last, n)
                act.wait_ge(x1_ready, L * STEPS + STEPS)

                def shifted(c):
                    n = L * CHUNKS + c
                    for s in range(2):
                        act.wait_ge(f_cent, n)
                        act.activation(fx[s][0:64, :], X1[0:64, bass.ds((c + s) * CH, CH)], ACT.Copy)
                        act.activation(fx[s][64:P, :], X1p[64:P, bass.ds((c + s) * CH, CH)], ACT.Copy).then_inc(b_step, 1)
                    for s in range(2):
                        act.wait_ge(b_step, n + (s + 1))
                        act.activation(fx[s][64:P, 0:1], fx[s][64:P, 0:1], ACT.Identity,
                                       scale=shown[64:P, bass.ds((c + s) * 4, 1)]).then_inc(f_x, 1)

                def norm_pair(c, last):
                    n = L * CHUNKS + c
                    for s in range(2):
                        act.wait_ge(f_cent, n + (s + 1))
                        act.activation(fq[s], fc[s], ACT.Square).then_inc(f_sq, 1)
                    if not last:
                        shifted(c + 2)
                    for s in range(2):
                        act.wait_ge(f_var, n + (s + 1))
                        act.activation(fl[s], t_b[s][:, :], ACT.Ln, bias=eps).then_inc(f_log, 1)
                    for s in range(2):
                        act.wait_ge(f_log, n + (s + 1))
                        act.wait_ge(f_norm, n * 2)
                        act.activation(fr[s], fl[s], ACT.Exp, scale=-0.5).then_inc(f_rstd, 1)

                shifted(0)
                with act.Fori(0, CHUNKS // 2 - 1) as g:
                    norm_pair(g * 2, False)
                norm_pair(CHUNKS - 2, True)

                def feed(c, s):
                    n = L * CHUNKS + c
                    for m, (lo, size) in enumerate(FF_BLOCKS):
                        act.wait_ge(f_gate, n * 3 + m + 1)
                        act.wait_ge(f_prod, n * 3 + max(m - 1, 0))
                        act.activation(gl[m % 2][0:size, :], s_b[m % 2][0:size, :], ACT.Gelu, bias=b_1[0:size, 3 + m:4 + m]).then_inc(f_gelu, 1)

                act.preload_act_table(ACT.Gelu)
                with act.Fori(0, CHUNKS // 2) as g:
                    feed(g * 2, 0)
                    feed(g * 2 + 1, 1)

        @block.vector
        def _(dve):
            def rope(t, i8, n):
                dve.wait_ge(sq_ready, cnt(t, 4, n + 1))
                x = p_b[n % 2][:, :].rearrange("p (h c) -> p h c", c=LD)
                which = 0 if n < 2 else 2
                cos = table[:, bass.ds(i8, 1), which, :].to_broadcast([P, 8, LD])
                sin = table[:, bass.ds(i8, 1), which + 1, :]
                dve.tensor_tensor(t1[:, n, :, :], x, cos, ALU.mult)
                H = LD // 2
                dve.tensor_tensor(t2[:, n, :, 0:H], x[:, :, H:LD], sin[:, :, 0:H].to_broadcast([P, 8, H]), ALU.mult)
                dve.tensor_tensor(t2[:, n, :, H:LD], x[:, :, 0:H], sin[:, :, H:LD].to_broadcast([P, 8, H]), ALU.mult).then_inc(rope_ready, 1)

            def square_sum(t, n):
                dve.tensor_reduce(ssq[:, 8 * n:8 * n + 8], sq[:, n % 2, :, :], AX.X, ALU.add).then_inc(ssq_step, 1)

            def guard(t):
                dve.wait_ge(ssq_step, cnt(t, 5, 4))
                dve.tensor_scalar(ssq_c[:, :], ssq[:, :], 1e-24, None, ALU.max).then_inc(ssq_step, 1)

            def unit(t, n):
                if n == 0:
                    dve.wait_ge(inv_step, cnt(t, 2, 2))
                dve.wait_ge(rope_sum, cnt(t, 4, n + 1))
                dve.tensor_tensor(t1[:, n, :, :], t1[:, n, :, :], inv_n[:, 8 * n:8 * n + 8].unsqueeze(2).to_broadcast([P, 8, LD]),
                                  ALU.mult).then_inc(q_unit, 1)

            def max_prev(t):
                dve.wait_ge(scores, cnt(t, 5, 3))
                dve.tensor_reduce(top_prev[:, :], s_b[2][0:WINDOW, :].rearrange("p (h c) -> p h c", c=WINDOW), AX.X,
                                  ALU.max).then_inc(max_step, 1)

            def less_max(t, g, prior):
                dve.wait_ge(scores, cnt(t, 5, g + 2 if g >= 2 else g + 1))
                if prior:
                    dve.wait_ge(p_turned, cnt(t - 1, 4, g + 1))
                s = s_b[g % 2][:, :].rearrange("p (h c) -> p h c", c=P)
                hs = slice(g * HG, g * HG + HG)
                dve.tensor_reduce(top[:, hs], s, AX.X, ALU.max).then_inc(max_step, 1)
                dve.wait_ge(max_step, cnt(t, 9, 2 + 2 * g))
                dve.tensor_tensor(top[0:WINDOW, hs], top[0:WINDOW, hs], top_prev[:, hs], ALU.max).then_inc(max_step, 1)
                dve.wait_ge(max_step, cnt(t, 9, 3 + 2 * g))
                dve.tensor_tensor(z[:, g, :, :], s, top[:, hs].unsqueeze(2).to_broadcast([P, HG, P]), ALU.subtract).then_inc(sub_ready, 1)

            def less_max_prev(t):
                dve.wait_ge(pp_turned, t)
                s = s_b[2][0:WINDOW, :].rearrange("p (h c) -> p h c", c=WINDOW)
                dve.tensor_tensor(z_prev[:, :, :], s, top[0:WINDOW, :].unsqueeze(2).to_broadcast([WINDOW, LH, WINDOW]),
                                  ALU.subtract).then_inc(sub_ready, 1)

            def inverse_sums(t):
                dve.wait_ge(exp_ready, t * 5 + 5)
                dve.tensor_reduce(sums_prev[:, :], z_prev[:, :, :], AX.X, ALU.add).then_inc(sum_step, 1)
                dve.wait_ge(sum_step, cnt(t, 3, 1))
                dve.tensor_tensor(sums[0:WINDOW, :], sums[0:WINDOW, :], sums_prev[:, :], ALU.add).then_inc(sum_step, 1)
                dve.wait_ge(sum_step, cnt(t, 3, 2))
                dve.reciprocal(inv_s[:, :], sums[:, :]).then_inc(sum_step, 1)

            def add_x(L, i):
                t = L * STEPS + i
                dve.wait_ge(o_mm, t + 1)
                dve.tensor_tensor(X1[:, bass.ds(i * P, P)], X[:, bass.ds(i * P, P)], w_b[:, 0:P], ALU.add).then_inc(x1_ready, 1)

            def step(L, i, has_c, has_a):
                t = L * STEPS + i
                i8 = (i + 1) % TILES
                if has_a:
                    for n in range(2):
                        rope(t + 1, i8, n)
                        square_sum(t + 1, n)
                max_prev(t)
                less_max(t, 0, has_c)
                less_max(t, 1, has_c)
                if has_a:
                    for n in range(2, 4):
                        rope(t + 1, i8, n)
                        square_sum(t + 1, n)
                    guard(t + 1)
                less_max(t, 2, has_c)
                less_max(t, 3, has_c)
                if has_a:
                    for n in range(2):
                        unit(t + 1, n)
                less_max_prev(t)
                inverse_sums(t)
                if has_c:
                    add_x(L, i - 1)

            with dve.Fori(0, DEPTH) as L:
                dve.wait_ge(qkv_loaded, L * QKV_LOADS + QKV_LOADS)
                dve.wait_ge(f_done, L * CHUNKS)
                for k in range(4):
                    ins = dve.tensor_tensor(table[:, :, k, :], base[:, :, k, :], qk_scale[:, k, :].unsqueeze(1).to_broadcast([P, TILES, LD]),
                                            ALU.mult)
                ins.then_inc(table_step, 1)
                dve.wait_ge(table_step, L + 3)
                t = L * STEPS
                for n in range(4):
                    rope(t, 0, n)
                    square_sum(t, n)
                guard(t)
                for n in range(2):
                    unit(t, n)
                step(L, 0, False, True)
                with dve.Fori(0, NT // 2 - 1) as g:
                    step(L, g * 2 + 1, True, True)
                    step(L, g * 2 + 2, True, True)
                step(L, NT - 1, True, False)
                add_x(L, NT - 1)

                with dve.Fori(0, CHUNKS // 2) as g:
                    n = L * CHUNKS + g * 2
                    dve.wait_ge(ffn_loaded, L * FFN_LOADS + FFN_LOADS)
                    for s in range(2):
                        dve.wait_ge(f_mean, n + (s + 1))
                        dve.wait_ge(f_sq, n)
                        dve.tensor_tensor(fc[s], fx[s], p_b[s][:, :], ALU.subtract).then_inc(f_cent, 1)
                    for s in range(2):
                        dve.wait_ge(f_rstd, n + (s + 1))
                        dve.tensor_tensor(fn[s], fc[s], fr[s], ALU.mult).then_inc(f_norm, 1)
                    for s in range(2):
                        dve.wait_ge(f_norm, n * 2 + (s + 1))
                        dve.tensor_scalar(X[:, bass.ds((g * 2 + s) * CH, CH)], fn[s], vec[:, 0:1], vec[:, 1:2], ALU.mult,
                                          ALU.add).then_inc(f_norm, 1)

                def feed(c, s):
                    n = L * CHUNKS + c
                    for m, (lo, size) in enumerate(FF_BLOCKS):
                        dve.wait_ge(f_lin, n * 3 + m + 1)
                        dve.wait_ge(f_gelu, n * 3 + m + 1)
                        if m == 0:
                            dve.wait_ge(f_out, n)
                        dve.scalar_tensor_tensor(hh[m][0:size, :], p_b[m % 2][0:size, :], b_1[0:size, m:m + 1], gl[m % 2][0:size, :],
                                                 ALU.add, ALU.mult).then_inc(f_prod, 1)
                    dve.wait_ge(f_out, n + 1)
                    dve.scalar_tensor_tensor(X[:, bass.ds(c * CH, CH)], t_b[s][:, :], vec[:, 2:3], X1[:, bass.ds(c * CH, CH)], ALU.add,
                                             ALU.add).then_inc(f_done, 1)

                with dve.Fori(0, CHUNKS // 2) as g:
                    feed(g * 2, 0)
                    feed(g * 2 + 1, 1)

        layers.close()

        landed = [sem(f"d_x_landed{i}") for i in range(2)]
        e_sum = sem("d_end_sum_ready")
        e_ln = Norm(sem, "d_end_ln")
        e_done = sem("d_end_done")
        with nc.Block() as block:
            @block.sync
            def _(sp):
                for c in range(CHUNKS):
                    if c >= 2:
                        sp.wait_ge(e_sum, c - 1)
                    sp.dma_start(fx[c % 2], kept_x[:, c * CH:c * CH + CH]).then_inc(landed[c % 2], 16)

            @block.tensor
            def _(pe):
                for c in range(CHUNKS):
                    pe.wait_ge(e_sum, c + 1)
                    norm_pe(pe, e_ln, c, mean_w, X[:, c * CH:c * CH + CH], fq[0], p_b[0][:, :], p_b[1][:, :])

            @block.scalar
            def _(act):
                for c in range(CHUNKS):
                    norm_act(act, e_ln, c, fc[0], fq[0], p_b[1][:, :], fl[0], eps)

            @block.vector
            def _(dve):
                for c in range(CHUNKS):
                    x = X[:, c * CH:c * CH + CH]
                    dve.wait_ge(landed[c % 2], 16 * (c // 2) + 16)
                    dve.tensor_tensor(x, x, fx[c % 2], ALU.add).then_inc(e_sum, 1)
                    dve.wait_ge(e_sum, c + 1)
                    norm_dve(dve, e_ln, c, x, fc[0], fl[0], fr[0], p_b[0][:, :])
                    dve.tensor_tensor(x, fc[0], fr[0], ALU.mult).then_inc(e_done, 1)


def build(nc, d, out):
    with ExitStack() as ctx:
        def sem(label):
            return ctx.enter_context(nc.semaphore(label))

        Xp = ctx.enter_context(nc.sbuf_tensor("X", [P, 1 + TOKENS], F32))
        X1p = ctx.enter_context(nc.sbuf_tensor("X1", [P, 1 + TOKENS], F32))
        X, X1 = Xp[:, 1:], X1p[:, 1:]
        ident = ctx.enter_context(nc.sbuf_tensor("ident", [P, P], F32))
        mean_w = ctx.enter_context(nc.sbuf_tensor("mean_weights", [P, P], F32))
        eps = ctx.enter_context(nc.sbuf_tensor("eps", [P, 1], F32))
        const_step = sem("const_step")
        with nc.Block() as block:
            @block.gpsimd
            def _(pool):
                pool.memset(mean_w[:, :], 1.0 / DIM)
                pool.memset(eps[:, :], EPS)
                pool.memset(ident[:, :], 0.0).then_inc(const_step, 1)
                pool.wait_ge(const_step, 1)
                pool.affine_select(out=ident[:, :], in_=ident[:, :], pattern=[[-1, P]], compare_op=ALU.not_equal, fill=1.0,
                                   base=0, channel_multiplier=1)
        consts = (ident[:, :], mean_w[:, :], eps[:, 0:1])

        def early_sem(label):
            return nc.alloc_semaphore(name=label)

        with nc.cleanup_on_exit():
            load_tokens(nc, early_sem, d["x"], X, ident[:, :])
            mamba(nc, early_sem, "a", X, X1, dict(in_proj=d["a_in_proj"], conv=d["a_conv"], x_proj=d["a_x_proj"], dt=d["a_dt"],
                                                  out_proj=d["a_out_proj"], vectors=d["a_vectors"]), consts)
            experts(nc, early_sem, X, d, consts)
            mqa(nc, early_sem, X, X1, d, consts)
        mamba(nc, sem, "c", X, X1, dict(in_proj=d["c_w_in"], taps=d["c_conv_w"], x_proj=d["c_w_xproj"], dt=d["c_w_dt"],
                                        out_proj=d["c_w_out"], vectors=d["c_vectors"], a_log=d["c_a_log"]), consts)
        local_layers(nc, sem, Xp, X1p, d, consts)
        store_tokens(nc, sem, out, X, ident[:, :])


def layout(i):
    def t(a):
        return np.ascontiguousarray(np.transpose(a))

    def cols(*vs):
        parts = [v.reshape(-1, P).T for v in vs]
        n = sum(p.shape[1] for p in parts)
        parts.append(np.zeros((P, 8 - n), np.float32))
        return np.ascontiguousarray(np.concatenate(parts, axis=1))

    def thrice(w, low):
        return np.ascontiguousarray(np.concatenate([w[:, low:]] * 3 + [w[:, :low]], axis=1))

    swap = np.concatenate([np.arange(LD // 2, LD), np.arange(LD // 2)])
    q, k = i["L1_ffn_q_scale"], i["L1_ffn_k_scale"]
    scales = np.broadcast_to(np.stack([q, q[:, swap], k, k[:, swap]], axis=1)[:, None], (DEPTH, P, 4, LD))
    b1 = np.zeros((DEPTH, P, 6), np.float32)
    for m, (lo, size) in enumerate(FF_BLOCKS):
        b1[:, :size, m] = i["L1_ffn_b1"][:, lo:lo + size]
        b1[:, :size, 3 + m] = i["L1_ffn_b1"][:, FFI + lo:FFI + lo + size]
    wqkv = i["L1_ffn_Wqkv"].reshape(DEPTH, DIM, 3, LH, LD).copy()
    wqkv[:, :, 2] = wqkv[:, :, 2][:, :, PLACES]
    wo = i["L1_ffn_Wo"].reshape(DEPTH, LH, LD, DIM)[:, PLACES].reshape(DEPTH, INNER, DIM)
    return {
        "x": i["L0_attn_x"],
        "a_in_proj": t(i["L0_attn_in_proj_w"]),
        "a_conv": np.ascontiguousarray(np.transpose(i["L0_attn_conv_w"], (2, 1, 0))),
        "a_x_proj": thrice(t(i["L0_attn_x_proj_w"]), 1),
        "a_dt": t(i["L0_attn_dt_w"]),
        "a_out_proj": t(i["L0_attn_out_proj_w"]),
        "a_vectors": cols(i["L0_attn_conv_b"], i["L0_attn_dt_b"], i["L0_attn_norm_w"], i["L0_attn_norm_b"]),
        "b_gate": np.ascontiguousarray(np.concatenate([i["L0_ffn_Wg"], i["L0_ffn_Wt"]], axis=1)),
        "b_gate_bias": np.ascontiguousarray(np.broadcast_to(np.concatenate([i["L0_ffn_bg"], i["L0_ffn_bt"]]), (P, 9))),
        "b_w1": i["L0_ffn_W1"],
        "b_b1": np.ascontiguousarray(i["L0_ffn_b1"].reshape(8, 4, P).transpose(2, 0, 1).reshape(P, 32)),
        "b_w2": i["L0_ffn_W2"],
        "b_b2": i["L0_ffn_b2"],
        "q_wqkv": i["L1_attn_wqkv"],
        "q_bias": np.ascontiguousarray(i["L1_attn_bqkv"].reshape(-1, 1)),
        "q_value_bias": np.ascontiguousarray(np.broadcast_to(i["L1_attn_bqkv"][DIM + HD:], (P, HD))),
        "q_key_pick": np.ascontiguousarray(np.repeat(np.array([[k == p for p in range(3)] for k in K_PART], np.float32), HD, axis=0)),
        "q_w_out": i["L1_attn_w_attn_out"],
        "q_b_out": np.ascontiguousarray(i["L1_attn_b_attn_out"].reshape(-1, 1)),
        "c_w_in": i["L1_attn_w_in"],
        "c_conv_w": i["L1_attn_conv_w"],
        "c_w_xproj": thrice(i["L1_attn_w_xproj"], 8),
        "c_w_dt": i["L1_attn_w_dt"],
        "c_w_out": i["L1_attn_w_out"],
        "c_a_log": i["L1_attn_A_log"],
        "c_vectors": cols(i["L1_attn_conv_b"], i["L1_attn_b_dt"], np.zeros(2 * P, np.float32), i["L1_attn_Dp"]),
        "d_wqkv": wqkv.reshape(DEPTH, DIM, 3 * INNER),
        "d_wo": wo,
        "d_w1": i["L1_ffn_W1"],
        "d_w2": i["L1_ffn_W2"],
        "d_scales": scales,
        "d_b1": b1,
        "d_ln": np.ascontiguousarray(np.stack([i["L1_ffn_ln_g"], i["L1_ffn_ln_b"], i["L1_ffn_b2"]], axis=2)),
    }


def kernel(**inputs):
    import numpy as _np
    import concourse.bacc as _bacc
    from concourse import mybir as _mybir
    from concourse.bass_utils import run_bass_kernel_spmd as _run

    nc = _bacc.Bacc("TRN2", target_bir_lowering=False, num_devices=1)
    arrays, aps = {}, {}
    for name, a in layout({k: _np.asarray(v) for k, v in inputs.items()}).items():
        a = _np.ascontiguousarray(a)
        arrays[f"in_{name}"] = a
        aps[name] = nc.dram_tensor(f"in_{name}", a.shape, _mybir.dt.from_np(a.dtype), kind="ExternalInput").ap()
    out = nc.dram_tensor("out_0", (BATCH, SEQ, DIM), F32, kind="ExternalOutput").ap()
    build(nc, aps, out)
    r = _run(nc, [arrays], core_ids=[0])
    return r.results[0]["out_0"]
```
